# Optimizing a Trainium2 kernel written in Bass

```python
import numpy as np
import jax
import jax.numpy as jnp

def _softmax(x, axis=-1):
    return jax.nn.softmax(x, axis=axis)

def _gelu(x):
    return jax.nn.gelu(x, approximate=True)

def _silu(x):
    return jax.nn.silu(x)

def _sigmoid(x):
    return jax.nn.sigmoid(x)

def _layernorm(x, axis=-1, eps=1e-05):
    m = jnp.mean(x, axis=axis, keepdims=True)
    v = jnp.var(x, axis=axis, keepdims=True)
    return (x - m) / jnp.sqrt(v + eps)

def _scatter_add(tgt, idx, src, axis=0):
    return tgt.at[idx].add(src)

def _segment_sum(src, seg, n):
    return jax.ops.segment_sum(src, seg, n)
kernel_name = 'mk_seq_preln_d2_jaxref_r8_0a7589'

def setup_inputs(seed: int=0):
    np.random.seed(seed)
    _w = jnp.asarray

    def _L0_attn_setup():
        import jax, jax.numpy as jnp
        import numpy as np
        EMBED_DIM = 128
        NUM_HEADS = 16
        HEAD_DIM = EMBED_DIM // NUM_HEADS
        LAMBDA_ENTANGLE = 0.35
        key = jax.random.key(seed)
        ks = jax.random.split(key, 10)
        B, S, D = (2, 256, EMBED_DIM)
        init = 1.0 / np.sqrt(D)
        x = jax.random.normal(ks[0], (B, S, D), dtype=jnp.float32)
        Wq = jax.random.uniform(ks[1], (D, D), jnp.float32, -init, init)
        bq = jax.random.uniform(ks[2], (D,), jnp.float32, -init, init)
        Wk = jax.random.uniform(ks[3], (D, D), jnp.float32, -init, init)
        bk = jax.random.uniform(ks[4], (D,), jnp.float32, -init, init)
        Wv = jax.random.uniform(ks[5], (D, D), jnp.float32, -init, init)
        bv = jax.random.uniform(ks[6], (D,), jnp.float32, -init, init)
        Wo = jax.random.uniform(ks[7], (D, D), jnp.float32, -init, init)
        bo = jax.random.uniform(ks[8], (D,), jnp.float32, -init, init)
        J_attn = jax.random.normal(ks[9], (NUM_HEADS, HEAD_DIM, HEAD_DIM), dtype=jnp.float32) * 0.02
        lambda_attn = jnp.asarray(LAMBDA_ENTANGLE, dtype=jnp.float32)
        return {'x': x, 'Wq': Wq, 'bq': bq, 'Wk': Wk, 'bk': bk, 'Wv': Wv, 'bv': bv, 'Wo': Wo, 'bo': bo, 'J_attn': J_attn, 'lambda_attn': lambda_attn}
    _L0_attn_in = _L0_attn_setup()

    def _L0_ffn_setup():
        import jax, jax.numpy as jnp
        import numpy as np
        S, B, H, I, E = (64, 2, 128, 352, 8)
        key = jax.random.key(seed)
        ks = jax.random.split(key, 5)
        return {'hidden_states': jax.random.normal(ks[0], (S, B, H), dtype=jnp.float32), 'router_w': jax.random.normal(ks[1], (E, H), dtype=jnp.float32) * 0.02, 'gate_w': jax.random.normal(ks[2], (E, I, H), dtype=jnp.float32) * 0.02, 'up_w': jax.random.normal(ks[3], (E, I, H), dtype=jnp.float32) * 0.02, 'down_w': jax.random.normal(ks[4], (E, H, I), dtype=jnp.float32) * 0.02}
    _L0_ffn_in = _L0_ffn_setup()

    def _L1_attn_setup():
        import jax, jax.numpy as jnp
        import numpy as np
        B, L = (4, 256)
        D_MODEL = 128
        D_STATE = 16
        D_CONV = 4
        EXPAND = 2
        D_INNER = EXPAND * D_MODEL
        key = jax.random.key(seed)
        ks = jax.random.split(key, 10)
        g = lambda k, shape, s: jax.random.normal(k, shape, jnp.float32) * s
        A = jnp.tile(jnp.arange(1, D_STATE + 1, dtype=jnp.float32)[None, :], (D_INNER, 1))
        return {'x': g(ks[0], (B, L, D_MODEL), 1.0), 'W_in': g(ks[1], (D_MODEL, 2 * D_INNER), 0.02), 'conv_w': g(ks[2], (D_INNER, 1, D_CONV), 0.1), 'conv_b': g(ks[3], (D_INNER,), 0.02), 'W_delta': g(ks[4], (D_MODEL, D_INNER), 0.02), 'b_delta': g(ks[5], (D_INNER,), 0.02), 'W_B': g(ks[6], (D_MODEL, D_STATE), 0.02), 'W_C': g(ks[7], (D_MODEL, D_STATE), 0.02), 'W_out': g(ks[8], (D_INNER, D_MODEL), 0.02), 'A_log': jnp.log(A), 'D': jnp.ones((D_INNER,), jnp.float32)}
    _L1_attn_in = _L1_attn_setup()

    def _L1_ffn_setup():
        import jax, jax.numpy as jnp
        import numpy as np
        TOP_K = 2
        key = jax.random.key(seed)
        k0, k1, k2, k3, k4 = jax.random.split(key, 5)
        B, S, H, I, E = (4, 256, 128, 352, 8)
        s_h = 1.0 / np.sqrt(H)
        s_i = 1.0 / np.sqrt(I)
        return {'x': jax.random.normal(k0, (B, S, H), jnp.float32), 'w_router': jax.random.normal(k1, (E, H), jnp.float32) * s_h, 'w_gate': jax.random.normal(k2, (E, I, H), jnp.float32) * s_h, 'w_up': jax.random.normal(k3, (E, I, H), jnp.float32) * s_h, 'w_down': jax.random.normal(k4, (E, H, I), jnp.float32) * s_i}
    _L1_ffn_in = _L1_ffn_setup()
    _d = {'L0_attn_x': _L0_attn_in['x'], 'L0_attn_Wq': _L0_attn_in['Wq'], 'L0_attn_bq': _L0_attn_in['bq'], 'L0_attn_Wk': _L0_attn_in['Wk'], 'L0_attn_bk': _L0_attn_in['bk'], 'L0_attn_Wv': _L0_attn_in['Wv'], 'L0_attn_bv': _L0_attn_in['bv'], 'L0_attn_Wo': _L0_attn_in['Wo'], 'L0_attn_bo': _L0_attn_in['bo'], 'L0_attn_J_attn': _L0_attn_in['J_attn'], 'L0_attn_lambda_attn': _L0_attn_in['lambda_attn'], 'L0_ffn_router_w': _L0_ffn_in['router_w'], 'L0_ffn_gate_w': _L0_ffn_in['gate_w'], 'L0_ffn_up_w': _L0_ffn_in['up_w'], 'L0_ffn_down_w': _L0_ffn_in['down_w'], 'L1_attn_W_in': _L1_attn_in['W_in'], 'L1_attn_conv_w': _L1_attn_in['conv_w'], 'L1_attn_conv_b': _L1_attn_in['conv_b'], 'L1_attn_W_delta': _L1_attn_in['W_delta'], 'L1_attn_b_delta': _L1_attn_in['b_delta'], 'L1_attn_W_B': _L1_attn_in['W_B'], 'L1_attn_W_C': _L1_attn_in['W_C'], 'L1_attn_W_out': _L1_attn_in['W_out'], 'L1_attn_A_log': _L1_attn_in['A_log'], 'L1_attn_D': _L1_attn_in['D'], 'L1_ffn_w_router': _L1_ffn_in['w_router'], 'L1_ffn_w_gate': _L1_ffn_in['w_gate'], 'L1_ffn_w_up': _L1_ffn_in['w_up'], 'L1_ffn_w_down': _L1_ffn_in['w_down']}
    _x0 = _d['L0_attn_x']
    _d['L0_attn_x'] = jax.random.normal(jax.random.fold_in(jax.random.key(seed), 1), (4, 512, 128), dtype=_x0.dtype)
    del _x0
    return _d

def reference(L0_attn_x, L0_attn_Wq, L0_attn_bq, L0_attn_Wk, L0_attn_bk, L0_attn_Wv, L0_attn_bv, L0_attn_Wo, L0_attn_bo, L0_attn_J_attn, L0_attn_lambda_attn, L0_ffn_router_w, L0_ffn_gate_w, L0_ffn_up_w, L0_ffn_down_w, L1_attn_W_in, L1_attn_conv_w, L1_attn_conv_b, L1_attn_W_delta, L1_attn_b_delta, L1_attn_W_B, L1_attn_W_C, L1_attn_W_out, L1_attn_A_log, L1_attn_D, L1_ffn_w_router, L1_ffn_w_gate, L1_ffn_w_up, L1_ffn_w_down):

    def _L0_attn_ref(x, Wq, bq, Wk, bk, Wv, bv, Wo, bo, J_attn, lambda_attn):
        import jax, jax.numpy as jnp
        import numpy as np
        EMBED_DIM = 128
        NUM_HEADS = 16
        HEAD_DIM = EMBED_DIM // NUM_HEADS
        LAMBDA_ENTANGLE = 0.35
        B, S, D = x.shape
        H, Hd = (NUM_HEADS, HEAD_DIM)
        scale = jnp.sqrt(jnp.asarray(Hd, dtype=x.dtype))

        def heads(W, b):
            y = jnp.einsum('bsd,ed->bse', x, W) + b
            return y.reshape(B, S, H, Hd).transpose(0, 2, 1, 3)
        Q = heads(Wq, bq)
        K = heads(Wk, bk)
        V = heads(Wv, bv)
        scores = jnp.einsum('bhid,bhjd->bhij', Q, K) / scale
        QJ = jnp.einsum('bhid,hde->bhie', jnp.tanh(Q), J_attn)
        delta = jnp.einsum('bhie,bhje->bhij', QJ, jnp.tanh(K))
        scores = scores + lambda_attn * delta
        causal = jnp.triu(jnp.ones((S, S), dtype=bool), k=1)
        scores = jnp.where(causal, -jnp.inf, scores)
        probs = jax.nn.softmax(scores, axis=-1)
        out = jnp.einsum('bhij,bhjd->bhid', probs, V)
        out = out.transpose(0, 2, 1, 3).reshape(B, S, D)
        return jnp.einsum('bsd,ed->bse', out, Wo) + bo

    def _L0_ffn_ref(hidden_states, router_w, gate_w, up_w, down_w):
        import jax, jax.numpy as jnp
        import numpy as np
        S, B, H, I, E = (64, 2, 128, 352, 8)
        router_logits = jnp.einsum('sbh,eh->sbe', hidden_states, router_w)
        routing_indices = jnp.argmax(router_logits, axis=-1)
        out = jnp.zeros_like(hidden_states)
        for e in range(E):
            mask = (routing_indices == e)[..., None]
            xe = jnp.where(mask, hidden_states, 0.0)
            g = jnp.einsum('sbh,ih->sbi', xe, gate_w[e])
            u = jnp.einsum('sbh,ih->sbi', xe, up_w[e])
            ye = jnp.einsum('sbi,hi->sbh', jax.nn.silu(g) * u, down_w[e])
            out = out + jnp.where(mask, ye, 0.0)
        return out

    def _L1_attn_ref(x, W_in, conv_w, conv_b, W_delta, b_delta, W_B, W_C, W_out, A_log, D):
        import jax, jax.numpy as jnp
        import numpy as np
        B, L = (4, 256)
        D_MODEL = 128
        D_STATE = 16
        D_CONV = 4
        EXPAND = 2
        D_INNER = EXPAND * D_MODEL
        Bsz, Lh, _ = x.shape
        xp = x @ W_in
        x_gate, x_in = jnp.split(xp, 2, axis=-1)
        x_in = jax.nn.silu(x_gate) * x_in
        xc = jnp.swapaxes(x_in, 1, 2)
        xc = jax.lax.conv_general_dilated(xc, conv_w, window_strides=(1,), padding=[(D_CONV - 1, 0)], dimension_numbers=('NCH', 'OIH', 'NCH'), feature_group_count=conv_w.shape[0])
        xc = xc + conv_b[None, :, None]
        x_in = jnp.swapaxes(xc, 1, 2)
        delta = jax.nn.softplus(x @ W_delta + b_delta)
        Bm = x @ W_B
        Cm = x @ W_C
        A = -jnp.exp(A_log)

        def step(h, inputs):
            d_t, b_t, c_t, xt = inputs
            dA = jnp.exp(d_t[..., None] * A)
            h = dA * h + (d_t * xt)[..., None] * b_t[:, None, :]
            y_t = jnp.einsum('bn,bdn->bd', c_t, h)
            return (h, y_t)
        h0 = jnp.zeros((Bsz, D_INNER, D_STATE), x.dtype)
        seq = (jnp.swapaxes(delta, 0, 1), jnp.swapaxes(Bm, 0, 1), jnp.swapaxes(Cm, 0, 1), jnp.swapaxes(x_in, 0, 1))
        _, ys = jax.lax.scan(step, h0, seq)
        y = jnp.swapaxes(ys, 0, 1) + D * x_in
        return y @ W_out

    def _L1_ffn_ref(x, w_router, w_gate, w_up, w_down):
        import jax, jax.numpy as jnp
        import numpy as np
        TOP_K = 2
        B, S, H = x.shape
        E = w_router.shape[0]
        xf = x.reshape(-1, H)
        logits = jnp.einsum('th,eh->te', xf, w_router)
        probs = jax.nn.softmax(logits, axis=-1)
        topw, topi = jax.lax.top_k(probs, TOP_K)
        topw = topw / jnp.sum(topw, axis=-1, keepdims=True)
        onehot = (topi[..., None] == jnp.arange(E)).astype(x.dtype)
        combine = jnp.einsum('tk,tke->te', topw, onehot)
        gate = jax.nn.silu(jnp.einsum('th,eih->eti', xf, w_gate))
        up = jnp.einsum('th,eih->eti', xf, w_up)
        down = jnp.einsum('eti,ehi->eth', gate * up, w_down)
        out = jnp.einsum('eth,te->th', down, combine)
        return out.reshape(B, S, H)
    x = L0_attn_x
    x = x + _L0_attn_ref(_layernorm(x, axis=-1), L0_attn_Wq, L0_attn_bq, L0_attn_Wk, L0_attn_bk, L0_attn_Wv, L0_attn_bv, L0_attn_Wo, L0_attn_bo, L0_attn_J_attn, L0_attn_lambda_attn)
    x = x + _L0_ffn_ref(_layernorm(x, axis=-1), L0_ffn_router_w, L0_ffn_gate_w, L0_ffn_up_w, L0_ffn_down_w)
    x = x + _L1_attn_ref(_layernorm(x, axis=-1), L1_attn_W_in, L1_attn_conv_w, L1_attn_conv_b, L1_attn_W_delta, L1_attn_b_delta, L1_attn_W_B, L1_attn_W_C, L1_attn_W_out, L1_attn_A_log, L1_attn_D)
    x = x + _L1_ffn_ref(_layernorm(x, axis=-1), L1_ffn_w_router, L1_ffn_w_gate, L1_ffn_w_up, L1_ffn_w_down)
    return x

_drawn_inputs = setup_inputs


def setup_inputs(seed=0):
    import zlib

    import numpy as np

    out = dict(_drawn_inputs(seed))
    spreads = {'L1_attn_D': (1.0, 0.6)}
    factors = {'L0_attn_bq': 17.621,
     'L0_attn_bk': 64.0,
     'L0_attn_J_attn': 40.806,
     'L1_attn_W_in': 3.48,
     'L1_attn_conv_w': 3.396,
     'L1_attn_W_delta': 8.0,
     'L1_attn_b_delta': 8.0,
     'L1_attn_W_B': 7.849,
     'L1_attn_W_C': 8.0,
     'L1_attn_W_out': 2.808,
     'L1_attn_A_log': 8.0}
    for name, (base, spread) in spreads.items():
        noise = np.random.default_rng([zlib.crc32(name.encode()), seed]).standard_normal(out[name].shape)
        drawn = base * np.exp(spread * noise) if base else spread * noise
        out[name] = jnp.asarray(drawn.astype(out[name].dtype))
    for name, factor in factors.items():
        out[name] = (out[name] * factor).astype(out[name].dtype)
    return out
```

```python
from contextlib import ExitStack

import concourse.bass as bass
from concourse import mybir

F32 = mybir.dt.float32
BF16 = mybir.dt.bfloat16
I32 = mybir.dt.int32
U32 = mybir.dt.uint32
ACT = mybir.ActivationFunctionType
ALU = mybir.AluOpType
AX_X = mybir.AxisListType.X

P = 128
B, S, D = 4, 512, 128
H, HD = 16, 8
TT = S // P
NT = B * TT
EPS = 1e-5
QK_SCALE = HD ** -0.5
HP = 32
GROUP = P // HP
SCORE_COLS = sum(S - P * j for j in range(TT))


ROWS = 12 * HD
Q_ORDER = (0, 0, 1, 1, 0, 2)
K_ORDER = (0, 1, 0, 1, 2, 0)
DVE_LINKS = 18
SSM_LINKS = 13
SSM_ACT_LINKS = 3
ROUTE_LINKS = {1: 18, 2: 26}


class Chain:

    def __init__(self, eng, sem, turn, per):
        self.eng, self.sem, self.turn, self.per, self.n = eng, sem, turn, per, 0

    def __call__(self, ins):
        self.n += 1
        ins.then_inc(self.sem, 1)
        self.eng.wait_ge(self.sem, self.turn * self.per + self.n)

    def done(self):
        assert self.n == self.per, (self.n, self.per)


def layer_norm_stats(nc, ctx, tag, x_sb):
    stats = ctx.enter_context(nc.sbuf_tensor(f"{tag}_stats", [P, NT, 6], F32))
    mv = ctx.enter_context(nc.sbuf_tensor(f"{tag}_mv", [P, NT, 2], F32))
    std = ctx.enter_context(nc.sbuf_tensor(f"{tag}_std", [P, NT], F32))
    rstd = ctx.enter_context(nc.sbuf_tensor(f"{tag}_rstd", [P, NT], F32))
    eps = ctx.enter_context(nc.sbuf_tensor(f"{tag}_eps", [P, 1], F32))
    stats_done = ctx.enter_context(nc.semaphore(f"{tag}_stats_done"))
    mv_done = ctx.enter_context(nc.semaphore(f"{tag}_mv_done"))
    std_done = ctx.enter_context(nc.semaphore(f"{tag}_std_done"))
    rstd_done = ctx.enter_context(nc.semaphore(f"{tag}_rstd_done"))

    def on_vector(dve):
        nc.vector.memset(eps[:], EPS).then_inc(mv_done, 1)
        for t in range(NT):
            nc.vector.bn_stats(stats[:, t, :], x_sb[:, t, :]).then_inc(stats_done, 1)
        for t in range(NT):
            dve.wait_ge(stats_done, t + 1)
            nc.vector.bn_aggr(mv[:, t, :], stats[:, t, :]).then_inc(mv_done, 1)
        dve.wait_ge(std_done, 1)
        nc.vector.reciprocal(rstd[:], std[:]).then_inc(rstd_done, 1)
        dve.wait_ge(rstd_done, 1)

    def on_scalar(act):
        act.wait_ge(mv_done, NT + 1)
        nc.scalar.activation(std[:], mv[:, :, 1], ACT.Sqrt, bias=eps[:]).then_inc(std_done, 1)

    return mv, rstd, on_vector, on_scalar


def attention(nc, x_sb, A):
    with ExitStack() as ctx:
        sb = lambda name, shape, dt=F32: ctx.enter_context(nc.sbuf_tensor(name, shape, dt))
        sem = lambda name: ctx.enter_context(nc.semaphore(name))

        w = {n: sb(f"a_{n}", [P, D]) for n in ("wq", "wk", "wv", "wo", "J")}
        ident = sb("a_ident", [P, P])
        ident_b = sb("a_ident_b", [P, P], BF16)
        mask_q = sb("a_mask_q", [P, P], BF16)
        mask_k = sb("a_mask_k", [P, P], BF16)
        head_rows = sb("a_head_rows", [P, H, P], BF16)
        bq, bk, lam = sb("a_bq", [P, 1]), sb("a_bk", [P, 1]), sb("a_lam", [P, 1])
        bqs = sb("a_bqs", [P, 1])
        bv, bo = sb("a_bv", [P, D]), sb("a_bo", [P, D])
        wqs = sb("a_wqs", [P, D])
        xn = sb("a_xn", [P, TT, D])
        xnT = sb("a_xnT", [P, S])
        tanh_q, tanh_k = sb("a_tanh_q", [P, S]), sb("a_tanh_k", [P, S])
        rest = sb("a_rest", [P, 4, S])
        parts = sb("a_parts", [P, 4, 3, S], BF16)
        QA = sb("a_QA", [P, H, S], BF16)
        KA = sb("a_KA", [P, H, S], BF16)
        V = sb("a_V", [P, TT, H, HP])
        row_max = sb("a_row_max", [P, TT, H])
        max_rest = sb("a_max_rest", [P, TT, H])
        max_parts = sb("a_max_parts", [P, TT, 3, H], BF16)
        neg_max = sb("a_neg_max", [P, S], BF16)
        probs = sb("a_probs", [P, 2, GROUP, SCORE_COLS])
        OT = sb("a_OT", [P, 2, S])
        den = sb("a_den", [P, 2, TT, GROUP])
        O = sb("a_O", [P, TT, H, HD])
        OnT = sb("a_OnT", [P, S])
        xo = sb("a_xo", [P, TT, D])
        misc = [ctx.enter_context(nc.psum_tensor(f"a_misc{i}", [P, S], F32)) for i in range(2)]
        sc = ctx.enter_context(nc.psum_tensor("a_sc", [P, 2, 2, S], F32))
        pv = ctx.enter_context(nc.psum_tensor("a_pv", [P, 2, S], F32))

        loaded = sem("a_loaded")
        consts_ready = sem("a_consts_ready")
        xn_ready, xnT_psum, xnT_ready = sem("a_xn_ready"), sem("a_xnT_psum"), sem("a_xnT_ready")
        q_psum, q_read_act, q_read_dve = sem("a_q_psum"), sem("a_q_read_act"), sem("a_q_read_dve")
        tq_ready, j_psum, j_read = sem("a_tq_ready"), sem("a_j_psum"), sem("a_j_read")
        k_psum, k_read = sem("a_k_psum"), sem("a_k_read")
        hi_ready = sem("a_hi_ready")
        parts_ready = sem("a_parts_ready")
        v_psum, v_ready = sem("a_v_psum"), sem("a_v_ready")
        stacked = sem("a_stacked")
        max_psum, max_read = sem("a_max_psum"), sem("a_max_read")
        maxparts_ready, maxT_psum, negmax_ready = sem("a_maxparts"), sem("a_maxT_psum"), sem("a_negmax")
        st_psum, exp_done, pv_psum = sem("a_st_psum"), sem("a_exp_done"), sem("a_pv_psum")
        ot_ready, ot_psum, o_ready = sem("a_ot_ready"), sem("a_ot_psum"), sem("a_o_ready")
        onT_psum, onT_ready, out_psum, x_done = (sem("a_onT_psum"), sem("a_onT_ready"),
                                                 sem("a_out_psum"), sem("a_x_done"))
        dve_chain = sem("a_dve_chain")
        mv, rstd, ln_vector, ln_scalar = layer_norm_stats(nc, ctx, "a", x_sb)
        LOADS = 19
        NPAIR = H // 2
        STEPS = 3 * NPAIR
        NG = H // GROUP
        DMAS = 24

        def place(h, j):
            return {0: 0, 1: S, 3: S + 3 * P, 2: 2 * S}[j]

        block = ctx.enter_context(nc.Block())

        @block.sync
        def _(sp):
            for n in w:
                sp.dma_start(w[n][:], A[n]).then_inc(loaded, 16)
            for dst, name in ((ident, "ident"), (ident_b, "ident_b"), (mask_q, "mask_q"),
                              (mask_k, "mask_k"), (head_rows, "head_rows"), (bq, "bq"), (bk, "bk")):
                sp.dma_start(dst[:], A[name]).then_inc(loaded, 16)
            sp.dma_start(lam[:], A["lam"].broadcast_to([P, 1])).then_inc(loaded, 16)
            for dst, name in ((bv, "bv"), (bo, "bo")):
                sp.dma_start(dst[:], A[name].broadcast_to([P, D])).then_inc(loaded, 16)
            for b in range(B):
                sp.dma_start(x_sb[:, b * TT:(b + 1) * TT, :],
                             A["x"][b].rearrange("(n p) d -> p n d", p=P)).then_inc(loaded, 16)

            def spread(b, after_first):
                if after_first:
                    sp.wait_ge(st_psum, b * STEPS)
                for f, (stack, feature, order) in enumerate((
                        (QA, 0, Q_ORDER), (KA, 0, K_ORDER), (KA, 1, K_ORDER), (QA, 1, Q_ORDER))):
                    x = f
                    sp.wait_ge(parts_ready, b * 4 + f + 1)
                    for blk, part in enumerate(order):
                        r0 = 2 * HD * blk + HD * feature
                        sp.dma_start(stack[r0:r0 + HD, :, :], parts[:, x, part, :]).then_inc(stacked, 16)

            spread(0, False)
            with sp.Fori(1, B) as b:
                spread(b, True)

        @block.vector
        def _(dve):
            dve.wait_ge(loaded, 16 * LOADS)
            ln_vector(dve)
            nc.vector.tensor_scalar(wqs[:], w["wq"][:], QK_SCALE, None, ALU.mult).then_inc(consts_ready, 1)
            nc.vector.tensor_scalar(bqs[:], bq[:], QK_SCALE, None, ALU.mult).then_inc(consts_ready, 1)
            nc.vector.memset(V[:], 0.0).then_inc(consts_ready, 1)
            nc.vector.memset(neg_max[:], 0.0).then_inc(consts_ready, 1)
            dve.wait_ge(consts_ready, 4)
            nc.vector.memset(V[:, :, :, HD:HD + 1], 1.0).then_inc(consts_ready, 1)
            dve.wait_ge(consts_ready, 5)

            def turn(b, first):
                link = Chain(dve, dve_chain, b, DVE_LINKS)
                if not first:
                    dve.wait_ge(xnT_psum, b)
                for t in range(TT):
                    last = nc.vector.tensor_scalar(xn[:, t, :], x_sb[:, bass.ds(b * TT + t, 1), :],
                                                   mv[:, bass.ds(b * TT + t, 1), 0],
                                                   rstd[:, bass.ds(b * TT + t, 1)],
                                                   ALU.subtract, ALU.mult)
                last.then_inc(xn_ready, 1)
                dve.wait_ge(v_psum, b + 1)
                if not first:
                    dve.wait_ge(pv_psum, b * NG)
                nc.vector.tensor_tensor(V[:, :, :, 0:HD],
                                        misc[0][:].rearrange("p (n h r) -> p n h r", h=H, r=HD),
                                        bv[:].rearrange("p (o h r) -> p o h r", o=1, r=HD)
                                        .broadcast_to([P, TT, H, HD]), ALU.add).then_inc(v_ready, 1)
                if not first:
                    dve.wait_ge(stacked, b * 16 * DMAS)

                def low_parts(x, rest_of):
                    dve.wait_ge(hi_ready, b * 4 + x + 1)
                    link(rest_of())
                    link(nc.vector.tensor_copy(parts[:, x, 1, :], rest[:, x, :]))
                    nc.vector.tensor_tensor(parts[:, x, 2, :], rest[:, x, :], parts[:, x, 1, :],
                                            ALU.subtract).then_inc(parts_ready, 1)

                def rest_q():
                    return nc.vector.scalar_tensor_tensor(out=rest[:, 0, :], in0=misc[1][:], scalar=bqs[:],
                                                          in1=parts[:, 0, 0, :], op0=ALU.add, op1=ALU.subtract)

                def rest_k():
                    return nc.vector.scalar_tensor_tensor(out=rest[:, 1, :], in0=sc[:, 0, 0, :], scalar=bk[:],
                                                          in1=parts[:, 1, 0, :], op0=ALU.add, op1=ALU.subtract)

                def rest_tk():
                    return nc.vector.tensor_tensor(rest[:, 2, :], tanh_k[:], parts[:, 2, 0, :], ALU.subtract)

                def rest_qj():
                    return nc.vector.scalar_tensor_tensor(out=rest[:, 3, :], in0=misc[1][:], scalar=lam[:],
                                                          in1=parts[:, 3, 0, :], op0=ALU.mult, op1=ALU.subtract)

                low_parts(0, rest_q)
                low_parts(1, rest_k)
                low_parts(2, rest_tk)
                low_parts(3, rest_qj)
                for p in range(NPAIR):
                    for r in range(TT):
                        s = p * TT + r
                        dve.wait_ge(max_psum, b * NPAIR * TT + s + 1)
                        nc.vector.reduce_max(row_max[:, r, 2 * p:2 * p + 2], sc[:, s % 2, :, 0:P * (r + 1)],
                                             AX_X).then_inc(max_read, 1)
                dve.wait_ge(max_read, b * NPAIR * TT + NPAIR * TT)
                link(nc.vector.tensor_scalar(max_rest[:], row_max[:], -1.0, None, ALU.mult))
                link(nc.vector.tensor_copy(max_parts[:, :, 0, :], max_rest[:]))
                link(nc.vector.tensor_tensor(max_rest[:], max_rest[:], max_parts[:, :, 0, :], ALU.subtract))
                link(nc.vector.tensor_copy(max_parts[:, :, 1, :], max_rest[:]))
                nc.vector.tensor_tensor(max_parts[:, :, 2, :], max_rest[:], max_parts[:, :, 1, :],
                                        ALU.subtract).then_inc(maxparts_ready, 1)
                dve.wait_ge(maxT_psum, b + 1)
                nc.vector.tensor_copy(neg_max[0:3 * H, :], misc[0][0:3 * H, :]).then_inc(negmax_ready, 1)
                for g in range(NG):
                    dve.wait_ge(pv_psum, b * NG + g + 1)
                    if g >= 2:
                        dve.wait_ge(ot_psum, b * NG + g - 1)
                    nc.vector.tensor_copy(OT[:, g % 2, :], pv[:, g % 2, :]).then_inc(ot_ready, 1)
                    dve.wait_ge(ot_psum, b * NG + g + 1)
                    tok = misc[g % 2][:].rearrange("p (n k c) -> p n k c", n=TT, k=GROUP)
                    link(nc.vector.reciprocal(den[:, g % 2, :, :], tok[:, :, :, HD]))
                    nc.vector.tensor_tensor(O[:, :, GROUP * g:GROUP * (g + 1), :], tok[:, :, :, 0:HD],
                                            den[:, g % 2, :, :].rearrange("p n (k o) -> p n k o", o=1)
                                            .broadcast_to([P, TT, GROUP, HD]), ALU.mult).then_inc(o_ready, 1)
                dve.wait_ge(out_psum, b + 1)
                xb = x_sb[:, bass.ds(b * TT, TT), :]
                link(nc.vector.tensor_tensor(xo[:], misc[1][:].rearrange("p (n d) -> p n d", n=TT), xb, ALU.add))
                link(nc.vector.tensor_tensor(xb, xo[:], bo[:].rearrange("p (o d) -> p o d", o=1)
                                             .broadcast_to([P, TT, D]), ALU.add))
                link.done()

            turn(0, True)
            with dve.Fori(1, B) as b:
                turn(b, False)

        @block.scalar
        def _(act):
            ln_scalar(act)

            def turn(b, first):
                act.wait_ge(xnT_psum, b + 1)
                nc.scalar.copy(xnT[:], misc[0][:]).then_inc(xnT_ready, 1)
                act.wait_ge(q_psum, b + 1)
                if first:
                    act.wait_ge(consts_ready, 5)
                else:
                    act.wait_ge(stacked, b * 16 * DMAS)
                nc.scalar.activation(tanh_q[:], misc[1][:], ACT.Tanh, bias=bq[:],
                                     scale=1.0 / QK_SCALE).then_inc(tq_ready, 1)
                nc.scalar.activation(parts[:, 0, 0, :], misc[1][:], ACT.Identity, bias=bqs[:]).then_inc(hi_ready, 1)
                act.wait_ge(k_psum, b + 1)
                nc.scalar.activation(tanh_k[:], sc[:, 0, 0, :], ACT.Tanh, bias=bk[:]).then_inc(k_read, 1)
                nc.scalar.activation(parts[:, 1, 0, :], sc[:, 0, 0, :], ACT.Identity, bias=bk[:]).then_inc(hi_ready, 1)
                act.wait_ge(k_read, b + 1)
                nc.scalar.copy(parts[:, 2, 0, :], tanh_k[:]).then_inc(hi_ready, 1)
                act.wait_ge(j_psum, b + 1)
                nc.scalar.activation(parts[:, 3, 0, :], misc[1][:], ACT.Copy, scale=lam[:]).then_inc(hi_ready, 1)
                for s in range(STEPS):
                    pair, kind = divmod(s, 3)
                    h = 2 * pair + (kind if kind < 2 else 0)
                    g, k = divmod(h, GROUP)
                    act.wait_ge(st_psum, b * STEPS + s + 1)
                    if g >= 2 or not first:
                        act.wait_ge(pv_psum, b * NG + g - 1)
                    if kind < 2:
                        ins = nc.scalar.activation(probs[:, g % 2, k, 0:2 * S],
                                                   sc[:, s % 2, :, :].rearrange("p a n -> p (a n)"), ACT.Exp)
                    else:
                        ins = nc.scalar.activation(probs[:, g % 2, k:k + 2, 2 * S:SCORE_COLS],
                                                   sc[:, s % 2, 0, :].rearrange("p (a n) -> p a n", a=2), ACT.Exp)
                    ins.then_inc(exp_done, 1)
                act.wait_ge(onT_psum, b + 1)
                nc.scalar.copy(OnT[:], misc[0][:]).then_inc(onT_ready, 1)

            turn(0, True)
            with act.Fori(1, B) as b:
                turn(b, False)

        @block.tensor
        def _(pe):
            pe.wait_ge(loaded, 16 * LOADS)
            pe.wait_ge(consts_ready, 5)
            mm = nc.tensor.matmul

            def turn(b, first):
                pe.wait_ge(xn_ready, b + 1)
                if not first:
                    pe.wait_ge(onT_ready, b)
                for t in range(TT):
                    last = nc.tensor.transpose(misc[0][:, t * P:(t + 1) * P], xn[:, t, :], ident[:])
                last.then_inc(xnT_psum, 1)
                pe.wait_ge(xnT_ready, b + 1)
                if not first:
                    pe.wait_ge(dve_chain, b * DVE_LINKS)
                mm(misc[1][:], wqs[:], xnT[:], start=True, stop=True).then_inc(q_psum, 1)
                for t in range(TT):
                    last = mm(misc[0][:, t * P:(t + 1) * P], xnT[:, t * P:(t + 1) * P], w["wv"][:],
                              start=True, stop=True)
                last.then_inc(v_psum, 1)
                if not first:
                    pe.wait_ge(exp_done, b * STEPS)
                mm(sc[:, 0, 0, :], w["wk"][:], xnT[:], start=True, stop=True).then_inc(k_psum, 1)
                pe.wait_ge(tq_ready, b + 1)
                pe.wait_ge(parts_ready, b * 4 + 1)
                mm(misc[1][:], w["J"][:], tanh_q[:], start=True, stop=True).then_inc(j_psum, 1)

                pe.wait_ge(parts_ready, b * 4 + 4)
                pe.wait_ge(stacked, (b + 1) * (16 * DMAS))
                for p in range(NPAIR):
                    for r in range(TT):
                        s = p * TT + r
                        if s >= 2:
                            pe.wait_ge(max_read, b * NPAIR * TT + s - 1)
                        for a in range(2):
                            h = 2 * p + a
                            q = slice(r * P, (r + 1) * P)
                            mm(sc[:, s % 2, a, 0:P * (r + 1)], QA[0:ROWS, h, q], KA[0:ROWS, h, 0:P * (r + 1)],
                               start=True, stop=False)
                            last = mm(sc[:, s % 2, a, q], ident_b[:], mask_q[:], start=False, stop=True)
                        last.then_inc(max_psum, 1)
                pe.wait_ge(maxparts_ready, b + 1)
                pe.wait_ge(v_ready, b + 1)
                for t in range(TT):
                    last = mm(misc[0][0:3 * H, t * P:(t + 1) * P],
                              max_parts[:, t, :, :].rearrange("p k h -> p (k h)"), ident_b[:],
                              start=True, stop=True)
                last.then_inc(maxT_psum, 1)
                pe.wait_ge(negmax_ready, b + 1)

                def scores_t(out, h, j):
                    mm(out, KA[0:ROWS, h, j * P:(j + 1) * P], QA[0:ROWS, h, j * P:S], start=True, stop=False)
                    mm(out, head_rows[:, h, :], neg_max[:, j * P:S], start=False, stop=False)
                    return mm(out[:, 0:P], ident_b[:], mask_k[:], start=False, stop=True)

                def group_out(g):
                    pe.wait_ge(exp_done, b * STEPS + 6 * (g + 1))
                    if g >= 2 or not first:
                        pe.wait_ge(ot_ready, b * NG + g - 1)
                    for j in range(TT):
                        for k in range(GROUP):
                            c = place(0, j)
                            last = mm(pv[k * HP:(k + 1) * HP, g % 2, j * P:S], V[:, j, GROUP * g + k, :],
                                      probs[:, g % 2, k, c:c + S - j * P], start=(j == 0), stop=(j == TT - 1))
                    last.then_inc(pv_psum, 1)

                def tokens(g):
                    pe.wait_ge(ot_ready, b * NG + g + 1)
                    if g >= 2:
                        pe.wait_ge(o_ready, b * NG + g - 1)
                    if g == 1:
                        pe.wait_ge(parts_ready, b * 4 + 4)
                    for t in range(TT):
                        last = nc.tensor.transpose(misc[g % 2][:, t * P:(t + 1) * P],
                                                   OT[:, g % 2, t * P:(t + 1) * P], ident[:])
                    last.then_inc(ot_psum, 1)

                for s in range(STEPS):
                    pair, kind = divmod(s, 3)
                    if s >= 2:
                        pe.wait_ge(exp_done, b * STEPS + s - 1)
                    for a in range(1 if kind < 2 else 2):
                        h = 2 * pair + (kind if kind < 2 else a)
                        if kind < 2:
                            scores_t(sc[:, s % 2, 0, :], h, 0)
                            scores_t(sc[:, s % 2, 1, 0:3 * P], h, 1)
                            last = scores_t(sc[:, s % 2, 1, 3 * P:S], h, 3)
                        else:
                            last = scores_t(sc[:, s % 2, 0, a * 2 * P:(a + 1) * 2 * P], h, 2)
                    last.then_inc(st_psum, 1)
                    if s % 6 == 1 and s > 6:
                        group_out(s // 6 - 1)
                    if s % 6 == 3 and s > 6:
                        tokens(s // 6 - 1)
                group_out(NG - 1)
                tokens(NG - 1)
                pe.wait_ge(o_ready, b * NG + NG)
                for t in range(TT):
                    last = nc.tensor.transpose(misc[0][:, t * P:(t + 1) * P],
                                               O[:, t, :, :].rearrange("p h r -> p (h r)"), ident[:])
                last.then_inc(onT_psum, 1)
                pe.wait_ge(onT_ready, b + 1)
                for t in range(TT):
                    last = mm(misc[1][:, t * P:(t + 1) * P], OnT[:, t * P:(t + 1) * P], w["wo"][:],
                              start=True, stop=True)
                last.then_inc(out_psum, 1)

            turn(0, True)
            with pe.Fori(1, B) as b:
                turn(b, False)


E, I = 8, 352
CHUNKS = [(c, min(P, I - c)) for c in range(0, I, P)]


def routed_ffn(nc, x_sb, A, tag, top_k):
    KT = top_k * NT
    NS = (KT * P + E * (P - 1)) // P
    assert NS % 2 == 1
    with ExitStack() as ctx:
        sb = lambda name, shape, dt=F32: ctx.enter_context(nc.sbuf_tensor(f"{tag}_{name}", shape, dt))
        sem = lambda name: ctx.enter_context(nc.semaphore(f"{tag}_{name}"))
        ps = lambda name, shape: ctx.enter_context(nc.psum_tensor(f"{tag}_{name}", shape, F32))

        wg, wu = sb("wg", [P, E, I]), sb("wu", [P, E, I])
        wd = sb("wd", [P, len(CHUNKS), E, D])
        wr = sb("wr", [P, E])
        ident = sb("ident", [P, P])
        before = sb("before", [P, P], BF16)
        ones = sb("ones", [P, P], BF16)
        rank = sb("rank", [P, E])
        steps = sb("steps", [P, NT + 1 if NT + 1 > NS else NS])
        zeros = sb("zeros", [P, D])
        xn = sb("xn", [P, NT, D])
        xnT = sb("xnT", [P, 2, S])
        logits = sb("logits", [P, NT, E])
        score = sb("score", [P, NT, E])
        best = sb("best", [P, NT, 1])
        top = sb("top", [P, top_k, NT, 1])
        onehot = sb("onehot", [P, top_k, NT, E])
        onehot_b = sb("onehot_b", [P, top_k, NT, E], BF16)
        weight = sb("weight", [P, top_k, NT])
        gap, gap_sum = sb("gap", [P, NT]), sb("gap_sum", [P, NT])
        over = sb("over", [P, E, KT + 1])
        tiles = sb("tiles", [P, E])
        ends = sb("ends", [P, E])
        starts = sb("starts", [P, E])
        place = sb("place", [P, KT, E])
        pos_f = sb("pos_f", [P, KT])
        pos = sb("pos", [P, KT], U32)
        passed = sb("passed", [P, NS, E])
        expert_f = sb("expert_f", [P, NS])
        expert = sb("expert", [P, NS], I32)
        xs = sb("xs", [P, 2, D])
        xsT = sb("xsT", [P, 2, P])
        sg, hid = sb("sg", [P, 2, I]), sb("hid", [P, 2, I])
        hidT = sb("hidT", [P, 2, len(CHUNKS), P])
        y = sb("y", [P, 2, D])
        back = sb("back", [P, KT, D])
        sorted_x = nc.dram_tensor(f"{tag}_sorted_x", (NS * P, D), F32, kind="Internal").ap()
        sorted_y = nc.dram_tensor(f"{tag}_sorted_y", (NS * P, D), F32, kind="Internal").ap()
        p_turn, p_rank = ps("p_turn", [P, S]), ps("p_rank", [P, KT + 1, E])
        p_g, p_u = ps("p_g", [P, 2, 512]), ps("p_u", [P, 2, 512])
        p_h, p_y = ps("p_h", [P, len(CHUNKS) * P]), ps("p_y", [P, D])

        loaded, cleared, moved = sem("loaded"), sem("cleared"), sem("moved")
        zeros_ready, ones_ready = sem("zeros_ready"), sem("ones_ready")
        xn_ready, xnT_psum, xnT_ready = sem("xn_ready"), sem("xnT_psum"), sem("xnT_ready")
        logit_psum, logit_psum_part = sem("logit_psum"), sem("logit_psum_part")
        onehot_ready, rank_psum, pos_ready = sem("onehot_ready"), sem("rank_psum"), sem("pos_ready")
        gap_ready, exp_ready, weight_ready = sem("gap_ready"), sem("exp_ready"), sem("weight_ready")
        expert_ready = sem("expert_ready")
        xs_in = [sem("xs_in0"), sem("xs_in1")]
        xs_psum, xsT_ready = sem("xs_psum"), sem("xsT_ready")
        g_psum, sg_ready, u_psum, hid_ready = sem("g_psum"), sem("sg_ready"), sem("u_psum"), sem("hid_ready")
        h_psum, hidT_ready, y_psum, y_ready = sem("h_psum"), sem("hidT_ready"), sem("y_psum"), sem("y_ready")
        y_out = [sem("y_out0"), sem("y_out1")]
        gathered = sem("gathered")
        chain = sem("chain")
        mv, rstd, ln_vector, ln_scalar = layer_norm_stats(nc, ctx, tag, x_sb)
        LOADS = 7 + len(CHUNKS)
        NGRP = NT // TT

        block = ctx.enter_context(nc.Block())

        @block.sync
        def _(sp):
            for dst, name in ((wr, "wr"), (wg, "wg"), (wu, "wu")):
                sp.dma_start(dst[:], A[f"{tag}_{name}"]).then_inc(loaded, 16)
            for c, (c0, cn) in enumerate(CHUNKS):
                sp.dma_start(wd[0:cn, c, :, :], A[f"{tag}_wd"][c0:c0 + cn]).then_inc(loaded, 16)
            sp.dma_start(ident[:], A["ident"]).then_inc(loaded, 16)
            sp.dma_start(before[:], A["before"]).then_inc(loaded, 16)
            sp.dma_start(rank[:], A["rank"].broadcast_to([P, E])).then_inc(loaded, 16)
            sp.dma_start(steps[:], A["steps"][:, 0:steps.shape[1]].broadcast_to([P, steps.shape[1]])
                         ).then_inc(loaded, 16)
            sp.wait_ge(zeros_ready, 1)
            sp.dma_start(sorted_x.rearrange("(s p) d -> p s d", p=P),
                         zeros[:].rearrange("p (o d) -> p o d", o=1).broadcast_to([P, NS, D])
                         ).then_inc(cleared, 16)

            sp.wait_ge(moved, 16 * KT)

            def tile_in(s, k, nth, free=None):
                if free is not None:
                    sp.wait_ge(xs_psum, free)
                sp.dma_start(xs[:, k, :], sorted_x[bass.ds(s * P, P), :]).then_inc(xs_in[k], 16)

            def tile_out(s, k):
                sp.wait_ge(y_ready, s + 1)
                sp.dma_start(sorted_y[bass.ds(s * P, P), :], y[:, k, :]).then_inc(y_out[k], 16)

            tile_in(0, 0, 0)
            tile_in(1, 1, 0)
            tile_in(2, 0, 1, 1)
            tile_out(0, 0)
            with sp.Fori(0, (NS - 3) // 2) as m:
                for j in range(2):
                    s = 2 * m + 1 + j
                    tile_in(s + 2, (1 + j) % 2, None, s + 1)
                    tile_out(s, (1 + j) % 2)
            for s in (NS - 2, NS - 1):
                tile_out(s, s % 2)

        @block.vector
        def _(dve):
            link = Chain(dve, chain, 0, ROUTE_LINKS[top_k])
            nc.vector.memset(zeros[:], 0.0).then_inc(zeros_ready, 1)
            nc.vector.memset(ones[:], 1.0).then_inc(ones_ready, 1)
            ln_vector(dve)
            for t in range(NT):
                ins = nc.vector.tensor_scalar(xn[:, t, :], x_sb[:, t, :], mv[:, t, 0:1], rstd[:, t:t + 1],
                                              ALU.subtract, ALU.mult)
                if t % TT == TT - 1:
                    ins.then_inc(xn_ready, 1)
            dve.wait_ge(logit_psum, 1)
            link(nc.vector.tensor_copy(logits[:], p_rank[:, 0:NT, :]))
            dve.wait_ge(loaded, 16 * LOADS)
            across = lambda a: a.broadcast_to([P, NT, E])
            for k in range(top_k):
                link(nc.vector.reduce_max(top[:, k, :, 0], logits[:], AX_X))
                link(nc.vector.tensor_tensor(score[:], logits[:], across(top[:, k, :, :]), ALU.is_equal))
                link(nc.vector.tensor_tensor(score[:], score[:], across(rank[:].rearrange("p (o e) -> p o e", o=1)),
                                             ALU.mult))
                link(nc.vector.reduce_max(best[:, :, 0], score[:], AX_X))
                link(nc.vector.tensor_tensor(onehot[:, k, :, :], score[:], across(best[:]), ALU.is_equal))
                if k + 1 < top_k:
                    link(nc.vector.scalar_tensor_tensor(out=logits[:], in0=onehot[:, k, :, :], scalar=-1e30,
                                                        in1=logits[:], op0=ALU.mult, op1=ALU.add))
            nc.vector.tensor_copy(onehot_b[:], onehot[:]).then_inc(onehot_ready, 1)
            if top_k == 2:
                nc.vector.tensor_tensor(gap[:], top[:, 1, :, 0], top[:, 0, :, 0], ALU.subtract).then_inc(gap_ready, 1)
                dve.wait_ge(exp_ready, 1)
                link(nc.vector.tensor_scalar(gap_sum[:], gap[:], 1.0, None, ALU.add))
                link(nc.vector.reciprocal(weight[:, 0, :], gap_sum[:]))
                nc.vector.tensor_tensor(weight[:, 1, :], gap[:], weight[:, 0, :], ALU.mult).then_inc(weight_ready, 1)
            dve.wait_ge(rank_psum, 1)
            cnt = p_rank[:, KT, :].rearrange("p (e o) -> p e o", o=1).broadcast_to([P, E, KT + 1])
            limit = steps[:, 0:KT + 1].rearrange("p (o n) -> p o n", o=1).broadcast_to([P, E, KT + 1])
            link(nc.vector.tensor_scalar(over[:], limit, float(P), None, ALU.mult))
            link(nc.vector.tensor_tensor(over[:], cnt, over[:], ALU.is_gt))
            link(nc.vector.reduce_sum(tiles[:], over[:], AX_X))
            link(nc.vector.tensor_tensor_scan(ends[:], tiles[:], tiles[:], 0.0, ALU.add, ALU.bypass))
            link(nc.vector.tensor_tensor(starts[:], ends[:], tiles[:], ALU.subtract))
            link(nc.vector.tensor_scalar(starts[:], starts[:], float(P), None, ALU.mult))
            over_tiles = lambda a: a.rearrange("p (o e) -> p o e", o=1).broadcast_to([P, KT, E])
            link(nc.vector.tensor_tensor(place[:], p_rank[:, 0:KT, :], over_tiles(starts[:]), ALU.add))
            link(nc.vector.tensor_tensor(place[:], place[:], onehot[:].rearrange("p k t e -> p (k t) e"), ALU.mult))
            link(nc.vector.reduce_sum(pos_f[:], place[:], AX_X))
            nc.vector.tensor_copy(pos[:], pos_f[:]).then_inc(pos_ready, 1)
            link(nc.vector.tensor_tensor(passed[:], ends[:].rearrange("p (o e) -> p o e", o=1)
                                         .broadcast_to([P, NS, E]),
                                         steps[:, 0:NS].rearrange("p (s o) -> p s o", o=1)
                                         .broadcast_to([P, NS, E]), ALU.is_le))
            link(nc.vector.reduce_sum(expert_f[:], passed[:], AX_X))
            link(nc.vector.tensor_scalar(expert_f[:], expert_f[:], float(E - 1), None, ALU.min))
            nc.vector.tensor_copy(expert[:], expert_f[:]).then_inc(expert_ready, 1)
            link.done()

            def hidden(s, k, later):
                dve.wait_ge(sg_ready, s + 1)
                dve.wait_ge(u_psum, s + 1)
                if later:
                    dve.wait_ge(h_psum, s - 1)
                nc.vector.tensor_tensor(hid[:, k, :], sg[:, k, :], p_u[:, k, 0:I], ALU.mult).then_inc(hid_ready, 1)

            def turned(s, k, later):
                dve.wait_ge(h_psum, s + 1)
                if later:
                    dve.wait_ge(y_psum, s - 1)
                full = len(CHUNKS) - 1
                nc.vector.tensor_copy(hidT[:, k, 0:full, :], p_h[:, 0:full * P]
                                      .rearrange("p (c n) -> p c n", n=P)).then_inc(hidT_ready, 1)
                rows = CHUNKS[-1][1]
                nc.vector.tensor_copy(hidT[0:rows, k, full, :], p_h[0:rows, full * P:]).then_inc(hidT_ready, 1)

            hidden(0, 0, False)
            hidden(1, 1, False)
            turned(0, 0, False)
            hidden(2, 0, True)
            turned(1, 1, False)
            with dve.Fori(0, (NS - 3) // 2) as m:
                for j in range(2):
                    s = 2 * m + 3 + j
                    hidden(s, (1 + j) % 2, True)
                    turned(s - 1, j, True)
            turned(NS - 1, (NS - 1) % 2, True)
            if top_k == 2:
                dve.wait_ge(weight_ready, 1)
            for v in range(KT):
                k, t = divmod(v, NT)
                dve.wait_ge(gathered, 16 * KT)
                if k:
                    dve.wait_ge(chain, ROUTE_LINKS[top_k] + v - NT + 1)
                if top_k == 2:
                    ins = nc.vector.scalar_tensor_tensor(out=x_sb[:, t, :], in0=back[:, v, :],
                                                         scalar=weight[:, k, t:t + 1], in1=x_sb[:, t, :],
                                                         op0=ALU.mult, op1=ALU.add)
                else:
                    ins = nc.vector.tensor_tensor(x_sb[:, t, :], back[:, v, :], x_sb[:, t, :], ALU.add)
                ins.then_inc(chain, 1)

        @block.scalar
        def _(act):
            ln_scalar(act)
            for g in range(NGRP):
                act.wait_ge(xnT_psum, g + 1)
                if g >= 2:
                    act.wait_ge(logit_psum_part, g - 1)
                nc.scalar.copy(xnT[:, g % 2, :], p_turn[:]).then_inc(xnT_ready, 1)
            if top_k == 2:
                act.wait_ge(gap_ready, 1)
                nc.scalar.activation(gap[:], gap[:], ACT.Exp).then_inc(exp_ready, 1)

            def into(s, k, later):
                act.wait_ge(xs_psum, s + 1)
                if later:
                    act.wait_ge(u_psum, s - 1)
                nc.scalar.copy(xsT[:, k, :], p_turn[:, k * P:(k + 1) * P]).then_inc(xsT_ready, 1)

            def gate(s, k, later):
                act.wait_ge(g_psum, s + 1)
                if later:
                    act.wait_ge(hid_ready, s - 1)
                nc.scalar.activation(sg[:, k, :], p_g[:, k, 0:I], ACT.Silu).then_inc(sg_ready, 1)

            def result(s, k, later):
                act.wait_ge(y_psum, s + 1)
                if later is not None:
                    act.wait_ge(y_out[k], later)
                nc.scalar.copy(y[:, k, :], p_y[:]).then_inc(y_ready, 1)

            into(0, 0, False)
            gate(0, 0, False)
            into(1, 1, False)
            gate(1, 1, False)
            into(2, 0, True)
            result(0, 0, None)
            gate(2, 0, True)
            result(1, 1, None)
            with act.Fori(0, (NS - 3) // 2) as m:
                for j in range(2):
                    s = 2 * m + 3 + j
                    into(s, (1 + j) % 2, True)
                    gate(s, (1 + j) % 2, True)
                    result(s - 1, j, 16 * (m + 1))
            result(NS - 1, (NS - 1) % 2, 16 * ((NS - 1) // 2))

        @block.gpsimd
        def _(pool):
            pool.wait_ge(cleared, 16)
            pool.wait_ge(pos_ready, 1)
            for v in range(KT):
                nc.gpsimd.indirect_dma_start(sorted_x, bass.IndirectOffsetOnAxis(ap=pos[:, v:v + 1], axis=0),
                                             xn[:, v % NT, :], None).then_inc(moved, 16)
            pool.wait_ge(y_out[0], 16 * ((NS + 1) // 2))
            pool.wait_ge(y_out[1], 16 * (NS // 2))
            for v in range(KT):
                nc.gpsimd.indirect_dma_start(back[:, v, :], None, sorted_y,
                                             bass.IndirectOffsetOnAxis(ap=pos[:, v:v + 1], axis=0)
                                             ).then_inc(gathered, 16)

        @block.tensor
        def _(pe):
            mm = nc.tensor.matmul
            pe.wait_ge(loaded, 16 * LOADS)
            pe.wait_ge(ones_ready, 1)
            for g in range(NGRP):
                pe.wait_ge(xn_ready, g + 1)
                if g:
                    pe.wait_ge(xnT_ready, g)
                for t in range(TT):
                    last = nc.tensor.transpose(p_turn[:, t * P:(t + 1) * P], xn[:, g * TT + t, :], ident[:])
                last.then_inc(xnT_psum, 1)
                pe.wait_ge(xnT_ready, g + 1)
                for t in range(TT):
                    last = mm(p_rank[:, g * TT + t, :], xnT[:, g % 2, t * P:(t + 1) * P], wr[:],
                              start=(g == 0 and t == 0), stop=(g == NGRP - 1 and t == TT - 1), skip_group_check=True)
                if g < NGRP - 1:
                    last.then_inc(logit_psum_part, 1)
            last.then_inc(logit_psum, 1)
            pe.wait_ge(onehot_ready, 1)
            flat = onehot_b[:].rearrange("p k t e -> p (k t) e")
            mm(p_rank[:, 0:KT, :], before[:], flat, start=True, stop=False, skip_group_check=True)
            for v in range(KT):
                last = mm(p_rank[:, v + 1:KT + 1, :], ones[:],
                          flat[:, v:v + 1, :].broadcast_to([P, KT - v, E]), start=False, stop=(v == KT - 1),
                          skip_group_check=True)
            last.then_inc(rank_psum, 1)
            pe.wait_ge(expert_ready, 1)

            def first_half(s, k, nth, later):
                pe.wait_ge(xs_in[k], nth)
                if later:
                    pe.wait_ge(xsT_ready, s - 1)
                nc.tensor.transpose(p_turn[:, k * P:(k + 1) * P], xs[:, k, :], ident[:]).then_inc(xs_psum, 1)
                e = pe.value_load(expert[0:1, bass.ds(s, 1)], min_val=0, max_val=E - 1)
                pe.wait_ge(xsT_ready, s + 1)
                if later:
                    pe.wait_ge(sg_ready, s - 1)
                mm(p_g[:, k, 0:I], xsT[:, k, :], wg[:, bass.ds(e, 1), :], start=True, stop=True).then_inc(g_psum, 1)
                if later:
                    pe.wait_ge(hid_ready, s - 1)
                mm(p_u[:, k, 0:I], xsT[:, k, :], wu[:, bass.ds(e, 1), :], start=True, stop=True).then_inc(u_psum, 1)

            def second_half(s, k, later):
                pe.wait_ge(hid_ready, s + 1)
                if later:
                    pe.wait_ge(hidT_ready, 2 * s)
                for c, (c0, cn) in enumerate(CHUNKS):
                    last = nc.tensor.transpose(p_h[0:cn, c * P:(c + 1) * P], hid[:, k, c0:c0 + cn], ident[:])
                last.then_inc(h_psum, 1)
                e = pe.value_load(expert[0:1, bass.ds(s, 1)], min_val=0, max_val=E - 1)
                pe.wait_ge(hidT_ready, 2 * s + 2)
                if later:
                    pe.wait_ge(y_ready, s)
                for c, (c0, cn) in enumerate(CHUNKS):
                    last = mm(p_y[:], hidT[0:cn, k, c, :], wd[0:cn, c, bass.ds(e, 1), :],
                              start=(c == 0), stop=(c == len(CHUNKS) - 1))
                last.then_inc(y_psum, 1)

            first_half(0, 0, 16, False)
            first_half(1, 1, 16, False)
            second_half(0, 0, False)
            first_half(2, 0, 32, True)
            second_half(1, 1, True)
            with pe.Fori(0, (NS - 3) // 2) as m:
                for j in range(2):
                    s = 2 * m + 3 + j
                    first_half(s, (1 + j) % 2, 16 * (m + 2 + j), True)
                    second_half(s - 1, j, True)
            second_half(NS - 1, (NS - 1) % 2, True)


DI, DS, DC = 256, 16, 4
HALVES = DI // P
QUAD = 32


def state_space(nc, x_sb, A):
    with ExitStack() as ctx:
        sb = lambda name, shape, dt=F32: ctx.enter_context(nc.sbuf_tensor(f"m_{name}", shape, dt))
        sem = lambda name: ctx.enter_context(nc.semaphore(f"m_{name}"))
        ps = lambda name, shape: ctx.enter_context(nc.psum_tensor(f"m_{name}", shape, F32))

        w_in = sb("w_in", [P, 2 * DI])
        w_delta = sb("w_delta", [P, DI])
        w_bc = sb("w_bc", [P, 3 * QUAD])
        w_out = sb("w_out", [P, HALVES, D])
        conv_w = sb("conv_w", [P, HALVES, DC])
        conv_b, b_delta, skip = sb("conv_b", [P, HALVES]), sb("b_delta", [P, HALVES]), sb("skip", [P, HALVES])
        a_log, a_neg = sb("a_log", [P, HALVES, DS]), sb("a_neg", [P, HALVES, DS])
        state_rows = sb("state_rows", [P, 2 * DS, P], BF16)
        ident = sb("ident", [P, P])
        xn = sb("xn", [P, TT, D])
        xnT = sb("xnT", [P, S])
        gate = sb("gate", [P, HALVES, S])
        xi = sb("xi", [P, HALVES, DC - 1 + S])
        xc = sb("xc", [P, HALVES, S])
        size, rate = sb("size", [P, HALVES, S]), sb("rate", [P, HALVES, S])
        soft = sb("soft", [P, HALVES, S])
        dx = sb("dx", [P, HALVES, S])
        bc_rest = sb("bc_rest", [P, S])
        bc_mid = sb("bc_mid", [P, S], BF16)
        bc = sb("bc", [P, S], BF16)
        b_all = sb("b_all", [P, 2, S])
        decay = sb("decay", [P, 2, HALVES, S])
        inflow = sb("inflow", [P, 2, HALVES, S])
        state = sb("state", [P, 2, HALVES, S])
        seen = sb("seen", [P, 2, HALVES, S])
        skipped = sb("skipped", [P, HALVES, S])
        outT = sb("outT", [P, S])
        proj = ps("proj", [P, 2, S])
        p_b, p_c = ps("b", [P, 2, S]), ps("c", [P, 2, S])
        p_out = ps("out", [P, S])
        p_turn = ps("turn", [P, S])

        loaded = sem("loaded")
        a_exp, consts_ready = sem("a_exp"), sem("consts_ready")
        xn_ready, xnT_psum, xnT_ready = sem("xn_ready"), sem("xnT_psum"), sem("xnT_ready")
        proj_psum, proj_read = sem("proj_psum"), sem("proj_read")
        gate_ready, size_ready = sem("gate_ready"), sem("size_ready")
        bc_hi, bc_sub, bc_mid_ready, bc_ready = sem("bc_hi"), sem("bc_sub"), sem("bc_mid_ready"), sem("bc_ready")
        rate_ready, dx_ready = sem("rate_ready"), sem("dx_ready")
        b_psum, b_ready, c_psum = sem("b_psum"), sem("b_ready"), sem("c_psum")
        decay_ready, inflow_ready = sem("decay_ready"), sem("inflow_ready")
        state_ready, seen_ready, out_psum = sem("state_ready"), sem("seen_ready"), sem("out_psum")
        skip_ready, outT_ready, turn_psum, x_done = (sem("skip_ready"), sem("outT_ready"),
                                                     sem("turn_psum"), sem("x_done"))
        act_chain, dve_chain = sem("act_chain"), sem("dve_chain")
        mv, rstd, ln_vector, ln_scalar = layer_norm_stats(nc, ctx, "m", x_sb)
        LOADS = 11
        PROJ = ([("gate", 0), ("x", 0), ("gate", 1), ("x", 1), ("bc", 0), ("delta", 0), ("delta", 1)])
        NP_ = len(PROJ)

        block = ctx.enter_context(nc.Block())

        @block.sync
        def _(sp):
            for dst, name in ((w_in, "w_in"), (w_delta, "w_delta"), (w_bc, "w_bc"), (w_out, "w_out"),
                              (conv_w, "conv_w"), (conv_b, "conv_b"), (b_delta, "b_delta"), (skip, "skip"),
                              (a_log, "a_log"), (state_rows, "state_rows"), (ident, "ident")):
                sp.dma_start(dst[:], A[name if name == "ident" else f"m_{name}"]).then_inc(loaded, 16)

        @block.vector
        def _(dve):
            nc.vector.memset(xi[:, :, 0:DC - 1], 0.0).then_inc(consts_ready, 1)
            ln_vector(dve)
            dve.wait_ge(loaded, 16 * LOADS)
            dve.wait_ge(a_exp, 1)
            nc.vector.tensor_scalar(a_neg[:], a_neg[:], -1.0, None, ALU.mult).then_inc(consts_ready, 1)
            dve.wait_ge(consts_ready, 2)

            def turn(b, first):
                link = Chain(dve, dve_chain, b, SSM_LINKS)
                if not first:
                    dve.wait_ge(xnT_psum, b)
                for t in range(TT):
                    last = nc.vector.tensor_scalar(xn[:, t, :], x_sb[:, bass.ds(b * TT + t, 1), :],
                                                   mv[:, bass.ds(b * TT + t, 1), 0],
                                                   rstd[:, bass.ds(b * TT + t, 1)],
                                                   ALU.subtract, ALU.mult)
                last.then_inc(xn_ready, 1)
                for half in range(HALVES):
                    dve.wait_ge(gate_ready, b * HALVES + half + 1)
                    dve.wait_ge(proj_psum, b * NP_ + 2 * half + 2)
                    link(nc.vector.tensor_tensor(xi[:, half, DC - 1:], gate[:, half, :], proj[:, 1, :], ALU.mult))
                dve.wait_ge(bc_hi, b + 1)
                nc.vector.tensor_tensor(bc_rest[0:3 * QUAD, :], proj[0:3 * QUAD, 0, :], bc[0:3 * QUAD, :],
                                        ALU.subtract).then_inc(bc_sub, 1)
                dve.wait_ge(bc_sub, b + 1)
                link(nc.vector.tensor_copy(bc_mid[0:3 * QUAD, :], bc_rest[0:3 * QUAD, :]))
                link(nc.vector.tensor_copy(bc[QUAD:2 * QUAD, :], bc_mid[QUAD:2 * QUAD, :]))
                nc.vector.tensor_tensor(bc[2 * QUAD:3 * QUAD, :], bc_rest[2 * QUAD:3 * QUAD, :],
                                        bc_mid[2 * QUAD:3 * QUAD, :], ALU.subtract).then_inc(bc_ready, 1)
                for half in range(HALVES):
                    dve.wait_ge(proj_psum, b * NP_ + 6 + half)
                    nc.vector.tensor_scalar(rate[:, half, :], proj[:, (5 + half) % 2, :], b_delta[:, half:half + 1],
                                            0.0, ALU.add, ALU.max).then_inc(proj_read, 1)
                for half in range(HALVES):
                    link(nc.vector.tensor_scalar(xc[:, half, :], xi[:, half, 0:S], conv_w[:, half, 0:1],
                                                 conv_b[:, half:half + 1], ALU.mult, ALU.add))
                    for k in range(1, DC):
                        link(nc.vector.scalar_tensor_tensor(out=xc[:, half, :], in0=xi[:, half, k:k + S],
                                                            scalar=conv_w[:, half, k:k + 1], in1=xc[:, half, :],
                                                            op0=ALU.mult, op1=ALU.add))
                dve.wait_ge(size_ready, b + 1)
                dve.wait_ge(proj_read, (b + 1) * HALVES)
                nc.vector.tensor_tensor(rate[:], rate[:], soft[:], ALU.add).then_inc(rate_ready, 1)
                dve.wait_ge(rate_ready, b + 1)
                nc.vector.tensor_tensor(dx[:], rate[:], xc[:], ALU.mult).then_inc(dx_ready, 1)
                for half in range(HALVES):
                    ins = nc.vector.tensor_scalar(skipped[:, half, :], xc[:, half, :], skip[:, half:half + 1],
                                                  None, ALU.mult)
                ins.then_inc(skip_ready, 1)

                for n in range(DS):
                    k = n % 2
                    dve.wait_ge(inflow_ready, b * DS + n + 1)
                    dve.wait_ge(decay_ready, b * DS + n + 1)
                    for half in range(HALVES):
                        last = nc.vector.tensor_tensor_scan(state[:, k, half, :], decay[:, k, half, :],
                                                            inflow[:, k, half, :], 0.0, ALU.mult, ALU.add)
                    last.then_inc(state_ready, 1)
                    dve.wait_ge(state_ready, b * DS + n + 1)
                    dve.wait_ge(c_psum, b * DS + n + 1)
                    if n >= 2 or not first:
                        dve.wait_ge(out_psum, b * (DS + 1) + n - (n < 2))
                    nc.vector.tensor_tensor(seen[:, k, :, :], state[:, k, :, :],
                                            p_c[:, k, :].rearrange("p (o t) -> p o t", o=1)
                                            .broadcast_to([P, HALVES, S]), ALU.mult).then_inc(seen_ready, 1)
                dve.wait_ge(turn_psum, b + 1)
                xb = x_sb[:, bass.ds(b * TT, TT), :]
                link(nc.vector.tensor_tensor(xb, p_turn[:].rearrange("p (n d) -> p n d", n=TT), xb, ALU.add))
                link.done()

            turn(0, True)
            with dve.Fori(1, B) as b:
                turn(b, False)

        @block.gpsimd
        def _(pool):
            def turn(b, first):
                pool.wait_ge(dx_ready, b + 1)
                for n in range(DS):
                    k = n % 2
                    pool.wait_ge(b_ready, b * DS + n + 1)
                    if n >= 2 or not first:
                        pool.wait_ge(state_ready, b * DS + n - 1)
                    nc.gpsimd.tensor_tensor(inflow[:, k, :, :], dx[:], b_all[:, k, :]
                                            .rearrange("p (o t) -> p o t", o=1)
                                            .broadcast_to([P, HALVES, S]), ALU.mult).then_inc(inflow_ready, 1)

            turn(0, True)
            with pool.Fori(1, B) as b:
                turn(b, False)

        @block.scalar
        def _(act):
            ln_scalar(act)
            act.wait_ge(loaded, 16 * LOADS)
            nc.scalar.activation(a_neg[:], a_log[:], ACT.Exp).then_inc(a_exp, 1)

            def turn(b, first):
                link = Chain(act, act_chain, b, SSM_ACT_LINKS)
                act.wait_ge(xnT_psum, b + 1)
                nc.scalar.copy(xnT[:], p_turn[:]).then_inc(xnT_ready, 1)
                for half in range(HALVES):
                    act.wait_ge(proj_psum, b * NP_ + 2 * half + 1)
                    nc.scalar.activation(gate[:, half, :], proj[:, 0, :], ACT.Silu).then_inc(gate_ready, 1)
                act.wait_ge(proj_psum, b * NP_ + 5)
                if not first:
                    act.wait_ge(c_psum, b * DS)
                nc.scalar.copy(bc[0:3 * QUAD, :], proj[0:3 * QUAD, 0, :]).then_inc(bc_hi, 1)
                for half in range(HALVES):
                    act.wait_ge(proj_psum, b * NP_ + 6 + half)
                    act.wait_ge(proj_read, b * HALVES + half + 1)
                    link(nc.scalar.activation(size[:, half, :], proj[:, (5 + half) % 2, :], ACT.Abs,
                                              bias=b_delta[:, half:half + 1]))
                link(nc.scalar.activation(size[:], size[:], ACT.Exp, scale=-1.0))
                nc.scalar.activation(soft[:], size[:], ACT.Ln, bias=1.0).then_inc(size_ready, 1)
                act.wait_ge(rate_ready, b + 1)
                for n in range(DS):
                    k = n % 2
                    act.wait_ge(b_psum, b * DS + n + 1)
                    if n >= 2 or not first:
                        act.wait_ge(inflow_ready, b * DS + n - 1)
                    nc.scalar.copy(b_all[:, k, :], p_b[:, k, :]).then_inc(b_ready, 1)
                    if n >= 2 or not first:
                        act.wait_ge(state_ready, b * DS + n - 1)
                    for half in range(HALVES):
                        last = nc.scalar.activation(decay[:, k, half, :], rate[:, half, :], ACT.Exp,
                                                    scale=a_neg[:, half, n:n + 1])
                    last.then_inc(decay_ready, 1)
                act.wait_ge(out_psum, (b + 1) * (DS + 1))
                nc.scalar.copy(outT[:], p_out[:]).then_inc(outT_ready, 1)
                link.done()

            turn(0, True)
            with act.Fori(1, B) as b:
                turn(b, False)

        @block.tensor
        def _(pe):
            mm = nc.tensor.matmul
            pe.wait_ge(loaded, 16 * LOADS)

            def turn(b, first):
                pe.wait_ge(xn_ready, b + 1)
                if not first:
                    pe.wait_ge(dve_chain, b * SSM_LINKS)
                for t in range(TT):
                    last = nc.tensor.transpose(p_turn[:, t * P:(t + 1) * P], xn[:, t, :], ident[:])
                last.then_inc(xnT_psum, 1)
                pe.wait_ge(xnT_ready, b + 1)
                for i, (what, half) in enumerate(PROJ):
                    rows = P
                    if what == "gate":
                        weights = w_in[:, half * P:(half + 1) * P]
                    elif what == "x":
                        weights = w_in[:, DI + half * P:DI + (half + 1) * P]
                    elif what == "delta":
                        weights = w_delta[:, half * P:(half + 1) * P]
                    else:
                        weights, rows = w_bc[:], 3 * QUAD
                    bank = {"gate": 0, "x": 1, "bc": 0, "delta": (1 + half) % 2}[what]
                    if i == 2:
                        pe.wait_ge(gate_ready, b * HALVES + 1)
                    if i == 3:
                        pe.wait_ge(dve_chain, b * SSM_LINKS + 1)
                    if i == 4:
                        pe.wait_ge(gate_ready, b * HALVES + 2)
                    if i == 5:
                        pe.wait_ge(dve_chain, b * SSM_LINKS + 2)
                    if i == 6:
                        pe.wait_ge(bc_sub, b + 1)
                    mm(proj[0:rows, bank, :], weights, xnT[:], start=True, stop=True).then_inc(proj_psum, 1)
                pe.wait_ge(bc_ready, b + 1)

                def spread(n):
                    k = n % 2
                    if n >= 2 or not first:
                        pe.wait_ge(b_ready, b * DS + n - 1)
                    mm(p_b[:, k, :], state_rows[0:3 * QUAD, n, :], bc[0:3 * QUAD, :],
                       start=True, stop=True).then_inc(b_psum, 1)
                    if n >= 2 or not first:
                        pe.wait_ge(seen_ready, b * DS + n - 1)
                    mm(p_c[:, k, :], state_rows[0:3 * QUAD, DS + n, :], bc[0:3 * QUAD, :],
                       start=True, stop=True).then_inc(c_psum, 1)

                spread(0)
                spread(1)
                pe.wait_ge(skip_ready, b + 1)
                if not first:
                    pe.wait_ge(outT_ready, b)
                for half in range(HALVES):
                    last = mm(p_out[:], w_out[:, half, :], skipped[:, half, :], start=(half == 0), stop=False)
                last.then_inc(out_psum, 1)
                for n in range(DS):
                    k = n % 2
                    pe.wait_ge(seen_ready, b * DS + n + 1)
                    for half in range(HALVES):
                        last = mm(p_out[:], w_out[:, half, :], seen[:, k, half, :], start=False,
                                  stop=(n == DS - 1 and half == HALVES - 1))
                    last.then_inc(out_psum, 1)
                    if n + 2 < DS:
                        spread(n + 2)
                pe.wait_ge(outT_ready, b + 1)
                for t in range(TT):
                    last = nc.tensor.transpose(p_turn[:, t * P:(t + 1) * P], outT[:, t * P:(t + 1) * P], ident[:])
                last.then_inc(turn_psum, 1)

            turn(0, True)
            with pe.Fori(1, B) as b:
                turn(b, False)


def store(nc, x_sb, out):
    with ExitStack() as ctx:
        stored = ctx.enter_context(nc.semaphore("stored"))
        block = ctx.enter_context(nc.Block())

        @block.sync
        def _(sp):
            for b in range(B):
                sp.dma_start(out[b].rearrange("(n p) d -> p n d", p=P),
                             x_sb[:, b * TT:(b + 1) * TT, :]).then_inc(stored, 16)
            sp.wait_ge(stored, 16 * B)


def program(nc, A, out):
    with ExitStack() as ctx:
        x_sb = ctx.enter_context(nc.sbuf_tensor("x_sb", [P, NT, D], F32))
        attention(nc, x_sb, A)
        routed_ffn(nc, x_sb, A, 'f0', 1)
        state_space(nc, x_sb, A)
        routed_ffn(nc, x_sb, A, 'f1', 2)
        store(nc, x_sb, out)


def host_arrays(inputs):
    import numpy as np
    i = {k: np.asarray(v) for k, v in inputs.items()}
    bf16_bits = lambda a: (np.asarray(a, np.float32).view(np.uint32) >> 16).astype(np.uint16)
    turned = lambda a: np.ascontiguousarray(np.swapaxes(a, -1, -2))
    r_major = lambda a: np.ascontiguousarray(a.reshape(a.shape[0], H, HD).swapaxes(1, 2).reshape(a.shape[0], D))
    A = {"x": i["L0_attn_x"]}
    A["wq"], A["wk"] = (r_major(turned(i[f"L0_attn_W{n}"])) for n in "qk")
    A["wv"], A["wo"] = turned(i["L0_attn_Wv"]), turned(i["L0_attn_Wo"])
    A["bq"], A["bk"] = (turned(r_major(i[f"L0_attn_b{n}"][None])) for n in "qk")
    A["bv"], A["bo"] = i["L0_attn_bv"][None], i["L0_attn_bo"][None]
    A["lam"] = i["L0_attn_lambda_attn"].reshape(1, 1)
    J = np.zeros((HD, H, HD, H), i["L0_attn_J_attn"].dtype)
    for h in range(H):
        J[:, h, :, h] = i["L0_attn_J_attn"][h]
    A["J"] = J.reshape(D, D)
    A["ident"] = np.eye(P, dtype=np.float32)
    A["ident_b"] = bf16_bits(np.eye(P))
    after = np.triu(np.ones((P, P), bool), 1)
    A["mask_q"] = bf16_bits(np.where(after, -1e30, 0.0))
    A["mask_k"] = np.ascontiguousarray(A["mask_q"].T)
    rows = np.zeros((P, H, P), np.float32)
    for h in range(H):
        rows[[h, H + h, 2 * H + h], h, :] = 1.0
    A["head_rows"] = bf16_bits(rows)
    for tag, names in (("f0", ("router_w", "gate_w", "up_w", "down_w")),
                       ("f1", ("w_router", "w_gate", "w_up", "w_down"))):
        r, g, u, d = (i[f"L{tag[1]}_ffn_{n}"] for n in names)
        A[f"{tag}_wr"] = turned(r)
        A[f"{tag}_wg"], A[f"{tag}_wu"] = (np.ascontiguousarray(a.transpose(2, 0, 1)) for a in (g, u))
        A[f"{tag}_wd"] = np.ascontiguousarray(d.transpose(2, 0, 1))
    A["m_w_in"], A["m_w_delta"] = i["L1_attn_W_in"], i["L1_attn_W_delta"]
    A["m_w_bc"] = np.concatenate([i["L1_attn_W_B"], i["L1_attn_W_C"]] * 3, axis=1)
    halves = lambda a: np.ascontiguousarray(a.reshape(HALVES, P, -1).swapaxes(0, 1))
    A["m_w_out"], A["m_conv_w"], A["m_a_log"] = (halves(i[f"L1_attn_{n}"]) for n in ("W_out", "conv_w", "A_log"))
    A["m_conv_b"], A["m_b_delta"], A["m_skip"] = (halves(i[f"L1_attn_{n}"])[:, :, 0]
                                                  for n in ("conv_b", "b_delta", "D"))
    picked = np.zeros((P, 2 * DS, P), np.float32)
    for n in range(2 * DS):
        picked[[n, QUAD + n, 2 * QUAD + n], n, :] = 1.0
    A["m_state_rows"] = bf16_bits(picked)
    A["before"] = bf16_bits(after)
    A["rank"] = np.arange(E, 0, -1, dtype=np.float32)[None]
    A["steps"] = np.arange(64, dtype=np.float32)[None]
    return A


def kernel(**inputs):
    import concourse.bacc as bacc
    from concourse.bass_utils import run_bass_kernel_spmd

    nc = bacc.Bacc("TRN2", target_bir_lowering=False, num_devices=1)
    arrays = host_arrays(inputs)
    aps = {n: nc.dram_tensor(f"in_{n}", a.shape, mybir.dt.from_np(a.dtype), kind="ExternalInput").ap()
           for n, a in arrays.items()}
    out = nc.dram_tensor("out", (B, S, D), F32, kind="ExternalOutput").ap()
    for n, a in arrays.items():
        if a.dtype.kind == "u":
            aps[n] = aps[n].bitcast(BF16)
    program(nc, aps, out)
    result = run_bass_kernel_spmd(nc, [{f"in_{n}": a for n, a in arrays.items()}], core_ids=[0])
    return result.results[0]["out"]
```

```python
from contextlib import ExitStack

import concourse.bass as bass
from concourse import mybir

F32 = mybir.dt.float32
BF16 = mybir.dt.bfloat16
I32 = mybir.dt.int32
U32 = mybir.dt.uint32
ACT = mybir.ActivationFunctionType
ALU = mybir.AluOpType
AX_X = mybir.AxisListType.X

P = 128
B, S, D = 4, 512, 128
H, HD = 16, 8
TT = S // P
NT = B * TT
EPS = 1e-5
QK_SCALE = HD ** -0.5
HP = 32
GROUP = P // HP
SCORE_COLS = sum(S - P * j for j in range(TT))


ROWS = 12 * HD
Q_ORDER = (0, 0, 1, 1, 0, 2)
K_ORDER = (0, 1, 0, 1, 2, 0)
TWO_ONES = 1 + 0x3F80 * 2.0 ** -23


def within(s, low, high=None):
    return not isinstance(s, int) or (low <= s and (high is None or s < high))


class Chain:

    def __init__(self, eng, sem):
        self.eng, self.sem, self.n = eng, sem, 0

    def __call__(self, ins):
        self.n += 1
        ins.then_inc(self.sem, 1)
        self.eng.wait_ge(self.sem, self.n)


def layer_norm_stats(nc, ctx, tag, x_sb):
    stats = ctx.enter_context(nc.sbuf_tensor(f"{tag}_stats", [P, NT, 6], F32))
    mv = ctx.enter_context(nc.sbuf_tensor(f"{tag}_mv", [P, NT, 2], F32))
    std = ctx.enter_context(nc.sbuf_tensor(f"{tag}_std", [P, NT], F32))
    rstd = ctx.enter_context(nc.sbuf_tensor(f"{tag}_rstd", [P, NT], F32))
    eps = ctx.enter_context(nc.sbuf_tensor(f"{tag}_eps", [P, 1], F32))
    stats_done = ctx.enter_context(nc.semaphore(f"{tag}_stats_done"))
    mv_done = ctx.enter_context(nc.semaphore(f"{tag}_mv_done"))
    std_done = ctx.enter_context(nc.semaphore(f"{tag}_std_done"))
    rstd_done = ctx.enter_context(nc.semaphore(f"{tag}_rstd_done"))

    def on_vector(dve):
        nc.vector.memset(eps[:], EPS).then_inc(mv_done, 1)
        for t in range(NT):
            nc.vector.bn_stats(stats[:, t, :], x_sb[:, t, :]).then_inc(stats_done, 1)
        for t in range(NT):
            dve.wait_ge(stats_done, t + 1)
            nc.vector.bn_aggr(mv[:, t, :], stats[:, t, :]).then_inc(mv_done, 1)
        dve.wait_ge(std_done, 1)
        nc.vector.reciprocal(rstd[:], std[:]).then_inc(rstd_done, 1)
        dve.wait_ge(rstd_done, 1)

    def on_scalar(act):
        act.wait_ge(mv_done, NT + 1)
        nc.scalar.activation(std[:], mv[:, :, 1], ACT.Sqrt, bias=eps[:]).then_inc(std_done, 1)

    return mv, rstd, on_vector, on_scalar


def attention(nc, x_sb, A):
    with ExitStack() as ctx:
        sb = lambda name, shape, dt=F32: ctx.enter_context(nc.sbuf_tensor(f"a_{name}", shape, dt))
        sem = lambda name: ctx.enter_context(nc.semaphore(f"a_{name}"))
        ps = lambda name, shape: ctx.enter_context(nc.psum_tensor(f"a_{name}", shape, F32))

        w = {n: sb(n, [P, D]) for n in ("wq", "wk", "wv", "wo", "J")}
        ident, ident_b = sb("ident", [P, P]), sb("ident_b", [P, P], BF16)
        mask_q = sb("mask_q", [P, P], BF16)
        mask_k = sb("mask_k", [P, P], BF16)
        bq, bk, lam, bqs = (sb(n, [P, 1]) for n in ("bq", "bk", "lam", "bqs"))
        bv, bo = sb("bv", [P, D]), sb("bo", [1, D])
        one = sb("one", [1, P])
        wqs = sb("wqs", [P, D])
        xn, xnT = sb("xn", [P, TT, D]), sb("xnT", [P, S])
        tanh_q = sb("tanh_q", [P, S])
        feat, rest = sb("feat", [P, 4, S]), sb("rest", [P, 4, S])
        parts = sb("parts", [P, 4, 3, S], BF16)
        QA, KA = (sb(n, [P, 2, H, S], BF16) for n in ("QA", "KA"))
        V = sb("V", [P, 2, TT, H, HP])
        row_max = sb("row_max", [P, 2, TT, GROUP])
        max_rest = sb("max_rest", [P, TT, GROUP])
        max_parts = sb("max_parts", [P, 2, TT, 3, GROUP], BF16)
        neg_max = sb("neg_max", [3 * GROUP, 2, S], BF16)
        probs = sb("probs", [P, 2, GROUP, SCORE_COLS])
        OT = sb("OT", [P, 2, S])
        den = sb("den", [P, TT, GROUP])
        O = sb("O", [P, 2, TT, H, HD])
        OnT = sb("OnT", [P, S])
        st = ps("st", [P, 2, S])
        mx = ps("mx", [P, 2, 2, S])
        pv, misc = ps("pv", [P, S]), ps("misc", [P, S])

        loaded, consts_ready = sem("loaded"), sem("consts_ready")
        xn_ready = sem("xn_ready")
        misc_full, misc_free = sem("misc_full"), sem("misc_free")
        feat_ready, tq_ready = sem("feat_ready"), sem("tq_ready")
        hi_ready, rest_ready, mid_ready, lo_ready = (sem(n) for n in ("hi_ready", "rest_ready",
                                                                      "mid_ready", "lo_ready"))
        stacked = sem("stacked")
        mx_psum, mx_read, maxparts_ready = sem("mx_psum"), sem("mx_read"), sem("maxparts_ready")
        negmax_ready = sem("negmax_ready")
        max_rows = [sem("max_rows0"), sem("max_rows1")]
        st_psum, exp_done, pv_psum, ot_ready = sem("st_psum"), sem("exp_done"), sem("pv_psum"), sem("ot_ready")
        dve_chain, padded = sem("dve_chain"), sem("padded")
        mv, rstd, ln_vector, ln_scalar = layer_norm_stats(nc, ctx, "a", x_sb)
        LOADS = 18
        NG = H // GROUP
        NQ = B * NG
        ST_UNITS, MX_UNITS = 10, 8
        SPREADS = 4 * len(Q_ORDER)
        FIRST, LAST = -2, NQ + 1

        def pe_jobs(t):
            jobs = {}
            b = t // NG + 1
            if t >= 0 and t % NG == 0 and b < B:
                jobs |= {0: [("xnT", b)], 2: [("Q", b)], 4: [("K", b)], 6: [("V", b)], 8: [("J", b)]}
            if 0 <= t + 1 < NQ:
                jobs[1] = [("max", t + 1)]
            if 0 <= t - 1 < NQ:
                jobs[3] = [("pv", t - 1)]
                jobs[7] = [("tokens", t - 1)]
            if t - 5 >= 0 and (t - 5) % NG == 0:
                jobs[0] = [("OnT", (t - 5) // NG)]
                jobs[5] = [("out", (t - 5) // NG)]
            return jobs

        MISC = [(job, 0) for job in ("xnT", "Q", "K", "V", "J")]
        for t in range(FIRST, LAST + 1):
            jobs = pe_jobs(t)
            MISC += [job for u in sorted(jobs) for job in jobs[u] if job[0] != "pv"]

        def misc_turn(job, index):
            return MISC.index((job, index))

        def misc_read(turn):
            job, b = MISC[turn]
            if job in "QKJ":
                return feat_ready, 4 * b + {"Q": 1, "K": 2, "J": 4}[job]
            return misc_free, sum(j not in "QKJ" for j, _ in MISC[:turn + 1])

        block = ctx.enter_context(nc.Block())

        @block.sync
        def _(sp):
            for b in range(B):
                sp.dma_start(x_sb[:, b * TT:(b + 1) * TT, :],
                             A["x"][b].rearrange("(n p) d -> p n d", p=P)).then_inc(loaded, 16)
            for n in w:
                sp.dma_start(w[n][:], A[n]).then_inc(loaded, 16)
            for dst, name in ((ident, "ident"), (ident_b, "ident_b"), (mask_q, "mask_q"),
                              (mask_k, "mask_k"), (bq, "bq"), (bk, "bk"), (bo, "bo")):
                sp.dma_start(dst[:], A[name]).then_inc(loaded, 16)
            sp.dma_start(lam[:], A["lam"].broadcast_to([P, 1])).then_inc(loaded, 16)
            sp.dma_start(bv[:], A["bv"].broadcast_to([P, D])).then_inc(loaded, 16)
            for b in range(B):
                if b >= 2:
                    sp.wait_ge(st_psum, ST_UNITS * NG * (b - 1))
                for x, (stack, feature, order) in enumerate((
                        (QA, 0, Q_ORDER), (KA, 0, K_ORDER), (KA, 1, K_ORDER), (QA, 1, Q_ORDER))):
                    sp.wait_ge(lo_ready, 4 * b + x + 1)
                    for blk, part in enumerate(order):
                        r0 = 2 * HD * blk + HD * feature
                        sp.dma_start(stack[r0:r0 + HD, b % 2, :, :], parts[:, x, part, :]).then_inc(stacked, 16)

        @block.gpsimd
        def _(pool):
            nc.gpsimd.memset(V[:], 0.0).then_inc(padded, 1)
            pool.wait_ge(padded, 1)
            nc.gpsimd.memset(V[:, :, :, :, HD:HD + 1], 1.0).then_inc(padded, 1)
            pool.wait_ge(padded, 2)
            nc.gpsimd.memset(KA[ROWS:ROWS + 3, :, :, :].bitcast(F32), TWO_ONES).then_inc(padded, 1)
            pool.wait_ge(padded, 3)
            for b in range(B):
                for x in range(4):
                    pool.wait_ge(hi_ready, 4 * b + x + 1)
                    nc.gpsimd.tensor_tensor(rest[:, x, :], feat[:, x, :], parts[:, x, 0, :],
                                            ALU.subtract).then_inc(rest_ready, 1)
                    pool.wait_ge(mid_ready, 4 * b + x + 1)
                    nc.gpsimd.tensor_tensor(parts[:, x, 2, :], rest[:, x, :], parts[:, x, 1, :],
                                            ALU.subtract).then_inc(lo_ready, 1)

        @block.vector
        def _(dve):
            dve.wait_ge(loaded, 16 * LOADS)
            nc.vector.tensor_scalar(wqs[:], w["wq"][:], QK_SCALE, None, ALU.mult).then_inc(consts_ready, 1)
            nc.vector.tensor_scalar(bqs[:], bq[:], QK_SCALE, None, ALU.mult).then_inc(consts_ready, 1)
            nc.vector.memset(one[:], 1.0).then_inc(consts_ready, 1)
            ln_vector(dve)
            link = Chain(dve, dve_chain)

            def normalise(b):
                if b:
                    dve.wait_ge(misc_full, misc_turn("xnT", b - 1) + 1)
                for t in range(b * TT, (b + 1) * TT):
                    last = nc.vector.tensor_scalar(xn[:, t % TT, :], x_sb[:, t, :], mv[:, t, 0:1],
                                                   rstd[:, t:t + 1], ALU.subtract, ALU.mult)
                last.then_inc(xn_ready, 1)

            def values(b):
                dve.wait_ge(misc_full, misc_turn("V", b) + 1)
                dve.wait_ge(padded, 2)
                if b >= 2:
                    dve.wait_ge(pv_psum, NG * (b - 1))
                nc.vector.tensor_tensor(V[:, b % 2, :, :, 0:HD],
                                        misc[:].rearrange("p (n h r) -> p n h r", h=H, r=HD),
                                        bv[:].rearrange("p (o h r) -> p o h r", o=1, r=HD)
                                        .broadcast_to([P, TT, H, HD]), ALU.add).then_inc(misc_free, 1)

            def first_part(b, x):
                dve.wait_ge(feat_ready, 4 * b + x + 1)
                if b:
                    dve.wait_ge(stacked, 16 * SPREADS * b)
                nc.vector.tensor_copy(parts[:, x, 0, :], feat[:, x, :]).then_inc(hi_ready, 1)

            def second_part(b, x):
                dve.wait_ge(rest_ready, 4 * b + x + 1)
                nc.vector.tensor_copy(parts[:, x, 1, :], rest[:, x, :]).then_inc(mid_ready, 1)

            def maximum(q, i):
                p, r = divmod(i, TT)
                m = MX_UNITS * q + i
                dve.wait_ge(mx_psum, m + 1)
                nc.vector.reduce_max(row_max[:, q % 2, r, 2 * p:2 * p + 2], mx[:, m % 2, :, 0:P * (r + 1)],
                                     AX_X).then_inc(mx_read, 1)

            def maximum_parts(q):
                dve.wait_ge(mx_read, MX_UNITS * (q + 1))
                if q >= 2:
                    dve.wait_ge(misc_full, misc_turn("max", q - 2) + 1)
                mp = max_parts[:, q % 2, :, :, :]
                link(nc.vector.tensor_scalar(max_rest[:], row_max[:, q % 2, :, :], -1.0, None, ALU.mult))
                link(nc.vector.tensor_copy(mp[:, :, 0, :], max_rest[:]))
                link(nc.vector.tensor_tensor(max_rest[:], max_rest[:], mp[:, :, 0, :], ALU.subtract))
                link(nc.vector.tensor_copy(mp[:, :, 1, :], max_rest[:]))
                nc.vector.tensor_tensor(mp[:, :, 2, :], max_rest[:], mp[:, :, 1, :],
                                        ALU.subtract).then_inc(maxparts_ready, 1)

            def outputs(q):
                b, g = divmod(q, NG)
                dve.wait_ge(misc_full, misc_turn("tokens", q) + 1)
                if b >= 2 and g == 0:
                    dve.wait_ge(misc_full, misc_turn("OnT", b - 2) + 1)
                tok = misc[:].rearrange("p (n k c) -> p n k c", n=TT, k=GROUP)
                link(nc.vector.reciprocal(den[:], tok[:, :, :, HD]))
                nc.vector.tensor_tensor(O[:, b % 2, :, GROUP * g:GROUP * (g + 1), :], tok[:, :, :, 0:HD],
                                        den[:].rearrange("p n (k o) -> p n k o", o=1)
                                        .broadcast_to([P, TT, GROUP, HD]), ALU.mult).then_inc(misc_free, 1)

            def residual(b):
                dve.wait_ge(misc_full, misc_turn("out", b) + 1)
                xb = x_sb[:, b * TT:(b + 1) * TT, :]
                nc.vector.tensor_tensor(xb, misc[:].rearrange("p (n d) -> p n d", n=TT), xb,
                                        ALU.add).then_inc(misc_free, 1)

            normalise(0)
            for x in range(2):
                first_part(0, x)
                second_part(0, x)
            first_part(0, 2)
            values(0)
            second_part(0, 2)
            first_part(0, 3)
            second_part(0, 3)
            for t in range(FIRST, LAST + 1):
                b = t // NG + 1
                making = t >= 0 and b < B
                a_step, b_step = making and t % NG == 0, making and t % NG == 1
                for i in range(MX_UNITS):
                    if t + 2 < NQ:
                        maximum(t + 2, i)
                    if a_step:
                        if i == 3:
                            first_part(b, 0)
                        if i == 5:
                            second_part(b, 0)
                            first_part(b, 1)
                            values(b)
                        if i == 7:
                            first_part(b, 2)
                            second_part(b, 1)
                    if b_step:
                        if i == 1:
                            second_part(b, 2)
                            first_part(b, 3)
                        if i == 4:
                            second_part(b, 3)
                    if i == 4 and (t - 5 >= 0 and (t - 5) % NG == 0):
                        residual((t - 5) // NG)
                    if i == 6 and 0 <= t - 1 < NQ:
                        outputs(t - 1)
                if t + 2 < NQ:
                    maximum_parts(t + 2)
                if (t + 1) % NG == 0 and t + 1 >= 0 and (t + 1) // NG + 1 < B:
                    normalise((t + 1) // NG + 1)

        @block.scalar
        def _(act):
            ln_scalar(act)

            def evacuate(job, index, ins):
                act.wait_ge(misc_full, misc_turn(job, index) + 1)
                ins().then_inc(misc_free, 1)

            def tokens_turned(b):
                if b:
                    act.wait_ge(misc_full, misc_turn("V", b - 1) + 1)
                evacuate("xnT", b, lambda: nc.scalar.copy(xnT[:], misc[:]))

            def feature(b, x, ins):
                if b:
                    act.wait_ge(lo_ready, 4 * b)
                ins().then_inc(feat_ready, 1)

            def queries(b):
                act.wait_ge(misc_full, misc_turn("Q", b) + 1)
                if b == 0:
                    act.wait_ge(consts_ready, 3)
                feature(b, 0, lambda: nc.scalar.activation(feat[:, 0, :], misc[:], ACT.Identity, bias=bqs[:]))
                act.wait_ge(feat_ready, 4 * b + 1)
                if b:
                    act.wait_ge(misc_full, misc_turn("J", b - 1) + 1)
                nc.scalar.activation(tanh_q[:], feat[:, 0, :], ACT.Tanh, scale=1.0 / QK_SCALE).then_inc(tq_ready, 1)

            def keys(b):
                act.wait_ge(misc_full, misc_turn("K", b) + 1)
                feature(b, 1, lambda: nc.scalar.activation(feat[:, 1, :], misc[:], ACT.Identity, bias=bk[:]))
                act.wait_ge(feat_ready, 4 * b + 2)
                nc.scalar.activation(feat[:, 2, :], feat[:, 1, :], ACT.Tanh).then_inc(feat_ready, 1)

            def entangled(b):
                act.wait_ge(misc_full, misc_turn("J", b) + 1)
                feature(b, 3, lambda: nc.scalar.activation(feat[:, 3, :], misc[:], ACT.Copy, scale=lam[:]))

            def maxima_turned(q):
                evacuate("max", q, lambda: nc.scalar.copy(neg_max[:, q % 2, :], misc[0:3 * GROUP, :]))

            def maxima_stacked(q):
                b, g = divmod(q, NG)
                act.wait_ge(*misc_read(misc_turn("max", q)))
                if b >= 2:
                    act.wait_ge(st_psum, ST_UNITS * NG * (b - 1))
                act.dma_start(QA[ROWS:ROWS + 3, b % 2, GROUP * g:GROUP * (g + 1), :],
                              neg_max[:, q % 2, :]).then_inc(max_rows[q % 2], 16)

            def exponential(q, u):
                n = ST_UNITS * q + u
                p, i = divmod(u, 5)
                act.wait_ge(st_psum, n + 1)
                if q >= 2:
                    act.wait_ge(pv_psum, q - 1)
                src = st[:, n % 2, :]
                if i < 2:
                    dst = probs[:, q % 2, 2 * p + i, 0:S]
                elif i < 4:
                    dst = probs[:, q % 2, 2 * p + i - 2, S:2 * S]
                else:
                    dst = probs[:, q % 2, 2 * p:2 * p + 2, 2 * S:SCORE_COLS]
                    src = src.rearrange("p (a n) -> p a n", a=2)
                nc.scalar.activation(dst, src, ACT.Exp).then_inc(exp_done, 1)

            def group_out(q):
                act.wait_ge(pv_psum, q + 1)
                if q >= 2:
                    act.wait_ge(misc_full, misc_turn("tokens", q - 2) + 1)
                nc.scalar.copy(OT[:, q % 2, :], pv[:]).then_inc(ot_ready, 1)

            def outputs_turned(b):
                if b:
                    act.wait_ge(misc_full, misc_turn("out", b - 1) + 1)
                evacuate("OnT", b, lambda: nc.scalar.copy(OnT[:], misc[:]))

            tokens_turned(0)
            queries(0)
            keys(0)
            entangled(0)
            for t in range(FIRST, LAST + 1):
                jobs = pe_jobs(t)
                for u in range(ST_UNITS):
                    if 0 <= t < NQ:
                        exponential(t, u)
                    for job, index in jobs.get(u, ()):
                        {"xnT": tokens_turned, "Q": queries, "K": keys, "J": entangled, "max": maxima_turned,
                         "OnT": outputs_turned}.get(job, lambda index: None)(index)
                    if u == 2 and 0 <= t + 1 < NQ:
                        maxima_stacked(t + 1)
                    if u == 5 and 0 <= t - 1 < NQ:
                        group_out(t - 1)

        @block.tensor
        def _(pe):
            pe.wait_ge(loaded, 16 * LOADS)
            pe.wait_ge(consts_ready, 3)
            mm = nc.tensor.matmul
            tiles = [slice(t * P, (t + 1) * P) for t in range(TT)]

            def side(job, index):
                if job == "pv":
                    return probs_values(index)
                turn = misc_turn(job, index)
                if turn:
                    pe.wait_ge(*misc_read(turn - 1))
                {"xnT": turn_tokens, "Q": queries, "K": keys, "V": values, "J": entangle, "max": turn_maxima,
                 "tokens": turn_outputs, "OnT": turn_heads, "out": project}[job](index).then_inc(misc_full, 1)

            def turn_tokens(b):
                pe.wait_ge(xn_ready, b + 1)
                for t in range(TT):
                    last = nc.tensor.transpose(misc[:, tiles[t]], xn[:, t, :], ident[:])
                return last

            def queries(b):
                pe.wait_ge(*misc_read(misc_turn("xnT", b)))
                return mm(misc[:], wqs[:], xnT[:], start=True, stop=True)

            def keys(b):
                return mm(misc[:], w["wk"][:], xnT[:], start=True, stop=True)

            def values(b):
                for t in range(TT):
                    last = mm(misc[:, tiles[t]], xnT[:, tiles[t]], w["wv"][:], start=True, stop=True)
                return last

            def entangle(b):
                pe.wait_ge(tq_ready, b + 1)
                return mm(misc[:], w["J"][:], tanh_q[:], start=True, stop=True)

            def turn_maxima(q):
                pe.wait_ge(maxparts_ready, q + 1)
                for t in range(TT):
                    last = mm(misc[0:3 * GROUP, tiles[t]], max_parts[:, q % 2, t, :, :].rearrange("p k h -> p (k h)"),
                              ident_b[:], start=True, stop=True)
                return last

            def probs_values(q):
                b, g = divmod(q, NG)
                pe.wait_ge(exp_done, ST_UNITS * (q + 1))
                if q:
                    pe.wait_ge(ot_ready, q)
                for j, c in ((0, 0), (1, S), (3, S + 3 * P), (2, 2 * S)):
                    for k in range(GROUP):
                        last = mm(pv[k * HP:(k + 1) * HP, j * P:S], V[:, b % 2, j, GROUP * g + k, :],
                                  probs[:, q % 2, k, c:c + S - j * P], start=(j == 0), stop=(j == 2))
                last.then_inc(pv_psum, 1)

            def turn_outputs(q):
                pe.wait_ge(ot_ready, q + 1)
                for t in range(TT):
                    last = nc.tensor.transpose(misc[:, tiles[t]], OT[:, q % 2, tiles[t]], ident[:])
                return last

            def turn_heads(b):
                pe.wait_ge(*misc_read(misc_turn("tokens", NG * b + NG - 1)))
                for t in range(TT):
                    last = nc.tensor.transpose(misc[:, tiles[t]], O[:, b % 2, t, :, :].rearrange("p h r -> p (h r)"),
                                               ident[:])
                return last

            def project(b):
                pe.wait_ge(*misc_read(misc_turn("OnT", b)))
                for t in range(TT):
                    mm(misc[:, tiles[t]], OnT[:, tiles[t]], w["wo"][:], start=True, stop=False)
                    last = mm(misc[:, tiles[t]], one[:], bo[:], start=False, stop=True)
                return last

            def scores_t(out, q, a, j):
                b, g = divmod(q, NG)
                h = GROUP * g + a
                mm(out, KA[0:ROWS + 3, b % 2, h, j * P:(j + 1) * P], QA[0:ROWS + 3, b % 2, h, j * P:S],
                   start=True, stop=False)
                return mm(out[:, 0:P], ident_b[:], mask_k[:], start=False, stop=True)

            def scores_unit(q, u):
                n = ST_UNITS * q + u
                p, i = divmod(u, 5)
                if n >= 2:
                    pe.wait_ge(exp_done, n - 1)
                out = st[:, n % 2, :]
                if i < 2:
                    last = scores_t(out, q, 2 * p + i, 0)
                elif i < 4:
                    scores_t(out[:, 0:3 * P], q, 2 * p + i - 2, 1)
                    last = scores_t(out[:, 3 * P:S], q, 2 * p + i - 2, 3)
                else:
                    scores_t(out[:, 0:2 * P], q, 2 * p, 2)
                    last = scores_t(out[:, 2 * P:S], q, 2 * p + 1, 2)
                last.then_inc(st_psum, 1)

            def maximum_unit(q, i):
                b, g = divmod(q, NG)
                p, r = divmod(i, TT)
                m = MX_UNITS * q + i
                if m >= 2:
                    pe.wait_ge(mx_read, m - 1)
                for a in range(2):
                    h = GROUP * g + 2 * p + a
                    mm(mx[:, m % 2, a, 0:P * (r + 1)], QA[0:ROWS, b % 2, h, tiles[r]],
                       KA[0:ROWS, b % 2, h, 0:P * (r + 1)], start=True, stop=False)
                    last = mm(mx[:, m % 2, a, tiles[r]], ident_b[:], mask_q[:], start=False, stop=True)
                last.then_inc(mx_psum, 1)

            for job in MISC[:5]:
                side(*job)
            for t in range(FIRST, LAST + 1):
                jobs = pe_jobs(t)
                if t + 2 < NQ and (t + 2) % NG == 0:
                    pe.wait_ge(stacked, 16 * SPREADS * ((t + 2) // NG + 1))
                if t == 0:
                    pe.wait_ge(padded, 3)
                if 0 <= t < NQ:
                    pe.wait_ge(max_rows[t % 2], 16 * (t // 2 + 1))
                for u in range(ST_UNITS):
                    for job in jobs.get(u, ()):
                        side(*job)
                    if 0 <= t < NQ:
                        scores_unit(t, u)
                    if t + 2 < NQ and u < MX_UNITS:
                        maximum_unit(t + 2, u)


E, I = 8, 352
IP = -(-I // P) * P
RING = 4


def routed_ffn(nc, x_sb, A, tag, top_k, out=None):
    KT = top_k * NT
    NS = (KT * P + E * (P - 1)) // P
    assert NS % RING == 3
    with ExitStack() as ctx:
        sb = lambda name, shape, dt=F32: ctx.enter_context(nc.sbuf_tensor(f"{tag}_{name}", shape, dt))
        sem = lambda name: ctx.enter_context(nc.semaphore(f"{tag}_{name}"))
        ps = lambda name, shape: ctx.enter_context(nc.psum_tensor(f"{tag}_{name}", shape, F32))

        w_all = sb("w_all", [P, E, 3 * IP])
        w_now = sb("w_now", [P, RING, 3 * IP])
        wr = sb("wr", [P, E])
        ident = sb("ident", [P, P])
        before = sb("before", [P, P], BF16)
        ones = sb("ones", [P, P], BF16)
        rank = sb("rank", [P, E])
        steps = sb("steps", [P, NT + 1 if NT + 1 > NS else NS])
        numbers = sb("numbers", [P, KT + NS])
        empty = sb("empty", [P, NS, D + 1])
        xn = sb("xn", [P, top_k, NT, D + 1])
        xnT = sb("xnT", [P, 2, S])
        logits = sb("logits", [P, NT, E])
        score = sb("score", [P, NT, E])
        best = sb("best", [P, NT, 1])
        top = sb("top", [P, top_k, NT, 1])
        onehot = sb("onehot", [P, top_k, NT, E])
        onehot_b = sb("onehot_b", [P, top_k, NT, E], BF16)
        weight = sb("weight", [P, top_k, NT])
        gap, gap_sum = sb("gap", [P, NT]), sb("gap_sum", [P, NT])
        over = sb("over", [P, E, KT + 1])
        tiles = sb("tiles", [P, E])
        ends = sb("ends", [P, E])
        starts = sb("starts", [P, E])
        place = sb("place", [P, KT, E])
        pos_f = sb("pos_f", [P, KT])
        pos = sb("pos", [P, KT], U32)
        passed = sb("passed", [P, NS, E])
        expert_f = sb("expert_f", [P, NS])
        expert = sb("expert", [P, NS], I32)
        xs, xsT = sb("xs", [P, RING, D + 1]), sb("xsT", [P, 2, P])
        pair = sb("pair", [P, RING], U32)
        sg, hid = sb("sg", [P, 2, IP]), sb("hid", [P, 2, IP])
        y = sb("y", [P, RING, D])
        back = sb("back", [P, KT, D])
        sorted_x = nc.dram_tensor(f"{tag}_sorted_x", (NS * P, D + 1), F32, kind="Internal").ap()
        pair_y = nc.dram_tensor(f"{tag}_pair_y", ((KT + NS) * P, D), F32, kind="Internal").ap()
        p_turn, p_rank = ps("p_turn", [P, 2, S]), ps("p_rank", [P, KT + 1, E])
        p_g, p_u = ps("p_g", [P, 2, 512]), ps("p_u", [P, 2, 512])
        p_y = ps("p_y", [P, D])

        loaded, cleared, moved = sem("loaded"), sem("cleared"), sem("moved")
        w_loaded, w_ready = sem("w_loaded"), sem("w_ready")
        empty_ready, ones_ready = sem("empty_ready"), sem("ones_ready")
        xn_ready, xnT_psum, xnT_ready = sem("xn_ready"), sem("xnT_psum"), sem("xnT_ready")
        logit_psum, logit_psum_part = sem("logit_psum"), sem("logit_psum_part")
        onehot_ready, rank_psum, pos_ready = sem("onehot_ready"), sem("rank_psum"), sem("pos_ready")
        if top_k == 2:
            gap_ready, exp_ready, weight_ready = sem("gap_ready"), sem("exp_ready"), sem("weight_ready")
        expert_ready = sem("expert_ready")
        xs_in = [sem(f"xs_in{r}") for r in range(RING)]
        xs_psum, xsT_ready = sem("xs_psum"), sem("xsT_ready")
        g_psum, sg_ready, u_psum, hid_ready = sem("g_psum"), sem("sg_ready"), sem("u_psum"), sem("hid_ready")
        y_psum, y_ready = sem("y_psum"), sem("y_ready")
        y_out = [sem(f"y_out{r}") for r in range(RING)]
        back_in = [sem(f"back_in{b}") for b in range(B)]
        pair_ready, route, x_done = sem("pair_ready"), sem("route"), sem("x_done")
        mv, rstd, ln_vector, ln_scalar = layer_norm_stats(nc, ctx, tag, x_sb)
        LOADS = 6
        TAKES = [(k, b * TT + t) for b in range(B) for k in range(top_k) for t in range(TT)]
        NGRP = NT // TT

        def run_steps(eng, step):
            for r in range(RING):
                step(r, r, 0)
            with eng.Fori(0, NS // RING - 1) as m:
                for r in range(RING):
                    step(RING * m + RING + r, r, m + 1)
            for r in range(NS % RING):
                step(NS - NS % RING + r, r, NS // RING)

        block = ctx.enter_context(nc.Block())

        @block.sync
        def _(sp):
            sp.dma_start(wr[:], A[f"{tag}_wr"]).then_inc(loaded, 16)
            sp.dma_start(numbers[:], A["numbers"][:, 0:KT + NS]).then_inc(loaded, 16)
            sp.dma_start(ident[:], A["ident"]).then_inc(loaded, 16)
            sp.dma_start(before[:], A["before"]).then_inc(loaded, 16)
            sp.dma_start(rank[:], A["rank"].broadcast_to([P, E])).then_inc(loaded, 16)
            sp.dma_start(steps[:], A["steps"][:, 0:steps.shape[1]].broadcast_to([P, steps.shape[1]])
                         ).then_inc(loaded, 16)
            sp.wait_ge(empty_ready, 2)
            sp.dma_start(sorted_x.rearrange("(s p) d -> p s d", p=P), empty[:]).then_inc(cleared, 16)

            for e in range(E):
                sp.dma_start(w_all[:, e, :], A[f"{tag}_w"][:, e, :]).then_inc(w_loaded, 16)

            def tile_in(s, r, q):
                if within(s, RING):
                    sp.wait_ge(xs_psum, s - RING + 1)
                    sp.wait_ge(pair_ready, s - RING + 1)
                sp.dma_start(xs[:, r, :], sorted_x[bass.ds(s * P, P), :]).then_inc(xs_in[r], 16)

            sp.wait_ge(moved, 16 * KT)
            run_steps(sp, tile_in)
            for r in range(RING):
                sp.wait_ge(y_out[r], 16 * ((NS - 1 - r) // RING + 1))
            for b in range(B):
                for k in range(top_k):
                    v = k * NT + b * TT
                    sp.dma_start(back[:, v:v + TT, :], pair_y[v * P:(v + TT) * P, :]
                                 .rearrange("(n p) d -> p n d", p=P)).then_inc(back_in[b], 16)
            if out is not None:
                stored = sem("stored")
                for b in range(B):
                    sp.wait_ge(x_done, KT * (b + 1) // B)
                    sp.dma_start(out[b].rearrange("(n p) d -> p n d", p=P),
                                 x_sb[:, b * TT:(b + 1) * TT, :]).then_inc(stored, 16)
                sp.wait_ge(stored, 16 * B)

        @block.vector
        def _(dve):
            link = Chain(dve, route)
            nc.vector.memset(ones[:], 1.0).then_inc(ones_ready, 1)
            ln_vector(dve)
            for t in range(NT):
                ins = nc.vector.tensor_scalar(xn[:, 0, t, 0:D], x_sb[:, t, :], mv[:, t, 0:1], rstd[:, t:t + 1],
                                              ALU.subtract, ALU.mult)
                if t % TT == TT - 1:
                    ins.then_inc(xn_ready, 1)
            dve.wait_ge(loaded, 16 * LOADS)
            nc.vector.tensor_copy(xn[:, :, :, D], numbers[:, 0:KT].rearrange("p (k t) -> p k t", k=top_k)
                                  ).then_inc(xn_ready, 1)
            if top_k == 2:
                dve.wait_ge(xn_ready, NGRP + 1)
                nc.vector.tensor_copy(xn[:, 1, :, 0:D], xn[:, 0, :, 0:D]).then_inc(xn_ready, 1)
            dve.wait_ge(logit_psum, 1)
            link(nc.vector.tensor_copy(logits[:], p_rank[:, 0:NT, :]))
            across = lambda a: a.broadcast_to([P, NT, E])
            for k in range(top_k):
                link(nc.vector.reduce_max(top[:, k, :, 0], logits[:], AX_X))
                link(nc.vector.tensor_tensor(score[:], logits[:], across(top[:, k, :, :]), ALU.is_equal))
                link(nc.vector.tensor_tensor(score[:], score[:], across(rank[:].rearrange("p (o e) -> p o e", o=1)),
                                             ALU.mult))
                link(nc.vector.reduce_max(best[:, :, 0], score[:], AX_X))
                link(nc.vector.tensor_tensor(onehot[:, k, :, :], score[:], across(best[:]), ALU.is_equal))
                if k + 1 < top_k:
                    link(nc.vector.scalar_tensor_tensor(out=logits[:], in0=onehot[:, k, :, :], scalar=-1e30,
                                                        in1=logits[:], op0=ALU.mult, op1=ALU.add))
            nc.vector.tensor_copy(onehot_b[:], onehot[:]).then_inc(onehot_ready, 1)
            if top_k == 2:
                nc.vector.tensor_tensor(gap[:], top[:, 1, :, 0], top[:, 0, :, 0], ALU.subtract).then_inc(gap_ready, 1)
                dve.wait_ge(exp_ready, 1)
                link(nc.vector.tensor_scalar(gap_sum[:], gap[:], 1.0, None, ALU.add))
                link(nc.vector.reciprocal(weight[:, 0, :], gap_sum[:]))
                nc.vector.tensor_tensor(weight[:, 1, :], gap[:], weight[:, 0, :], ALU.mult).then_inc(weight_ready, 1)
            dve.wait_ge(rank_psum, 1)
            cnt = p_rank[:, KT, :].rearrange("p (e o) -> p e o", o=1).broadcast_to([P, E, KT + 1])
            limit = steps[:, 0:KT + 1].rearrange("p (o n) -> p o n", o=1).broadcast_to([P, E, KT + 1])
            link(nc.vector.tensor_scalar(over[:], limit, float(P), None, ALU.mult))
            link(nc.vector.tensor_tensor(over[:], cnt, over[:], ALU.is_gt))
            link(nc.vector.reduce_sum(tiles[:], over[:], AX_X))
            link(nc.vector.tensor_tensor_scan(ends[:], tiles[:], tiles[:], 0.0, ALU.add, ALU.bypass))
            link(nc.vector.tensor_tensor(starts[:], ends[:], tiles[:], ALU.subtract))
            link(nc.vector.tensor_scalar(starts[:], starts[:], float(P), None, ALU.mult))
            over_tiles = lambda a: a.rearrange("p (o e) -> p o e", o=1).broadcast_to([P, KT, E])
            link(nc.vector.tensor_tensor(place[:], p_rank[:, 0:KT, :], over_tiles(starts[:]), ALU.add))
            link(nc.vector.tensor_tensor(place[:], place[:], onehot[:].rearrange("p k t e -> p (k t) e"), ALU.mult))
            link(nc.vector.reduce_sum(pos_f[:], place[:], AX_X))
            nc.vector.tensor_copy(pos[:], pos_f[:]).then_inc(pos_ready, 1)
            link(nc.vector.tensor_tensor(passed[:], ends[:].rearrange("p (o e) -> p o e", o=1)
                                         .broadcast_to([P, NS, E]),
                                         steps[:, 0:NS].rearrange("p (s o) -> p s o", o=1)
                                         .broadcast_to([P, NS, E]), ALU.is_le))
            link(nc.vector.reduce_sum(expert_f[:], passed[:], AX_X))
            link(nc.vector.tensor_scalar(expert_f[:], expert_f[:], float(E - 1), None, ALU.min))
            nc.vector.tensor_copy(expert[:], expert_f[:]).then_inc(expert_ready, 1)

            dve.wait_ge(expert_ready, 1)
            dve.wait_ge(w_loaded, 16 * E)

            def weights(s, r):
                e = dve.value_load(expert[0:1, bass.ds(s, 1)], min_val=0, max_val=E - 1)
                if within(s, RING):
                    dve.wait_ge(y_psum, s - RING + 1)
                nc.vector.tensor_copy(w_now[:, r, :], w_all[:, bass.ds(e, 1), :]).then_inc(w_ready, 1)

            def hidden(s, k):
                dve.wait_ge(sg_ready, s + 1)
                dve.wait_ge(u_psum, s + 1)
                if within(s, 2):
                    dve.wait_ge(y_psum, s - 1)
                nc.vector.tensor_tensor(hid[:, k, :], sg[:, k, :], p_u[:, k, 0:IP], ALU.mult).then_inc(hid_ready, 1)

            def pairs(s, r, q):
                dve.wait_ge(xs_in[r], 16 * (q + 1))
                if within(s, RING):
                    dve.wait_ge(y_out[r], 16 * q)
                nc.vector.tensor_copy(pair[:, r:r + 1], xs[:, r, D:D + 1]).then_inc(pair_ready, 1)

            def step(s, r, q):
                if within(s, 0, NS - 2):
                    weights(s + 2, (r + 2) % RING)
                if within(s, 0, NS - 1):
                    hidden(s + 1, (r + 1) % 2)
                    pairs(s + 1, (r + 1) % RING, q + (r + 1) // RING)

            weights(0, 0)
            weights(1, 1)
            hidden(0, 0)
            pairs(0, 0, 0)
            run_steps(dve, step)
            if top_k == 2:
                dve.wait_ge(weight_ready, 1)
            for n, (k, t) in enumerate(TAKES):
                dve.wait_ge(back_in[t // TT], 16 * top_k)
                if k:
                    dve.wait_ge(x_done, n - TT + 1)
                if top_k == 2:
                    ins = nc.vector.scalar_tensor_tensor(out=x_sb[:, t, :], in0=back[:, k * NT + t, :],
                                                         scalar=weight[:, k, t:t + 1], in1=x_sb[:, t, :],
                                                         op0=ALU.mult, op1=ALU.add)
                else:
                    ins = nc.vector.tensor_tensor(x_sb[:, t, :], back[:, t, :], x_sb[:, t, :], ALU.add)
                ins.then_inc(x_done, 1)

        @block.scalar
        def _(act):
            ln_scalar(act)
            for g in range(NGRP):
                act.wait_ge(xnT_psum, g + 1)
                if g >= 2:
                    act.wait_ge(logit_psum_part, g - 1)
                nc.scalar.copy(xnT[:, g % 2, :], p_turn[:, g % 2, :]).then_inc(xnT_ready, 1)
            if top_k == 2:
                act.wait_ge(gap_ready, 1)
                nc.scalar.activation(gap[:], gap[:], ACT.Exp).then_inc(exp_ready, 1)

            def into(s, k):
                act.wait_ge(xs_psum, s + 1)
                if within(s, 2):
                    act.wait_ge(u_psum, s - 1)
                nc.scalar.copy(xsT[:, k, :], p_turn[:, k, 0:P]).then_inc(xsT_ready, 1)

            def gate(s, k):
                act.wait_ge(g_psum, s + 1)
                if within(s, 2):
                    act.wait_ge(hid_ready, s - 1)
                nc.scalar.activation(sg[:, k, :], p_g[:, k, 0:IP], ACT.Silu).then_inc(sg_ready, 1)

            def result(s, r, q):
                act.wait_ge(y_psum, s + 1)
                if within(s, RING):
                    act.wait_ge(y_out[r], 16 * q)
                nc.scalar.copy(y[:, r, :], p_y[:]).then_inc(y_ready, 1)

            def step(s, r, q):
                if within(s, 0, NS - 1):
                    gate(s + 1, (r + 1) % 2)
                if within(s, 0, NS - 2):
                    into(s + 2, r % 2)
                result(s, r, q)

            into(0, 0)
            into(1, 1)
            gate(0, 0)
            run_steps(act, step)

        @block.gpsimd
        def _(pool):
            nc.gpsimd.memset(empty[:, :, 0:D], 0.0).then_inc(empty_ready, 1)
            pool.wait_ge(loaded, 16 * LOADS)
            nc.gpsimd.tensor_copy(empty[:, :, D], numbers[:, KT:KT + NS]).then_inc(empty_ready, 1)
            pool.wait_ge(cleared, 16)
            pool.wait_ge(pos_ready, 1)
            pool.wait_ge(xn_ready, NGRP + top_k)
            for v in range(KT):
                nc.gpsimd.indirect_dma_start(sorted_x, bass.IndirectOffsetOnAxis(ap=pos[:, v:v + 1], axis=0),
                                             xn[:, v // NT, v % NT, :], None).then_inc(moved, 16)

            for s in range(NS):
                r = s % RING
                pool.wait_ge(y_ready, s + 1)
                pool.wait_ge(pair_ready, s + 1)
                nc.gpsimd.indirect_dma_start(pair_y, bass.IndirectOffsetOnAxis(ap=pair[:, r:r + 1], axis=0),
                                             y[:, r, :], None).then_inc(y_out[r], 16)

        @block.tensor
        def _(pe):
            mm = nc.tensor.matmul
            pe.wait_ge(loaded, 16 * LOADS)
            pe.wait_ge(ones_ready, 1)
            for g in range(NGRP):
                pe.wait_ge(xn_ready, g + 1)
                if g >= 2:
                    pe.wait_ge(xnT_ready, g - 1)
                for t in range(TT):
                    last = nc.tensor.transpose(p_turn[:, g % 2, t * P:(t + 1) * P], xn[:, 0, g * TT + t, 0:D], ident[:])
                last.then_inc(xnT_psum, 1)
                pe.wait_ge(xnT_ready, g + 1)
                for t in range(TT):
                    last = mm(p_rank[:, g * TT + t, :], xnT[:, g % 2, t * P:(t + 1) * P], wr[:],
                              start=(g == 0 and t == 0), stop=(g == NGRP - 1 and t == TT - 1), skip_group_check=True)
                if g < NGRP - 1:
                    last.then_inc(logit_psum_part, 1)
            last.then_inc(logit_psum, 1)
            pe.wait_ge(onehot_ready, 1)
            flat = onehot_b[:].rearrange("p k t e -> p (k t) e")
            mm(p_rank[:, 0:KT, :], before[:], flat, start=True, stop=False, skip_group_check=True)
            for v in range(KT):
                last = mm(p_rank[:, v + 1:KT + 1, :], ones[:],
                          flat[:, v:v + 1, :].broadcast_to([P, KT - v, E]), start=False, stop=(v == KT - 1),
                          skip_group_check=True)
            last.then_inc(rank_psum, 1)

            def turn_in(s, r, q):
                pe.wait_ge(xs_in[r], 16 * (q + 1))
                if within(s, 2):
                    pe.wait_ge(xsT_ready, s - 1)
                nc.tensor.transpose(p_turn[:, r % 2, 0:P], xs[:, r, 0:D], ident[:]).then_inc(xs_psum, 1)

            def gate_up(s, r):
                k = r % 2
                pe.wait_ge(w_ready, s + 1)
                pe.wait_ge(xsT_ready, s + 1)
                if within(s, 2):
                    pe.wait_ge(hid_ready, s - 1)
                for to, done, w0 in ((p_g, g_psum, 0), (p_u, u_psum, IP)):
                    for c in range(0, IP, P):
                        last = mm(to[:, k, c:c + P], w_now[:, r, w0 + c:w0 + c + P], xsT[:, k, :],
                                  start=True, stop=True)
                    last.then_inc(done, 1)

            def down(s, r):
                pe.wait_ge(hid_ready, s + 1)
                if within(s, 1):
                    pe.wait_ge(y_ready, s)
                for c in range(0, IP, P):
                    last = mm(p_y[:], hid[:, r % 2, c:c + P], w_now[:, r, 2 * IP + c:2 * IP + c + P],
                              start=(c == 0), stop=(c == IP - P))
                last.then_inc(y_psum, 1)

            def step(s, r, q):
                if within(s, 0, NS - 1):
                    gate_up(s + 1, (r + 1) % RING)
                if within(s, 0, NS - 2):
                    turn_in(s + 2, (r + 2) % RING, q + (r + 2) // RING)
                down(s, r)

            turn_in(0, 0, 0)
            turn_in(1, 1, 0)
            gate_up(0, 0)
            run_steps(pe, step)


DI, DS, DC = 256, 16, 4
HALVES = DI // P
AHEAD = 4
QUAD = 32


def state_space(nc, x_sb, A):
    with ExitStack() as ctx:
        sb = lambda name, shape, dt=F32: ctx.enter_context(nc.sbuf_tensor(f"m_{name}", shape, dt))
        sem = lambda name: ctx.enter_context(nc.semaphore(f"m_{name}"))
        ps = lambda name, shape: ctx.enter_context(nc.psum_tensor(f"m_{name}", shape, F32))

        w_in = sb("w_in", [P, 2 * DI])
        w_delta = sb("w_delta", [P, DI])
        w_bc = sb("w_bc", [P, 3 * QUAD])
        w_out, w_skip = sb("w_out", [P, HALVES, D]), sb("w_skip", [P, HALVES, D])
        conv_w = sb("conv_w", [P, HALVES, DC])
        conv_b, b_delta, skip = (sb(n, [P, HALVES]) for n in ("conv_b", "b_delta", "skip"))
        a_log, a_neg = sb("a_log", [P, HALVES, DS]), sb("a_neg", [P, HALVES, DS])
        state_rows = sb("state_rows", [P, 2 * DS, P], BF16)
        ident = sb("ident", [P, P])
        xn, xnT = sb("xn", [P, TT, D]), sb("xnT", [P, S])
        gate = sb("gate", [P, HALVES, S])
        xi = sb("xi", [P, HALVES, DC - 1 + S])
        xc = sb("xc", [P, 2, HALVES, S])
        size, soft = sb("size", [P, HALVES, S]), sb("soft", [P, HALVES, S])
        rate, dx = sb("rate", [P, 2, HALVES, S]), sb("dx", [P, 2, HALVES, S])
        bc_rest, bc_mid = sb("bc_rest", [P, S]), sb("bc_mid", [P, S], BF16)
        bc = sb("bc", [P, 2, S], BF16)
        b_all = sb("b_all", [P, AHEAD, S])
        decay, inflow = (sb(n, [P, AHEAD, HALVES, S]) for n in ("decay", "inflow"))
        state, seen = sb("state", [P, 3, HALVES, S]), sb("seen", [P, 2, HALVES, S])
        outT = sb("outT", [P, S])
        misc = ps("misc", [P, 3, S])
        p_b, p_c = ps("b", [P, S]), ps("c", [P, 2, S])
        p_out = ps("out", [P, 2, S])

        loaded = sem("loaded")
        a_exp, consts_ready = sem("a_exp"), sem("consts_ready")
        xn_ready, xnT_ready = sem("xn_ready"), sem("xnT_ready")
        misc_full = sem("misc_full")
        gate_ready, xi_ready = sem("gate_ready"), sem("xi_ready")
        bc_hi, bc_sub, bc_mid_ready, bc_mid_put, bc_ready = (sem(n) for n in ("bc_hi", "bc_sub", "bc_mid_ready",
                                                                             "bc_mid_put", "bc_ready"))
        ramp_ready, size_ready, size_exp, soft_ready = (sem(n) for n in ("ramp_ready", "size_ready", "size_exp",
                                                                         "soft_ready"))
        conv_done = [sem(f"conv_done_{half}") for half in range(HALVES)]
        tail = sb("tail", [P, HALVES, S])
        tail_ready, rate_ready, dx_ready = sem("tail_ready"), sem("rate_ready"), sem("dx_ready")
        b_psum, b_ready, c_psum = sem("b_psum"), sem("b_ready"), sem("c_psum")
        decay_ready, inflow_ready = sem("decay_ready"), sem("inflow_ready")
        state_ready, seen_ready, out_psum = sem("state_ready"), sem("seen_ready"), sem("out_psum")
        outT_ready, x_done = sem("outT_ready"), sem("x_done")
        mv, rstd, ln_vector, ln_scalar = layer_norm_stats(nc, ctx, "m", x_sb)
        LOADS = 11
        N_STEPS = B * DS

        PREPARE = [("xnT", 0), ("gate", 0), ("gate", 1), ("x", 0), ("x", 1), ("bc", 0), ("delta", 0), ("delta", 1)]
        PE_SIDE = {0: [0], 2: [1], 3: [2], 5: [3], 6: [4], 7: [5], 8: [6], 9: [7]}
        uses = [(job, half, 0) for job, half in PREPARE]
        for i in range(N_STEPS + 4):
            b, n = divmod(i, DS)
            if n == 3 and b:
                uses.append(("back", 0, b - 1))
            if b + 1 < B:
                uses += [(*PREPARE[k], b + 1) for k in PE_SIDE.get(n, ())]

        def use(job, half, b):
            return uses.index((job, half, b))

        def bank(job, half, b):
            return misc[:, use(job, half, b) % 3, :]

        def read_of(k):
            job, half, b = uses[k]
            return {"xnT": (xnT_ready, b + 1), "gate": (gate_ready, HALVES * b + half + 1),
                    "x": (xi_ready, HALVES * b + half + 1), "bc": (bc_sub, b + 1),
                    "delta": (size_ready, HALVES * b + half + 1), "back": (x_done, b + 1)}[job]

        block = ctx.enter_context(nc.Block())

        @block.sync
        def _(sp):
            for dst, name in ((w_in, "w_in"), (w_delta, "w_delta"), (w_bc, "w_bc"), (w_out, "w_out"),
                              (conv_w, "conv_w"), (conv_b, "conv_b"), (b_delta, "b_delta"), (skip, "skip"),
                              (a_log, "a_log"), (state_rows, "state_rows"), (ident, "ident")):
                sp.dma_start(dst[:], A[name if name == "ident" else f"m_{name}"]).then_inc(loaded, 16)

        @block.vector
        def _(dve):
            nc.vector.memset(xi[:, :, 0:DC - 1], 0.0).then_inc(consts_ready, 1)
            nc.vector.memset(decay[:, :, :, 0:1], 0.0).then_inc(consts_ready, 1)
            ln_vector(dve)
            dve.wait_ge(loaded, 16 * LOADS)
            dve.wait_ge(a_exp, 1)
            nc.vector.tensor_scalar(a_neg[:], a_neg[:], -1.0, None, ALU.mult).then_inc(consts_ready, 1)
            for half in range(HALVES):
                nc.vector.tensor_scalar(w_skip[:, half, :], w_out[:, half, :], skip[:, half:half + 1], None,
                                        ALU.mult).then_inc(consts_ready, 1)
            dve.wait_ge(consts_ready, 5)

            def full(job, half, b):
                dve.wait_ge(misc_full, use(job, half, b) + 1)

            def normalise(b):
                if b:
                    full("xnT", 0, b - 1)
                for t in range(b * TT, (b + 1) * TT):
                    last = nc.vector.tensor_scalar(xn[:, t % TT, :], x_sb[:, t, :], mv[:, t, 0:1],
                                                   rstd[:, t:t + 1], ALU.subtract, ALU.mult)
                last.then_inc(xn_ready, 1)

            def gated(b, half):
                dve.wait_ge(gate_ready, HALVES * b + half + 1)
                full("x", half, b)
                if b:
                    dve.wait_ge(conv_done[half], DC * b)
                nc.vector.tensor_tensor(xi[:, half, DC - 1:], gate[:, half, :], bank("x", half, b),
                                        ALU.mult).then_inc(xi_ready, 1)

            def tap(b, half, k):
                dve.wait_ge(conv_done[half], DC * b + k)
                nc.vector.scalar_tensor_tensor(out=xc[:, b % 2, half, :], in0=xi[:, half, k:k + S],
                                               scalar=conv_w[:, half, k:k + 1], in1=xc[:, b % 2, half, :],
                                               op0=ALU.mult, op1=ALU.add).then_inc(conv_done[half], 1)

            def bc_rest_of(b):
                dve.wait_ge(bc_hi, b + 1)
                if b:
                    dve.wait_ge(bc_ready, b)
                rows = slice(0, 3 * QUAD)
                nc.vector.tensor_tensor(bc_rest[rows, :], bank("bc", 0, b)[rows, :], bc[rows, b % 2, :],
                                        ALU.subtract).then_inc(bc_sub, 1)

            def bc_second(b):
                dve.wait_ge(bc_sub, b + 1)
                nc.vector.tensor_copy(bc_mid[0:3 * QUAD, :], bc_rest[0:3 * QUAD, :]).then_inc(bc_mid_ready, 1)
                dve.wait_ge(bc_mid_ready, b + 1)
                nc.vector.tensor_copy(bc[QUAD:2 * QUAD, b % 2, :], bc_mid[QUAD:2 * QUAD, :]).then_inc(bc_mid_put, 1)

            def bc_third(b):
                dve.wait_ge(bc_mid_put, b + 1)
                nc.vector.tensor_tensor(bc[2 * QUAD:3 * QUAD, b % 2, :], bc_rest[2 * QUAD:3 * QUAD, :],
                                        bc_mid[2 * QUAD:3 * QUAD, :], ALU.subtract).then_inc(bc_ready, 1)

            def rates(b):
                dve.wait_ge(soft_ready, b + 1)
                dve.wait_ge(ramp_ready, HALVES * (b + 1))
                nc.vector.tensor_tensor(rate[:, b % 2, :, :], rate[:, b % 2, :, :], soft[:], ALU.add
                                        ).then_inc(rate_ready, 1)

            def residual(b):
                full("back", 0, b)
                xb = x_sb[:, b * TT:(b + 1) * TT, :]
                nc.vector.tensor_tensor(xb, bank("back", 0, b).rearrange("p (n d) -> p n d", n=TT), xb,
                                        ALU.add).then_inc(x_done, 1)

            normalise(0)
            for half in range(HALVES):
                gated(0, half)
            bc_rest_of(0)
            bc_second(0)
            bc_third(0)
            for half in range(HALVES):
                for k in range(1, DC - 1):
                    tap(0, half, k)
            rates(0)
            normalise(1)
            side = {7: [(gated, 0)], 8: [(gated, 1)], 9: [(tap, 0, 1)], 10: [(tap, 0, 2), (bc_rest_of,)],
                    11: [(bc_second,), (tap, 1, 1)], 12: [(bc_third,), (tap, 1, 2)], 14: [(rates,)]}

            def see(i):
                k = i % 2
                dve.wait_ge(state_ready, i + 1)
                dve.wait_ge(c_psum, i + 1)
                if i >= 2:
                    dve.wait_ge(out_psum, (i - 2) // DS + 1 + i - 1)
                nc.vector.tensor_tensor(seen[:, k, :, :], state[:, i % 3, :, :],
                                        p_c[:, k, :].rearrange("p (o t) -> p o t", o=1)
                                        .broadcast_to([P, HALVES, S]), ALU.mult).then_inc(seen_ready, 1)

            for i in range(N_STEPS):
                b, n = divmod(i, DS)
                dve.wait_ge(inflow_ready, i + 1)
                dve.wait_ge(decay_ready, i + 1)
                if i >= 3:
                    dve.wait_ge(seen_ready, i - 2)
                nc.vector.tensor_tensor_scan(state[:, i % 3, :, :].rearrange("p h t -> p (h t)"),
                                             decay[:, i % AHEAD, :, :].rearrange("p h t -> p (h t)"),
                                             inflow[:, i % AHEAD, :, :].rearrange("p h t -> p (h t)"),
                                             0.0, ALU.mult, ALU.add).then_inc(state_ready, 1)
                if b + 1 < B:
                    for job, *args in side.get(n, ()):
                        job(b + 1, *args)
                if n == DS - 1 and b + 2 < B:
                    normalise(b + 2)
                if n == 5 and b:
                    residual(b - 1)
                if i:
                    see(i - 1)
            see(N_STEPS - 1)
            residual(B - 1)

        @block.gpsimd
        def _(pool):
            def last_tap(b, half):
                pool.wait_ge(conv_done[half], DC * (b + 1) - 1)
                pool.wait_ge(tail_ready, HALVES * b + half + 1)
                nc.gpsimd.tensor_tensor(xc[:, b % 2, half, :], tail[:, half, :], xc[:, b % 2, half, :],
                                        ALU.add).then_inc(conv_done[half], 1)

            def drive(b):
                pool.wait_ge(rate_ready, b + 1)
                for half in range(HALVES):
                    pool.wait_ge(conv_done[half], DC * (b + 1))
                nc.gpsimd.tensor_tensor(dx[:, b % 2, :, :], rate[:, b % 2, :, :], xc[:, b % 2, :, :],
                                        ALU.mult).then_inc(dx_ready, 1)
                pool.wait_ge(dx_ready, b + 1)

            for half in range(HALVES):
                last_tap(0, half)
            drive(0)
            for i in range(N_STEPS):
                b, n = divmod(i, DS)
                k = i % AHEAD
                pool.wait_ge(b_ready, i + 1)
                if i >= AHEAD:
                    pool.wait_ge(state_ready, i - AHEAD + 1)
                nc.gpsimd.tensor_tensor(inflow[:, k, :, :], dx[:, b % 2, :, :], b_all[:, k, :]
                                        .rearrange("p (o t) -> p o t", o=1)
                                        .broadcast_to([P, HALVES, S]), ALU.mult).then_inc(inflow_ready, 1)
                if b + 1 < B:
                    if n in (13, 14):
                        last_tap(b + 1, n - 13)
                    if n == DS - 1:
                        drive(b + 1)

        @block.scalar
        def _(act):
            ln_scalar(act)
            act.wait_ge(loaded, 16 * LOADS)
            nc.scalar.activation(a_neg[:], a_log[:], ACT.Exp).then_inc(a_exp, 1)

            def full(job, half, b):
                act.wait_ge(misc_full, use(job, half, b) + 1)

            def tokens_turned(b):
                full("xnT", 0, b)
                if b:
                    full("delta", 1, b - 1)
                nc.scalar.copy(xnT[:], bank("xnT", 0, b)).then_inc(xnT_ready, 1)

            def gates(b):
                for half in range(HALVES):
                    full("gate", half, b)
                    if b:
                        act.wait_ge(xi_ready, HALVES * (b - 1) + half + 1)
                    nc.scalar.activation(gate[:, half, :], bank("gate", half, b), ACT.Silu).then_inc(gate_ready, 1)

            def bc_first(b):
                full("bc", 0, b)
                if b >= 2:
                    act.wait_ge(c_psum, DS * (b - 1))
                rows = slice(0, 3 * QUAD)
                nc.scalar.copy(bc[rows, b % 2, :], bank("bc", 0, b)[rows, :]).then_inc(bc_hi, 1)

            def sizes(b):
                for half in range(HALVES):
                    full("delta", half, b)
                    if b >= 2:
                        act.wait_ge(dx_ready, b - 1)
                    nc.scalar.activation(rate[:, b % 2, half, :], bank("delta", half, b), ACT.Relu,
                                         bias=b_delta[:, half:half + 1]).then_inc(ramp_ready, 1)
                    if b:
                        act.wait_ge(soft_ready, b)
                    nc.scalar.activation(size[:, half, :], bank("delta", half, b), ACT.Abs,
                                         bias=b_delta[:, half:half + 1]).then_inc(size_ready, 1)

            def softs(b):
                act.wait_ge(size_ready, HALVES * (b + 1))
                nc.scalar.activation(size[:], size[:], ACT.Exp, scale=-1.0).then_inc(size_exp, 1)
                act.wait_ge(size_exp, b + 1)
                if b:
                    act.wait_ge(rate_ready, b)
                nc.scalar.activation(soft[:], size[:], ACT.Ln, bias=1.0).then_inc(soft_ready, 1)

            def outer_taps(b):
                for half in range(HALVES):
                    act.wait_ge(xi_ready, HALVES * b + half + 1)
                    if b >= 2:
                        act.wait_ge(dx_ready, b - 1)
                        act.wait_ge(out_psum, (DS + 1) * (b - 2) + 1)
                    nc.scalar.activation(xc[:, b % 2, half, :], xi[:, half, 0:S], ACT.Identity,
                                         bias=conv_b[:, half:half + 1],
                                         scale=conv_w[:, half, 0:1]).then_inc(conv_done[half], 1)
                    if b:
                        act.wait_ge(conv_done[half], DC * b)
                    nc.scalar.activation(tail[:, half, :], xi[:, half, DC - 1:], ACT.Copy,
                                         scale=conv_w[:, half, DC - 1:DC]).then_inc(tail_ready, 1)

            def result(b):
                act.wait_ge(out_psum, (b + 1) * (DS + 1))
                if b:
                    full("back", 0, b - 1)
                nc.scalar.copy(outT[:], p_out[:, b % 2, :]).then_inc(outT_ready, 1)

            tokens_turned(0)
            gates(0)
            outer_taps(0)
            bc_first(0)
            sizes(0)
            softs(0)
            side = {4: [tokens_turned], 7: [gates], 10: [outer_taps], 11: [bc_first], 12: [sizes], 13: [softs]}
            for i in range(N_STEPS):
                b, n = divmod(i, DS)
                k = i % AHEAD
                if n == 0:
                    act.wait_ge(rate_ready, b + 1)
                act.wait_ge(b_psum, i + 1)
                if i >= AHEAD:
                    act.wait_ge(inflow_ready, i - AHEAD + 1)
                nc.scalar.copy(b_all[:, k, :], p_b[:]).then_inc(b_ready, 1)
                if i >= AHEAD:
                    act.wait_ge(state_ready, i - AHEAD + 1)
                for half in range(HALVES):
                    last = nc.scalar.activation(decay[:, k, half, 1:], rate[:, b % 2, half, 1:], ACT.Exp,
                                                scale=a_neg[:, half, n:n + 1])
                last.then_inc(decay_ready, 1)
                if n == 5 and b:
                    result(b - 1)
                if b + 1 < B:
                    for job in side.get(n, ()):
                        job(b + 1)
            result(B - 1)

        @block.tensor
        def _(pe):
            mm = nc.tensor.matmul
            pe.wait_ge(loaded, 16 * LOADS)

            def project(job, half, b):
                u = use(job, half, b)
                if u >= 3:
                    pe.wait_ge(*read_of(u - 3))
                out = bank(job, half, b)
                if job == "xnT":
                    pe.wait_ge(xn_ready, b + 1)
                    for t in range(TT):
                        last = nc.tensor.transpose(out[:, t * P:(t + 1) * P], xn[:, t, :], ident[:])
                elif job == "back":
                    pe.wait_ge(outT_ready, b + 1)
                    for t in range(TT):
                        last = nc.tensor.transpose(out[:, t * P:(t + 1) * P], outT[:, t * P:(t + 1) * P], ident[:])
                else:
                    weights = {"gate": w_in[:, half * P:(half + 1) * P],
                               "x": w_in[:, DI + half * P:DI + (half + 1) * P],
                               "delta": w_delta[:, half * P:(half + 1) * P], "bc": w_bc[:]}[job]
                    pe.wait_ge(xnT_ready, b + 1)
                    last = mm(out[0:weights.shape[1], :], weights, xnT[:], start=True, stop=True)
                last.then_inc(misc_full, 1)

            rows = slice(0, 3 * QUAD)

            def spread_b(i):
                b, n = divmod(i, DS)
                k = i % 2
                if n == 0:
                    pe.wait_ge(bc_ready, b + 1)
                if i:
                    pe.wait_ge(b_ready, i)
                mm(p_b[:], state_rows[rows, n, :], bc[rows, b % 2, :], start=True, stop=True).then_inc(b_psum, 1)

            def spread_c(i):
                b, n = divmod(i, DS)
                k = i % 2
                if i >= 2:
                    pe.wait_ge(seen_ready, i - 1)
                mm(p_c[:, k, :], state_rows[rows, DS + n, :], bc[rows, b % 2, :],
                   start=True, stop=True).then_inc(c_psum, 1)

            for job, half in PREPARE:
                project(job, half, 0)
            for i in range(AHEAD):
                spread_b(i)
            spread_c(0)
            for i in range(N_STEPS):
                b, n = divmod(i, DS)
                k = i % 2
                if n == 0:
                    for half in range(HALVES):
                        pe.wait_ge(conv_done[half], DC * (b + 1))
                    pe.wait_ge(consts_ready, 4)
                    if b >= 2:
                        pe.wait_ge(outT_ready, b - 1)
                    for half in range(HALVES):
                        last = mm(p_out[:, b % 2, :], w_skip[:, half, :], xc[:, b % 2, half, :], start=(half == 0), stop=False)
                    last.then_inc(out_psum, 1)
                if i + AHEAD < N_STEPS:
                    spread_b(i + AHEAD)
                if i + 1 < N_STEPS:
                    spread_c(i + 1)
                if n == 3 and b:
                    project("back", 0, b - 1)
                if b + 1 < B:
                    for j in PE_SIDE.get(n, ()):
                        project(*PREPARE[j], b + 1)
                pe.wait_ge(seen_ready, i + 1)
                for half in range(HALVES):
                    last = mm(p_out[:, b % 2, :], w_out[:, half, :], seen[:, k, half, :], start=False,
                              stop=(n == DS - 1 and half == HALVES - 1))
                last.then_inc(out_psum, 1)
            project("back", 0, B - 1)


def program(nc, A, out):
    with ExitStack() as ctx:
        x_sb = ctx.enter_context(nc.sbuf_tensor("x_sb", [P, NT, D], F32))
        attention(nc, x_sb, A)
        routed_ffn(nc, x_sb, A, 'f0', 1)
        state_space(nc, x_sb, A)
        routed_ffn(nc, x_sb, A, 'f1', 2, out)


def host_arrays(inputs):
    import numpy as np
    i = {k: np.asarray(v) for k, v in inputs.items()}
    bf16_bits = lambda a: (np.asarray(a, np.float32).view(np.uint32) >> 16).astype(np.uint16)
    turned = lambda a: np.ascontiguousarray(np.swapaxes(a, -1, -2))
    r_major = lambda a: np.ascontiguousarray(a.reshape(a.shape[0], H, HD).swapaxes(1, 2).reshape(a.shape[0], D))
    A = {"x": i["L0_attn_x"]}
    A["wq"], A["wk"] = (r_major(turned(i[f"L0_attn_W{n}"])) for n in "qk")
    A["wv"], A["wo"] = turned(i["L0_attn_Wv"]), turned(i["L0_attn_Wo"])
    A["bq"], A["bk"] = (turned(r_major(i[f"L0_attn_b{n}"][None])) for n in "qk")
    A["bv"], A["bo"] = i["L0_attn_bv"][None], i["L0_attn_bo"][None]
    A["lam"] = i["L0_attn_lambda_attn"].reshape(1, 1)
    J = np.zeros((HD, H, HD, H), i["L0_attn_J_attn"].dtype)
    for h in range(H):
        J[:, h, :, h] = i["L0_attn_J_attn"][h]
    A["J"] = J.reshape(D, D)
    A["ident"] = np.eye(P, dtype=np.float32)
    A["ident_b"] = bf16_bits(np.eye(P))
    after = np.triu(np.ones((P, P), bool), 1)
    A["mask_q"] = bf16_bits(np.where(after, -1e30, 0.0))
    A["mask_k"] = np.ascontiguousarray(A["mask_q"].T)
    for tag, names in (("f0", ("router_w", "gate_w", "up_w", "down_w")),
                       ("f1", ("w_router", "w_gate", "w_up", "w_down"))):
        r, g, u, d = (i[f"L{tag[1]}_ffn_{n}"] for n in names)
        A[f"{tag}_wr"] = turned(r)
        w = np.zeros((P, E, 3, IP), g.dtype)
        w[:, :, 0, :I], w[:, :, 1, :I] = g.transpose(2, 0, 1), u.transpose(2, 0, 1)
        rows = np.zeros((E, IP, D), d.dtype)
        rows[:, :I] = d.transpose(0, 2, 1)
        w[:, :, 2, :] = rows.reshape(E, IP // P, P, D).transpose(2, 0, 1, 3).reshape(P, E, IP)
        A[f"{tag}_w"] = w.reshape(P, E, 3 * IP)
    A["m_w_in"], A["m_w_delta"] = i["L1_attn_W_in"], i["L1_attn_W_delta"]
    A["m_w_bc"] = np.concatenate([i["L1_attn_W_B"], i["L1_attn_W_C"]] * 3, axis=1)
    halves = lambda a: np.ascontiguousarray(a.reshape(HALVES, P, -1).swapaxes(0, 1))
    A["m_w_out"], A["m_conv_w"], A["m_a_log"] = (halves(i[f"L1_attn_{n}"]) for n in ("W_out", "conv_w", "A_log"))
    A["m_conv_b"], A["m_b_delta"], A["m_skip"] = (halves(i[f"L1_attn_{n}"])[:, :, 0]
                                                  for n in ("conv_b", "b_delta", "D"))
    picked = np.zeros((P, 2 * DS, P), np.float32)
    for n in range(2 * DS):
        picked[[n, QUAD + n, 2 * QUAD + n], n, :] = 1.0
    A["m_state_rows"] = bf16_bits(picked)
    A["before"] = bf16_bits(after)
    A["rank"] = np.arange(E, 0, -1, dtype=np.float32)[None]
    A["numbers"] = np.arange(80, dtype=np.float32)[None] * P + np.arange(P, dtype=np.float32)[:, None]
    A["steps"] = np.arange(64, dtype=np.float32)[None]
    return A


def kernel(**inputs):
    import concourse.bacc as bacc
    from concourse.bass_utils import run_bass_kernel_spmd

    nc = bacc.Bacc("TRN2", target_bir_lowering=False, num_devices=1)
    arrays = host_arrays(inputs)
    aps = {n: nc.dram_tensor(f"in_{n}", a.shape, mybir.dt.from_np(a.dtype), kind="ExternalInput").ap()
           for n, a in arrays.items()}
    out = nc.dram_tensor("out", (B, S, D), F32, kind="ExternalOutput").ap()
    for n, a in arrays.items():
        if a.dtype.kind == "u":
            aps[n] = aps[n].bitcast(BF16)
    program(nc, aps, out)
    result = run_bass_kernel_spmd(nc, [{f"in_{n}": a for n, a in arrays.items()}], core_ids=[0])
    return result.results[0]["out"]
```

```python
from contextlib import ExitStack

import concourse.bass as bass
from concourse import mybir

F32 = mybir.dt.float32
BF16 = mybir.dt.bfloat16
I32 = mybir.dt.int32
U32 = mybir.dt.uint32
ACT = mybir.ActivationFunctionType
ALU = mybir.AluOpType
AX_X = mybir.AxisListType.X

P = 128
B, S, D = 4, 512, 128
H, HD = 16, 8
TT = S // P
NT = B * TT
EPS = 1e-5
E, I = 8, 352
IP = -(-I // P) * P
LOW_PART = 8
RING = 4
DI, DS, DC = 256, 16, 4
HALVES = DI // P
AHEAD = 4
QUAD = 32
QK_SCALE = HD ** -0.5
HP = 32
GROUP = P // HP
SCORE_COLS = sum(S - P * j for j in range(TT))
ROWS = 12 * HD
Q_ORDER = (0, 0, 1, 1, 0, 2)
K_ORDER = (0, 1, 0, 1, 2, 0)
TWO_ONES = 1 + 0x3F80 * 2.0 ** -23


def within(s, low, high=None):
    return not isinstance(s, int) or (low <= s and (high is None or s < high))


FIRST_F32 = (("wq", D), ("wk", D), ("wv", D), ("wo", D), ("J", D), ("ident", P), ("bv", D), ("bo", D),
             ("bq", 1), ("bk", 1), ("lam", 1))
FIRST_BF16 = (("ident_b", P), ("mask_q", P), ("mask_k", P))
LATER_F32 = (("numbers", 80), ("rank", E), ("steps", P), ("f0_wr", E), ("f1_wr", E), ("m_w_in", 2 * DI),
             ("m_w_delta", DI), ("m_w_bc", 3 * QUAD), ("m_w_out", DI), ("m_conv_w", DI // P * DC),
             ("m_conv_b", DI // P), ("m_b_delta", DI // P), ("m_skip", DI // P), ("m_a_log", DI // P * DS))
LATER_BF16 = (("before", P), ("m_state_rows", 2 * DS * P))
PACKS = {"first_f32": (FIRST_F32, F32), "first_bf16": (FIRST_BF16, BF16),
         "later_f32": (LATER_F32, F32), "later_bf16": (LATER_BF16, BF16)}


def constant_tiles(nc, ctx):
    packs, columns = {}, {}
    for pack, (names, dt) in PACKS.items():
        packs[pack] = ctx.enter_context(nc.sbuf_tensor(f"pack_{pack}", [P, sum(n for _, n in names)], dt))
        at = 0
        for name, n in names:
            columns[name] = packs[pack][:, at:at + n]
            at += n
    return packs, columns


class Chain:

    def __init__(self, eng, sem):
        self.eng, self.sem, self.n = eng, sem, 0

    def __call__(self, ins):
        self.n += 1
        ins.then_inc(self.sem, 1)
        self.eng.wait_ge(self.sem, self.n)


def layer_norm_stats(nc, ctx, tag, x_sb):
    stats = ctx.enter_context(nc.sbuf_tensor(f"{tag}_stats", [P, NT, 6], F32))
    mv = ctx.enter_context(nc.sbuf_tensor(f"{tag}_mv", [P, NT, 2], F32))
    std = ctx.enter_context(nc.sbuf_tensor(f"{tag}_std", [P, NT], F32))
    rstd = ctx.enter_context(nc.sbuf_tensor(f"{tag}_rstd", [P, NT], F32))
    table = ctx.enter_context(nc.sbuf_tensor(f"{tag}_table", [P, 1], F32))
    eps = ctx.enter_context(nc.sbuf_tensor(f"{tag}_eps", [P, 1], F32))
    stats_done = ctx.enter_context(nc.semaphore(f"{tag}_stats_done"))
    mv_done = ctx.enter_context(nc.semaphore(f"{tag}_mv_done"))
    std_done = ctx.enter_context(nc.semaphore(f"{tag}_std_done"))
    rstd_done = ctx.enter_context(nc.semaphore(f"{tag}_rstd_done"))

    def stats_of(dve, first, end):
        if first == 0:
            nc.vector.memset(eps[:], EPS).then_inc(mv_done, 1)
        for t in range(first, end):
            nc.vector.bn_stats(stats[:, t, :], x_sb[:, t, :]).then_inc(stats_done, 1)
        for t in range(first, end):
            dve.wait_ge(stats_done, t + 1)
            nc.vector.bn_aggr(mv[:, t, :], stats[:, t, :]).then_inc(mv_done, 1)

    def std_of(act, first, end):
        if first == 0:
            act.wait_ge(mv_done, 1)
            nc.scalar.activation(table[:], eps[:], ACT.Sqrt)
        act.wait_ge(mv_done, end + 1)
        nc.scalar.activation(std[:, first:end], mv[:, first:end, 1], ACT.Sqrt, bias=eps[:]
                             ).then_inc(std_done, end - first)

    def rstd_of(dve, first, end):
        dve.wait_ge(std_done, end)
        nc.vector.reciprocal(rstd[:, first:end], std[:, first:end]).then_inc(rstd_done, end - first)
        dve.wait_ge(rstd_done, end)

    return mv, rstd, stats_of, std_of, rstd_of


def attention(nc, x_sb, A, packs, C):
    with ExitStack() as ctx:
        sb = lambda name, shape, dt=F32: ctx.enter_context(nc.sbuf_tensor(f"a_{name}", shape, dt))
        sem = lambda name: ctx.enter_context(nc.semaphore(f"a_{name}"))
        ps = lambda name, shape: ctx.enter_context(nc.psum_tensor(f"a_{name}", shape, F32))

        w = {n: C[n] for n in ("wq", "wk", "wv", "wo", "J")}
        ident, ident_b, bq, bk, lam, bv, bo = (C[n] for n in ("ident", "ident_b", "bq", "bk", "lam", "bv", "bo"))
        mask_q, mask_k = C["mask_q"], C["mask_k"]
        bqs = sb("bqs", [P, 1])
        one = sb("one", [1, P])
        wqs = sb("wqs", [P, D])
        xn, xnT = sb("xn", [P, TT, D]), sb("xnT", [P, S])
        tanh_q = sb("tanh_q", [P, S])
        feat, rest = sb("feat", [P, 4, S]), sb("rest", [P, 4, S])
        parts = sb("parts", [P, 4, 3, S], BF16)
        QA, KA = (sb(n, [P, 2, H, S], BF16) for n in ("QA", "KA"))
        V = sb("V", [P, 2, TT, H, HP])
        row_max = sb("row_max", [P, 2, TT, GROUP])
        max_rest = sb("max_rest", [P, TT, GROUP])
        max_parts = sb("max_parts", [P, 2, TT, 3, GROUP], BF16)
        neg_max = sb("neg_max", [3 * GROUP, 2, S], BF16)
        probs = sb("probs", [P, 2, GROUP, SCORE_COLS])
        OT = sb("OT", [P, 2, S])
        den = sb("den", [P, TT, GROUP])
        O = sb("O", [P, 2, TT, H, HD])
        OnT = sb("OnT", [P, S])
        st = ps("st", [P, 2, S])
        mx = ps("mx", [P, 2, 2, S])
        pv, misc = ps("pv", [P, S]), ps("misc", [P, S])

        x_in, x_rest_in, first_in, later_in = (sem(n) for n in ("x_in", "x_rest_in", "first_in", "later_in"))
        consts_ready = sem("consts_ready")
        xn_ready = sem("xn_ready")
        misc_full, misc_free = sem("misc_full"), sem("misc_free")
        feat_ready, tq_ready = sem("feat_ready"), sem("tq_ready")
        hi_ready, rest_ready, mid_ready, lo_ready = (sem(n) for n in ("hi_ready", "rest_ready",
                                                                      "mid_ready", "lo_ready"))
        stacked, stacked_pool = sem("stacked"), sem("stacked_pool")
        mx_psum, mx_read, maxparts_ready = sem("mx_psum"), sem("mx_read"), sem("maxparts_ready")
        max_rows = [sem("max_rows0"), sem("max_rows1")]
        st_psum, exp_done, pv_psum, ot_ready = sem("st_psum"), sem("exp_done"), sem("pv_psum"), sem("ot_ready")
        dve_chain, padded = sem("dve_chain"), sem("padded")
        mv, rstd, stats_of, std_of, rstd_of = layer_norm_stats(nc, ctx, "a", x_sb)
        NG = H // GROUP
        NQ = B * NG
        ST_UNITS, MX_UNITS = 10, 8
        SPREADS = 4 * len(Q_ORDER)
        POOL_SPREADS = 4 * 2
        FIRST, LAST = -2, NQ + 1

        def pe_jobs(t):
            jobs = {u: [] for u in range(ST_UNITS)}
            b = (t + 1) // NG + 1
            if t % NG == NG - 2 and (t + 2) // NG + 1 < B:
                jobs[8].append(("xnT", (t + 2) // NG + 1))
            if t >= -1 and t % NG == NG - 1 and b < B:
                for u, job in ((1, "Q"), (5, "K"), (9, "J")):
                    jobs[u].append((job, b))
            if t >= 0 and t % NG == 0 and b < B:
                jobs[5].append(("V", b))
            if 0 <= t + 1 < NQ:
                jobs[3].append(("max", t + 1))
            if 0 <= t - 1 < NQ:
                jobs[2].append(("pv", t - 1))
                jobs[7].append(("tokens", t - 1))
            if t - 5 >= 0 and (t - 5) % NG == 0:
                jobs[0].append(("OnT", (t - 5) // NG))
                jobs[5].append(("out", (t - 5) // NG))
            return jobs

        MISC = [(job, 0) for job in ("xnT", "Q", "K", "J", "V")]
        for t in range(FIRST, LAST + 1):
            jobs = pe_jobs(t)
            MISC += [job for u in sorted(jobs) for job in jobs[u] if job[0] != "pv"]

        def misc_turn(job, index):
            return MISC.index((job, index))

        def misc_read(turn):
            job, b = MISC[turn]
            if job in "QKJ":
                return feat_ready, 4 * b + {"Q": 1, "K": 2, "J": 4}[job]
            return misc_free, sum(j not in "QKJ" for j, _ in MISC[:turn + 1])

        STACKS = ((QA, 0, Q_ORDER), (KA, 0, K_ORDER), (KA, 1, K_ORDER), (QA, 1, Q_ORDER))

        def blocks_of(x, part):
            return [blk for blk, k in enumerate(STACKS[x][2]) if k == part]

        def pool_blocks(x):
            return blocks_of(x, 0)[1:]

        def spread(eng, done, b, x, blk):
            stack, feature, order = STACKS[x]
            r0 = 2 * HD * blk + HD * feature
            eng.dma_start(stack[r0:r0 + HD, b % 2, :, :], parts[:, x, order[blk], :]).then_inc(done, 16)

        def rest_of(eng, x):
            return eng.tensor_tensor(rest[:, x, :], feat[:, x, :], parts[:, x, 0, :], ALU.subtract)

        def last_part(eng, x):
            return eng.tensor_tensor(parts[:, x, 2, :], rest[:, x, :], parts[:, x, 1, :], ALU.subtract)

        block = ctx.enter_context(nc.Block())

        @block.sync
        def _(sp):
            def x_of(b, done):
                sp.dma_start(x_sb[:, b * TT:(b + 1) * TT, :],
                             A["x"][b].rearrange("(n p) d -> p n d", p=P)).then_inc(done, 16)

            x_of(0, x_in)
            for pack in ("first_f32", "first_bf16"):
                sp.dma_start(packs[pack][:], A[pack]).then_inc(first_in, 16)
            for b in range(1, B):
                x_of(b, x_rest_in)
            for b in range(B):
                if b >= 2:
                    sp.wait_ge(st_psum, ST_UNITS * NG * (b - 1))
                for x in range(4):
                    for part, made in enumerate((hi_ready, mid_ready, lo_ready)):
                        sp.wait_ge(made, 4 * b + x + 1)
                        for blk in blocks_of(x, part):
                            if not (b == 0 and part == 0 and blk in pool_blocks(x)):
                                spread(sp, stacked, b, x, blk)
                if b == 0:
                    for pack in ("later_f32", "later_bf16"):
                        sp.dma_start(packs[pack][:], A[pack]).then_inc(later_in, 16)
            sp.wait_ge(later_in, 32)

        @block.gpsimd
        def _(pool):
            nc.gpsimd.memset(V[:], 0.0).then_inc(padded, 1)
            pool.wait_ge(padded, 1)
            nc.gpsimd.memset(V[:, :, :, :, HD:HD + 1], 1.0).then_inc(padded, 1)
            pool.wait_ge(padded, 2)
            nc.gpsimd.memset(KA[ROWS:ROWS + 3, :, :, :].bitcast(F32), TWO_ONES).then_inc(padded, 1)
            pool.wait_ge(padded, 3)
            for x in range(4):
                pool.wait_ge(hi_ready, x + 1)
                for blk in pool_blocks(x):
                    spread(nc.gpsimd, stacked_pool, 0, x, blk)
            for b in range(1, B):
                for x in range(4):
                    pool.wait_ge(hi_ready, 4 * b + x + 1)
                    rest_of(nc.gpsimd, x).then_inc(rest_ready, 1)
                    pool.wait_ge(mid_ready, 4 * b + x + 1)
                    last_part(nc.gpsimd, x).then_inc(lo_ready, 1)

        @block.vector
        def _(dve):
            link = Chain(dve, dve_chain)
            dve.wait_ge(x_in, 16)
            stats_of(dve, 0, TT)
            rstd_of(dve, 0, TT)

            def normalise(b):
                if b:
                    dve.wait_ge(misc_full, misc_turn("xnT", b - 1) + 1)
                for t in range(b * TT, (b + 1) * TT):
                    last = nc.vector.tensor_scalar(xn[:, t % TT, :], x_sb[:, t, :], mv[:, t, 0:1],
                                                   rstd[:, t:t + 1], ALU.subtract, ALU.mult)
                last.then_inc(xn_ready, 1)

            normalise(0)
            dve.wait_ge(first_in, 32)
            nc.vector.tensor_scalar(wqs[:], w["wq"][:], QK_SCALE, None, ALU.mult).then_inc(consts_ready, 1)
            nc.vector.tensor_scalar(bqs[:], bq[:], QK_SCALE, None, ALU.mult).then_inc(consts_ready, 1)
            nc.vector.memset(one[:], 1.0).then_inc(consts_ready, 1)
            dve.wait_ge(x_rest_in, 16 * (B - 1))
            stats_of(dve, TT, NT)
            rstd_of(dve, TT, NT)

            def values(b):
                dve.wait_ge(misc_full, misc_turn("V", b) + 1)
                dve.wait_ge(padded, 2)
                if b >= 2:
                    dve.wait_ge(pv_psum, NG * (b - 1))
                nc.vector.tensor_tensor(V[:, b % 2, :, :, 0:HD],
                                        misc[:].rearrange("p (n h r) -> p n h r", h=H, r=HD),
                                        bv[:].rearrange("p (o h r) -> p o h r", o=1, r=HD)
                                        .broadcast_to([P, TT, H, HD]), ALU.add).then_inc(misc_free, 1)

            def first_part(b, x):
                dve.wait_ge(feat_ready, 4 * b + x + 1)
                if b:
                    dve.wait_ge(stacked, 16 * (SPREADS * b - POOL_SPREADS))
                    dve.wait_ge(stacked_pool, 16 * POOL_SPREADS)
                nc.vector.tensor_copy(parts[:, x, 0, :], feat[:, x, :]).then_inc(hi_ready, 1)

            def second_part(b, x):
                dve.wait_ge(rest_ready, 4 * b + x + 1)
                nc.vector.tensor_copy(parts[:, x, 1, :], rest[:, x, :]).then_inc(mid_ready, 1)

            def maximum(q, i):
                p, r = divmod(i, TT)
                m = MX_UNITS * q + i
                dve.wait_ge(mx_psum, m + 1)
                nc.vector.reduce_max(row_max[:, q % 2, r, 2 * p:2 * p + 2], mx[:, m % 2, :, 0:P * (r + 1)],
                                     AX_X).then_inc(mx_read, 1)

            def maximum_parts(q):
                dve.wait_ge(mx_read, MX_UNITS * (q + 1))
                if q >= 2:
                    dve.wait_ge(misc_full, misc_turn("max", q - 2) + 1)
                mp = max_parts[:, q % 2, :, :, :]
                link(nc.vector.tensor_scalar(max_rest[:], row_max[:, q % 2, :, :], -1.0, None, ALU.mult))
                link(nc.vector.tensor_copy(mp[:, :, 0, :], max_rest[:]))
                link(nc.vector.tensor_tensor(max_rest[:], max_rest[:], mp[:, :, 0, :], ALU.subtract))
                link(nc.vector.tensor_copy(mp[:, :, 1, :], max_rest[:]))
                nc.vector.tensor_tensor(mp[:, :, 2, :], max_rest[:], mp[:, :, 1, :],
                                        ALU.subtract).then_inc(maxparts_ready, 1)

            def outputs(q):
                b, g = divmod(q, NG)
                dve.wait_ge(misc_full, misc_turn("tokens", q) + 1)
                if b >= 2 and g == 0:
                    dve.wait_ge(misc_full, misc_turn("OnT", b - 2) + 1)
                tok = misc[:].rearrange("p (n k c) -> p n k c", n=TT, k=GROUP)
                link(nc.vector.reciprocal(den[:], tok[:, :, :, HD]))
                nc.vector.tensor_tensor(O[:, b % 2, :, GROUP * g:GROUP * (g + 1), :], tok[:, :, :, 0:HD],
                                        den[:].rearrange("p n (k o) -> p n k o", o=1)
                                        .broadcast_to([P, TT, GROUP, HD]), ALU.mult).then_inc(misc_free, 1)

            def residual(b):
                dve.wait_ge(misc_full, misc_turn("out", b) + 1)
                xb = x_sb[:, b * TT:(b + 1) * TT, :]
                nc.vector.tensor_tensor(xb, misc[:].rearrange("p (n d) -> p n d", n=TT), xb,
                                        ALU.add).then_inc(misc_free, 1)

            for x in range(4):
                first_part(0, x)
                dve.wait_ge(hi_ready, x + 1)
                rest_of(nc.vector, x).then_inc(rest_ready, 1)
                second_part(0, x)
                dve.wait_ge(mid_ready, x + 1)
                last_part(nc.vector, x).then_inc(lo_ready, 1)
            values(0)
            normalise(1)
            for t in range(FIRST, LAST + 1):
                b = (t + 1) // NG + 1
                a_step, b_step = (b < B and t >= first and t % NG == first % NG for first in (-1, 0))
                for i in range(MX_UNITS):
                    if t + 2 < NQ:
                        maximum(t + 2, i)
                    if i == 1 and 0 <= t + 1 < NQ:
                        maximum_parts(t + 1)
                    if a_step:
                        if i == 5:
                            first_part(b, 0)
                        if i == 7:
                            first_part(b, 1)
                            second_part(b, 0)
                    if b_step:
                        if i == 0:
                            first_part(b, 2)
                        if i == 1:
                            second_part(b, 1)
                            first_part(b, 3)
                        if i == 3:
                            second_part(b, 2)
                        if i == 5:
                            values(b)
                            second_part(b, 3)
                    if i == 4 and (t - 5 >= 0 and (t - 5) % NG == 0):
                        residual((t - 5) // NG)
                    if i == 5 and 0 <= t - 1 < NQ:
                        outputs(t - 1)
                if (t + 3) % NG == 0 and (t + 3) // NG + 1 < B:
                    normalise((t + 3) // NG + 1)

        @block.scalar
        def _(act):
            std_of(act, 0, TT)

            def evacuate(job, index, ins):
                act.wait_ge(misc_full, misc_turn(job, index) + 1)
                ins().then_inc(misc_free, 1)

            def tokens_turned(b):
                if b:
                    act.wait_ge(misc_full, misc_turn("V", b - 1) + 1)
                evacuate("xnT", b, lambda: nc.scalar.copy(xnT[:], misc[:]))

            def feature(b, x, ins):
                if b:
                    act.wait_ge(lo_ready, 4 * b)
                ins().then_inc(feat_ready, 1)

            def queries(b):
                act.wait_ge(misc_full, misc_turn("Q", b) + 1)
                if b == 0:
                    act.wait_ge(consts_ready, 3)
                feature(b, 0, lambda: nc.scalar.activation(feat[:, 0, :], misc[:], ACT.Identity, bias=bqs[:]))
                act.wait_ge(feat_ready, 4 * b + 1)
                if b:
                    act.wait_ge(misc_full, misc_turn("J", b - 1) + 1)
                nc.scalar.activation(tanh_q[:], feat[:, 0, :], ACT.Tanh, scale=1.0 / QK_SCALE).then_inc(tq_ready, 1)

            def keys(b):
                act.wait_ge(misc_full, misc_turn("K", b) + 1)
                feature(b, 1, lambda: nc.scalar.activation(feat[:, 1, :], misc[:], ACT.Identity, bias=bk[:]))
                act.wait_ge(feat_ready, 4 * b + 2)
                nc.scalar.activation(feat[:, 2, :], feat[:, 1, :], ACT.Tanh).then_inc(feat_ready, 1)

            def entangled(b):
                act.wait_ge(misc_full, misc_turn("J", b) + 1)
                feature(b, 3, lambda: nc.scalar.activation(feat[:, 3, :], misc[:], ACT.Copy, scale=lam[:]))

            def maxima_turned(q):
                evacuate("max", q, lambda: nc.scalar.copy(neg_max[:, q % 2, :], misc[0:3 * GROUP, :]))

            def maxima_stacked(q):
                b, g = divmod(q, NG)
                act.wait_ge(*misc_read(misc_turn("max", q)))
                if b >= 2:
                    act.wait_ge(st_psum, ST_UNITS * NG * (b - 1))
                act.dma_start(QA[ROWS:ROWS + 3, b % 2, GROUP * g:GROUP * (g + 1), :],
                              neg_max[:, q % 2, :]).then_inc(max_rows[q % 2], 16)

            def exponential(q, u):
                n = ST_UNITS * q + u
                p, i = divmod(u, 5)
                act.wait_ge(st_psum, n + 1)
                if q >= 2:
                    act.wait_ge(pv_psum, q - 1)
                src = st[:, n % 2, :]
                if i < 2:
                    dst = probs[:, q % 2, 2 * p + i, 0:S]
                elif i < 4:
                    dst = probs[:, q % 2, 2 * p + i - 2, S:2 * S]
                else:
                    dst = probs[:, q % 2, 2 * p:2 * p + 2, 2 * S:SCORE_COLS]
                    src = src.rearrange("p (a n) -> p a n", a=2)
                nc.scalar.activation(dst, src, ACT.Exp).then_inc(exp_done, 1)

            def group_out(q):
                act.wait_ge(pv_psum, q + 1)
                if q >= 2:
                    act.wait_ge(misc_full, misc_turn("tokens", q - 2) + 1)
                nc.scalar.copy(OT[:, q % 2, :], pv[:]).then_inc(ot_ready, 1)

            def outputs_turned(b):
                if b:
                    act.wait_ge(misc_full, misc_turn("out", b - 1) + 1)
                evacuate("OnT", b, lambda: nc.scalar.copy(OnT[:], misc[:]))

            act.wait_ge(first_in, 32)
            tokens_turned(0)
            std_of(act, TT, NT)
            queries(0)
            keys(0)
            entangled(0)
            for t in range(FIRST, LAST + 1):
                jobs = pe_jobs(t)
                for u in range(ST_UNITS):
                    if 0 <= t < NQ:
                        exponential(t, u)
                    for job, index in jobs[u]:
                        {"xnT": tokens_turned, "Q": queries, "K": keys, "J": entangled, "max": maxima_turned,
                         "OnT": outputs_turned}.get(job, lambda index: None)(index)
                    if u == 4 and 0 <= t + 1 < NQ:
                        maxima_stacked(t + 1)
                    if u == 3 and 0 <= t - 1 < NQ:
                        group_out(t - 1)

        @block.tensor
        def _(pe):
            pe.wait_ge(first_in, 32)
            mm = nc.tensor.matmul
            tiles = [slice(t * P, (t + 1) * P) for t in range(TT)]

            def side(job, index):
                if job == "pv":
                    return probs_values(index)
                turn = misc_turn(job, index)
                if turn:
                    pe.wait_ge(*misc_read(turn - 1))
                {"xnT": turn_tokens, "Q": queries, "K": keys, "V": values, "J": entangle, "max": turn_maxima,
                 "tokens": turn_outputs, "OnT": turn_heads, "out": project}[job](index).then_inc(misc_full, 1)

            def turn_tokens(b):
                pe.wait_ge(xn_ready, b + 1)
                for t in range(TT):
                    last = nc.tensor.transpose(misc[:, tiles[t]], xn[:, t, :], ident[:])
                return last

            def queries(b):
                pe.wait_ge(*misc_read(misc_turn("xnT", b)))
                if b == 0:
                    pe.wait_ge(consts_ready, 3)
                return mm(misc[:], wqs[:], xnT[:], start=True, stop=True)

            def keys(b):
                return mm(misc[:], w["wk"][:], xnT[:], start=True, stop=True)

            def values(b):
                for t in range(TT):
                    last = mm(misc[:, tiles[t]], xnT[:, tiles[t]], w["wv"][:], start=True, stop=True)
                return last

            def entangle(b):
                pe.wait_ge(tq_ready, b + 1)
                return mm(misc[:], w["J"][:], tanh_q[:], start=True, stop=True)

            def turn_maxima(q):
                pe.wait_ge(maxparts_ready, q + 1)
                for t in range(TT):
                    last = mm(misc[0:3 * GROUP, tiles[t]], max_parts[:, q % 2, t, :, :].rearrange("p k h -> p (k h)"),
                              ident_b[:], start=True, stop=True)
                return last

            def probs_values(q):
                b, g = divmod(q, NG)
                pe.wait_ge(exp_done, ST_UNITS * (q + 1))
                if q:
                    pe.wait_ge(ot_ready, q)
                for j, c in ((0, 0), (1, S), (3, S + 3 * P), (2, 2 * S)):
                    for k in range(GROUP):
                        last = mm(pv[k * HP:(k + 1) * HP, j * P:S], V[:, b % 2, j, GROUP * g + k, :],
                                  probs[:, q % 2, k, c:c + S - j * P], start=(j == 0), stop=(j == 2))
                last.then_inc(pv_psum, 1)

            def turn_outputs(q):
                pe.wait_ge(ot_ready, q + 1)
                for t in range(TT):
                    last = nc.tensor.transpose(misc[:, tiles[t]], OT[:, q % 2, tiles[t]], ident[:])
                return last

            def turn_heads(b):
                pe.wait_ge(*misc_read(misc_turn("tokens", NG * b + NG - 1)))
                for t in range(TT):
                    last = nc.tensor.transpose(misc[:, tiles[t]], O[:, b % 2, t, :, :].rearrange("p h r -> p (h r)"),
                                               ident[:])
                return last

            def project(b):
                pe.wait_ge(*misc_read(misc_turn("OnT", b)))
                for t in range(TT):
                    mm(misc[:, tiles[t]], OnT[:, tiles[t]], w["wo"][:], start=True, stop=False)
                    last = mm(misc[:, tiles[t]], one[:], bo[0:1, :], start=False, stop=True)
                return last

            def scores_t(out, q, a, j):
                b, g = divmod(q, NG)
                h = GROUP * g + a
                mm(out, KA[0:ROWS + 3, b % 2, h, j * P:(j + 1) * P], QA[0:ROWS + 3, b % 2, h, j * P:S],
                   start=True, stop=False)
                return mm(out[:, 0:P], ident_b[:], mask_k[:], start=False, stop=True)

            def scores_unit(q, u):
                n = ST_UNITS * q + u
                p, i = divmod(u, 5)
                if n >= 2:
                    pe.wait_ge(exp_done, n - 1)
                out = st[:, n % 2, :]
                if i < 2:
                    last = scores_t(out, q, 2 * p + i, 0)
                elif i < 4:
                    scores_t(out[:, 0:3 * P], q, 2 * p + i - 2, 1)
                    last = scores_t(out[:, 3 * P:S], q, 2 * p + i - 2, 3)
                else:
                    scores_t(out[:, 0:2 * P], q, 2 * p, 2)
                    last = scores_t(out[:, 2 * P:S], q, 2 * p + 1, 2)
                last.then_inc(st_psum, 1)

            def maximum_unit(q, i):
                b, g = divmod(q, NG)
                p, r = divmod(i, TT)
                m = MX_UNITS * q + i
                if m >= 2:
                    pe.wait_ge(mx_read, m - 1)
                for a in range(2):
                    h = GROUP * g + 2 * p + a
                    mm(mx[:, m % 2, a, 0:P * (r + 1)], QA[0:ROWS, b % 2, h, tiles[r]],
                       KA[0:ROWS, b % 2, h, 0:P * (r + 1)], start=True, stop=False)
                    last = mm(mx[:, m % 2, a, tiles[r]], ident_b[:], mask_q[:], start=False, stop=True)
                last.then_inc(mx_psum, 1)

            for job in MISC[:5]:
                side(*job)
            for t in range(FIRST, LAST + 1):
                jobs = pe_jobs(t)
                if t + 2 < NQ and (t + 2) % NG == 0:
                    pe.wait_ge(stacked, 16 * (SPREADS * ((t + 2) // NG + 1) - POOL_SPREADS))
                    pe.wait_ge(stacked_pool, 16 * POOL_SPREADS)
                if t == 0:
                    pe.wait_ge(padded, 3)
                if 0 <= t < NQ:
                    pe.wait_ge(max_rows[t % 2], 16 * (t // 2 + 1))
                for u in range(ST_UNITS):
                    for job in jobs[u]:
                        side(*job)
                    if 0 <= t < NQ:
                        scores_unit(t, u)
                    if t + 2 < NQ and u < MX_UNITS:
                        maximum_unit(t + 2, u)




def routed_ffn(nc, x_sb, A, C, tag, top_k, out=None):
    KT = top_k * NT
    NS = (KT * P + E * (P - 1)) // P
    assert NS % RING == 3
    with ExitStack() as ctx:
        sb = lambda name, shape, dt=F32: ctx.enter_context(nc.sbuf_tensor(f"{tag}_{name}", shape, dt))
        sem = lambda name: ctx.enter_context(nc.semaphore(f"{tag}_{name}"))
        ps = lambda name, shape: ctx.enter_context(nc.psum_tensor(f"{tag}_{name}", shape, F32))

        w_all = sb("w_all", [P, E, 3 * IP])
        w_now = sb("w_now", [P, RING, 3 * IP])
        wr, ident = C[f"{tag}_wr"], C["ident"]
        before = C["before"]
        ones = sb("ones", [P, P], BF16)
        rank = C["rank"]
        steps = C["steps"]
        numbers = C["numbers"]
        xn = sb("xn", [P, NT, D])
        xnT = sb("xnT", [P, 2, S])
        logits = sb("logits", [P, NT, E])
        score = sb("score", [P, NT, E])
        best = sb("best", [P, NT, 1])
        top = sb("top", [P, top_k, NT, 1])
        onehot = sb("onehot", [P, top_k, NT, E])
        onehot_b = sb("onehot_b", [P, top_k, NT, E], BF16)
        weight = sb("weight", [P, top_k, NT])
        gap, gap_sum = sb("gap", [P, NT]), sb("gap_sum", [P, NT])
        over = sb("over", [P, E, KT + 1])
        tiles = sb("tiles", [P, E])
        ends = sb("ends", [P, E])
        starts = sb("starts", [P, E])
        place = sb("place", [P, KT, E])
        pos_f = sb("pos_f", [P, KT])
        pos = sb("pos", [P, KT], I32)
        low_i, low = sb("low_i", [P, KT], I32), sb("low", [P, KT])
        high = sb("high", [P, KT])
        tile_rows = sb("tile_rows", [P, NS])
        low_hot = sb("low_hot", [P, KT, P], BF16)
        high_hot = sb("high_hot", [P, KT, NS], BF16)
        number_hot = sb("number_hot", [P, KT, 2, NS], BF16)
        spare = sb("spare", [P, NS])
        number, token_f = sb("number", [P, NS]), sb("token_f", [P, NS])
        beyond = sb("beyond", [P, NS])
        pair, token = sb("pair", [P, NS], U32), sb("token", [P, NS], U32)
        passed = sb("passed", [P, NS, E])
        expert_f = sb("expert_f", [P, NS])
        expert = sb("expert", [P, NS], I32)
        xs, xsT = sb("xs", [P, RING, D]), sb("xsT", [P, 2, P])
        sg, hid = sb("sg", [P, 2, IP]), sb("hid", [P, 2, IP])
        y = sb("y", [P, RING, D])
        back = sb("back", [P, KT, D])
        tokens = nc.dram_tensor(f"{tag}_tokens", (NT * P, D), F32, kind="Internal").ap()
        pair_y = nc.dram_tensor(f"{tag}_pair_y", ((KT + NS) * P, D), F32, kind="Internal").ap()
        p_turn, p_rank = ps("p_turn", [P, 2, S]), ps("p_rank", [P, KT + 1, E])
        p_g, p_u = ps("p_g", [P, 2, 512]), ps("p_u", [P, 2, 512])
        p_y = ps("p_y", [P, D])

        tokens_out = sem("tokens_out")
        w_loaded, w_ready = sem("w_loaded"), sem("w_ready")
        xn_ready, xnT_psum, xnT_ready = sem("xn_ready"), sem("xnT_psum"), sem("xnT_ready")
        logit_psum, logit_psum_part = sem("logit_psum"), sem("logit_psum_part")
        onehot_ready, rank_psum = sem("onehot_ready"), sem("rank_psum")
        high_ready, number_ready, low_ready = sem("high_ready"), sem("number_ready"), sem("low_ready")
        number_psum, pair_ready = sem("number_psum"), sem("pair_ready")
        if top_k == 2:
            gap_ready, exp_ready, weight_ready = sem("gap_ready"), sem("exp_ready"), sem("weight_ready")
            weighted = sem("weighted")
        xs_in = [sem(f"xs_in{r}") for r in range(RING)]
        xs_psum, xsT_ready = sem("xs_psum"), sem("xsT_ready")
        g_psum, sg_ready, u_psum, hid_ready = sem("g_psum"), sem("sg_ready"), sem("u_psum"), sem("hid_ready")
        y_psum, y_ready = sem("y_psum"), sem("y_ready")
        y_out = [sem(f"y_out{r}") for r in range(RING)]
        back_in = [sem(f"back_in{b}") for b in range(B)]
        route, x_done = sem("route"), sem("x_done")
        mv, rstd, stats_of, std_of, rstd_of = layer_norm_stats(nc, ctx, tag, x_sb)
        NGRP = NT // TT

        def run_steps(eng, step):
            for r in range(RING):
                step(r, r, 0)
            with eng.Fori(0, NS // RING - 1) as m:
                for r in range(RING):
                    step(RING * m + RING + r, r, m + 1)
            for r in range(NS % RING):
                step(NS - NS % RING + r, r, NS // RING)

        block = ctx.enter_context(nc.Block())

        @block.sync
        def _(sp):
            for g in range(NGRP):
                sp.wait_ge(xn_ready, g + 1)
                sp.dma_start(tokens[g * TT * P:(g + 1) * TT * P, :].rearrange("(n p) d -> p n d", p=P),
                             xn[:, g * TT:(g + 1) * TT, :]).then_inc(tokens_out, 16)
            for e in range(E):
                sp.dma_start(w_all[:, e, :], A[f"{tag}_w"][:, e, :]).then_inc(w_loaded, 16)

            for r in range(RING):
                sp.wait_ge(y_out[r], 16 * ((NS - 1 - r) // RING + 1))
            for b in range(B):
                for k in range(top_k):
                    v = k * NT + b * TT
                    sp.dma_start(back[:, v:v + TT, :], pair_y[v * P:(v + TT) * P, :]
                                 .rearrange("(n p) d -> p n d", p=P)).then_inc(back_in[b], 16)
            if out is not None:
                stored = sem("stored")
                for b in range(B):
                    sp.wait_ge(x_done, b + 1)
                    sp.dma_start(out[b].rearrange("(n p) d -> p n d", p=P),
                                 x_sb[:, b * TT:(b + 1) * TT, :]).then_inc(stored, 16)
                sp.wait_ge(stored, 16 * B)

        @block.vector
        def _(dve):
            link = Chain(dve, route)
            link(nc.vector.memset(ones[:], 1.0))
            link(nc.vector.tensor_scalar(tile_rows[:], steps[:, 0:NS], float(P), None, ALU.mult))

            def normalise(g):
                rstd_of(dve, g * TT, (g + 1) * TT)
                for t in range(g * TT, (g + 1) * TT):
                    ins = nc.vector.tensor_scalar(xn[:, t, :], x_sb[:, t, :], mv[:, t, 0:1], rstd[:, t:t + 1],
                                                  ALU.subtract, ALU.mult)
                ins.then_inc(xn_ready, 1)

            for g in range(NGRP):
                stats_of(dve, g * TT, (g + 1) * TT)
                if g:
                    normalise(g - 1)
            normalise(NGRP - 1)
            dve.wait_ge(logit_psum, 1)
            link(nc.vector.tensor_copy(logits[:], p_rank[:, 0:NT, :]))
            across = lambda a: a.broadcast_to([P, NT, E])
            for k in range(top_k):
                link(nc.vector.reduce_max(top[:, k, :, 0], logits[:], AX_X))
                link(nc.vector.tensor_tensor(score[:], logits[:], across(top[:, k, :, :]), ALU.is_equal))
                link(nc.vector.tensor_tensor(score[:], score[:], across(rank[:].rearrange("p (o e) -> p o e", o=1)),
                                             ALU.mult))
                link(nc.vector.reduce_max(best[:, :, 0], score[:], AX_X))
                link(nc.vector.tensor_tensor(onehot[:, k, :, :], score[:], across(best[:]), ALU.is_equal))
                nc.vector.tensor_copy(onehot_b[:, k, :, :], onehot[:, k, :, :]).then_inc(onehot_ready, 1)
                if k + 1 < top_k:
                    link(nc.vector.scalar_tensor_tensor(out=logits[:], in0=onehot[:, k, :, :], scalar=-1e30,
                                                        in1=logits[:], op0=ALU.mult, op1=ALU.add))
            if top_k == 2:
                nc.vector.tensor_tensor(gap[:], top[:, 1, :, 0], top[:, 0, :, 0], ALU.subtract).then_inc(gap_ready, 1)
                dve.wait_ge(exp_ready, 1)
                link(nc.vector.tensor_scalar(gap_sum[:], gap[:], 1.0, None, ALU.add))
                link(nc.vector.reciprocal(weight[:, 0, :], gap_sum[:]))
                nc.vector.tensor_tensor(weight[:, 1, :], gap[:], weight[:, 0, :], ALU.mult).then_inc(weight_ready, 1)
            dve.wait_ge(rank_psum, 1)
            cnt = p_rank[:, KT, :].rearrange("p (e o) -> p e o", o=1).broadcast_to([P, E, KT + 1])
            limit = steps[:, 0:KT + 1].rearrange("p (o n) -> p o n", o=1).broadcast_to([P, E, KT + 1])
            link(nc.vector.tensor_scalar(over[:], limit, float(P), None, ALU.mult))
            link(nc.vector.tensor_tensor(over[:], cnt, over[:], ALU.is_gt))
            link(nc.vector.reduce_sum(tiles[:], over[:], AX_X))
            link(nc.vector.tensor_tensor_scan(ends[:], tiles[:], tiles[:], 0.0, ALU.add, ALU.bypass))
            link(nc.vector.tensor_tensor(starts[:], ends[:], tiles[:], ALU.subtract))
            link(nc.vector.tensor_scalar(starts[:], starts[:], float(P), None, ALU.mult))
            over_tiles = lambda a: a.rearrange("p (o e) -> p o e", o=1).broadcast_to([P, KT, E])
            link(nc.vector.tensor_tensor(place[:], p_rank[:, 0:KT, :], over_tiles(starts[:]), ALU.add))
            link(nc.vector.tensor_tensor(place[:], place[:], onehot[:].rearrange("p k t e -> p (k t) e"), ALU.mult))
            link(nc.vector.reduce_sum(pos_f[:], place[:], AX_X))
            link(nc.vector.tensor_copy(pos[:], pos_f[:]))
            link(nc.vector.tensor_scalar(low_i[:], pos[:], P - 1, None, ALU.bitwise_and))
            link(nc.vector.tensor_copy(low[:], low_i[:]))
            link(nc.vector.tensor_tensor(high[:], pos_f[:], low[:], ALU.subtract))
            col = lambda a, n: a.rearrange("p (v o) -> p v o", o=1).broadcast_to([P, KT, n])
            row = lambda a, n, k=KT: a.rearrange("p (o n) -> p o n", o=1).broadcast_to([P, k, n])
            nc.vector.tensor_tensor(high_hot[:], col(high[:], NS), row(tile_rows[:], NS), ALU.is_equal
                                    ).then_inc(high_ready, 1)
            dve.wait_ge(high_ready, 1)
            nc.vector.tensor_tensor(number_hot[:, :, 0, :], high_hot[:], col(steps[:, 1:KT + 1], NS), ALU.mult
                                    ).then_inc(number_ready, 1)
            for v in range(0, KT, LOW_PART):
                part = slice(v, v + LOW_PART)
                nc.vector.tensor_tensor(low_hot[:, part, :], low[:, part].rearrange("p (v o) -> p v o", o=1)
                                        .broadcast_to([P, LOW_PART, P]), row(steps[:, 0:P], P, LOW_PART), ALU.is_equal
                                        ).then_inc(low_ready, 1)
            dve.wait_ge(number_psum, 1)
            tiles_v, rows_p = p_y[:, 0:NS], p_y[:, NS:2 * NS]
            link(nc.vector.tensor_scalar(spare[:], tiles_v, 0.0, float(P), ALU.is_equal, ALU.mult))
            link(nc.vector.tensor_copy(number[:], rows_p))
            link(nc.vector.scalar_tensor_tensor(out=number[:], in0=tiles_v, scalar=float(P), in1=number[:],
                                                op0=ALU.mult, op1=ALU.add))
            link(nc.vector.tensor_scalar(number[:], number[:], -float(P), None, ALU.add))
            link(nc.vector.tensor_scalar(token_f[:], number[:], 0.0, None, ALU.max))
            if top_k == 2:
                link(nc.vector.tensor_scalar(beyond[:], number[:], float(NT * P), -float(NT * P), ALU.is_ge, ALU.mult))
                link(nc.vector.tensor_tensor(token_f[:], token_f[:], beyond[:], ALU.add))
            nc.vector.tensor_copy(token[:], token_f[:]).then_inc(pair_ready, 1)
            link(nc.vector.tensor_scalar(beyond[:], spare[:], 1.0 / P, None, ALU.mult))
            link(nc.vector.tensor_tensor(beyond[:], beyond[:], numbers[:, KT:KT + NS], ALU.mult))
            link(nc.vector.tensor_tensor(number[:], number[:], spare[:], ALU.add))
            link(nc.vector.tensor_tensor(number[:], number[:], beyond[:], ALU.add))
            nc.vector.tensor_copy(pair[:], number[:]).then_inc(pair_ready, 1)
            link(nc.vector.tensor_tensor(passed[:], ends[:].rearrange("p (o e) -> p o e", o=1)
                                         .broadcast_to([P, NS, E]),
                                         steps[:, 0:NS].rearrange("p (s o) -> p s o", o=1)
                                         .broadcast_to([P, NS, E]), ALU.is_le))
            link(nc.vector.reduce_sum(expert_f[:], passed[:], AX_X))
            link(nc.vector.tensor_scalar(expert_f[:], expert_f[:], float(E - 1), None, ALU.min))
            link(nc.vector.tensor_copy(expert[:], expert_f[:]))

            dve.wait_ge(w_loaded, 16 * E)

            def weights(s, r):
                e = dve.value_load(expert[0:1, bass.ds(s, 1)], min_val=0, max_val=E - 1)
                if within(s, RING):
                    dve.wait_ge(y_psum, s - RING + 1)
                nc.vector.tensor_copy(w_now[:, r, :], w_all[:, bass.ds(e, 1), :]).then_inc(w_ready, 1)

            def hidden(s, k):
                dve.wait_ge(sg_ready, s + 1)
                dve.wait_ge(u_psum, s + 1)
                if within(s, 2):
                    dve.wait_ge(y_psum, s - 1)
                nc.vector.tensor_tensor(hid[:, k, :], sg[:, k, :], p_u[:, k, 0:IP], ALU.mult).then_inc(hid_ready, 1)

            def step(s, r, q):
                if within(s, 0, NS - 2):
                    weights(s + 2, (r + 2) % RING)
                if within(s, 0, NS - 1):
                    hidden(s + 1, (r + 1) % 2)

            weights(0, 0)
            weights(1, 1)
            hidden(0, 0)
            run_steps(dve, step)
            if top_k == 2:
                dve.wait_ge(weight_ready, 1)
            for b in range(B):
                dve.wait_ge(back_in[b], 16 * top_k)
                if top_k == 2:
                    for t in range(b * TT, (b + 1) * TT):
                        last = nc.vector.scalar_tensor_tensor(out=x_sb[:, t, :], in0=back[:, t, :],
                                                              scalar=weight[:, 0, t:t + 1], in1=x_sb[:, t, :],
                                                              op0=ALU.mult, op1=ALU.add)
                    link(last)
                    dve.wait_ge(weighted, b + 1)
                v, xb = (top_k - 1) * NT + b * TT, x_sb[:, b * TT:(b + 1) * TT, :]
                nc.vector.tensor_tensor(xb, back[:, v:v + TT, :], xb, ALU.add).then_inc(x_done, 1)

        @block.scalar
        def _(act):
            std_of(act, 0, TT)
            for g in range(NGRP):
                if g + 1 < NGRP:
                    std_of(act, (g + 1) * TT, (g + 2) * TT)
                act.wait_ge(xnT_psum, g + 1)
                if g >= 2:
                    act.wait_ge(logit_psum_part, g - 1)
                nc.scalar.copy(xnT[:, g % 2, :], p_turn[:, g % 2, :]).then_inc(xnT_ready, 1)
            if top_k == 2:
                act.wait_ge(gap_ready, 1)
                nc.scalar.activation(gap[:], gap[:], ACT.Exp).then_inc(exp_ready, 1)
            act.wait_ge(high_ready, 1)
            nc.scalar.activation(number_hot[:, :, 1, :], high_hot[:], ACT.Copy, scale=numbers[:, 0:1]
                                 ).then_inc(number_ready, 1)

            def into(s, k):
                act.wait_ge(xs_psum, s + 1)
                if within(s, 2):
                    act.wait_ge(u_psum, s - 1)
                nc.scalar.copy(xsT[:, k, :], p_turn[:, k, 0:P]).then_inc(xsT_ready, 1)

            def gate(s, k):
                act.wait_ge(g_psum, s + 1)
                if within(s, 2):
                    act.wait_ge(hid_ready, s - 1)
                nc.scalar.activation(sg[:, k, :], p_g[:, k, 0:IP], ACT.Silu).then_inc(sg_ready, 1)

            def result(s, r, q):
                act.wait_ge(y_psum, s + 1)
                if within(s, RING):
                    act.wait_ge(y_out[r], 16 * q)
                nc.scalar.copy(y[:, r, :], p_y[:]).then_inc(y_ready, 1)

            def step(s, r, q):
                if within(s, 0, NS - 1):
                    gate(s + 1, (r + 1) % 2)
                if within(s, 0, NS - 2):
                    into(s + 2, r % 2)
                result(s, r, q)

            into(0, 0)
            into(1, 1)
            gate(0, 0)
            run_steps(act, step)
            if top_k == 2:
                act.wait_ge(weight_ready, 1)
                for b in range(B):
                    act.wait_ge(back_in[b], 16 * top_k)
                    for t in range(b * TT, (b + 1) * TT):
                        last = nc.scalar.activation(back[:, NT + t, :], back[:, NT + t, :], ACT.Copy,
                                                    scale=weight[:, 1, t:t + 1])
                    last.then_inc(weighted, 1)

        @block.gpsimd
        def _(pool):
            def tile_in(s):
                if s >= RING:
                    pool.wait_ge(xs_psum, s - RING + 1)
                nc.gpsimd.indirect_dma_start(xs[:, s % RING, :], None, tokens,
                                             bass.IndirectOffsetOnAxis(ap=token[:, s:s + 1], axis=0)
                                             ).then_inc(xs_in[s % RING], 16)

            pool.wait_ge(tokens_out, 16 * NGRP)
            pool.wait_ge(pair_ready, 1)
            for s in range(RING):
                tile_in(s)
            pool.wait_ge(pair_ready, 2)
            for s in range(NS):
                if s + RING < NS:
                    tile_in(s + RING)
                pool.wait_ge(y_ready, s + 1)
                nc.gpsimd.indirect_dma_start(pair_y, bass.IndirectOffsetOnAxis(ap=pair[:, s:s + 1], axis=0),
                                             y[:, s % RING, :], None).then_inc(y_out[s % RING], 16)

        @block.tensor
        def _(pe):
            mm = nc.tensor.matmul

            def turn_group(g):
                pe.wait_ge(xn_ready, g + 1)
                if g >= 2:
                    pe.wait_ge(xnT_ready, g - 1)
                for t in range(TT):
                    last = nc.tensor.transpose(p_turn[:, g % 2, t * P:(t + 1) * P], xn[:, g * TT + t, :], ident[:])
                last.then_inc(xnT_psum, 1)

            turn_group(0)
            for g in range(NGRP):
                if g + 1 < NGRP:
                    turn_group(g + 1)
                pe.wait_ge(xnT_ready, g + 1)
                for t in range(TT):
                    last = mm(p_rank[:, g * TT + t, :], xnT[:, g % 2, t * P:(t + 1) * P], wr[:],
                              start=(g == 0 and t == 0), stop=(g == NGRP - 1 and t == TT - 1), skip_group_check=True)
                if g < NGRP - 1:
                    last.then_inc(logit_psum_part, 1)
            last.then_inc(logit_psum, 1)
            pe.wait_ge(route, 1)
            flat = onehot_b[:].rearrange("p k t e -> p (k t) e")
            for k in range(top_k):
                pe.wait_ge(onehot_ready, k + 1)
                choice = slice(k * NT, (k + 1) * NT)
                mm(p_rank[:, choice, :], before[:], flat[:, choice, :], start=(k == 0), stop=False,
                   skip_group_check=True)
                for v in range(k * NT, (k + 1) * NT):
                    last = mm(p_rank[:, v + 1:KT + 1, :], ones[:],
                              flat[:, v:v + 1, :].broadcast_to([P, KT - v, E]), start=False, stop=(v == KT - 1),
                              skip_group_check=True)
            last.then_inc(rank_psum, 1)
            pe.wait_ge(number_ready, 2)
            for v in range(KT):
                if v % LOW_PART == 0:
                    pe.wait_ge(low_ready, v // LOW_PART + 1)
                last = mm(p_y[:, 0:2 * NS], low_hot[:, v, :], number_hot[:, v, :, :].rearrange("p k s -> p (k s)"),
                          start=(v == 0), stop=(v == KT - 1))
            last.then_inc(number_psum, 1)

            def turn_in(s, r, q):
                pe.wait_ge(xs_in[r], 16 * (q + 1))
                if within(s, 2):
                    pe.wait_ge(xsT_ready, s - 1)
                nc.tensor.transpose(p_turn[:, r % 2, 0:P], xs[:, r, :], ident[:]).then_inc(xs_psum, 1)

            def gate_up(s, r):
                k = r % 2
                pe.wait_ge(w_ready, s + 1)
                pe.wait_ge(xsT_ready, s + 1)
                if within(s, 2):
                    pe.wait_ge(hid_ready, s - 1)
                for to, done, w0 in ((p_g, g_psum, 0), (p_u, u_psum, IP)):
                    for c in range(0, IP, P):
                        last = mm(to[:, k, c:c + P], w_now[:, r, w0 + c:w0 + c + P], xsT[:, k, :],
                                  start=True, stop=True)
                    last.then_inc(done, 1)

            def down(s, r):
                pe.wait_ge(hid_ready, s + 1)
                if within(s, 1):
                    pe.wait_ge(y_ready, s)
                for c in range(0, IP, P):
                    last = mm(p_y[:], hid[:, r % 2, c:c + P], w_now[:, r, 2 * IP + c:2 * IP + c + P],
                              start=(c == 0), stop=(c == IP - P))
                last.then_inc(y_psum, 1)

            def step(s, r, q):
                if within(s, 0, NS - 1):
                    gate_up(s + 1, (r + 1) % RING)
                if within(s, 0, NS - 2):
                    turn_in(s + 2, (r + 2) % RING, q + (r + 2) // RING)
                down(s, r)

            turn_in(0, 0, 0)
            turn_in(1, 1, 0)
            gate_up(0, 0)
            run_steps(pe, step)





def state_space(nc, x_sb, C):
    with ExitStack() as ctx:
        sb = lambda name, shape, dt=F32: ctx.enter_context(nc.sbuf_tensor(f"m_{name}", shape, dt))
        sem = lambda name: ctx.enter_context(nc.semaphore(f"m_{name}"))
        ps = lambda name, shape: ctx.enter_context(nc.psum_tensor(f"m_{name}", shape, F32))

        w_in, w_delta = C["m_w_in"], C["m_w_delta"]
        w_bc = C["m_w_bc"]
        by_half = lambda name: C[name].rearrange("p (h n) -> p h n", h=HALVES)
        w_out, conv_w, a_log = by_half("m_w_out"), by_half("m_conv_w"), by_half("m_a_log")
        conv_b, b_delta, skip = C["m_conv_b"], C["m_b_delta"], C["m_skip"]
        state_rows = C["m_state_rows"].rearrange("p (n q) -> p n q", q=P)
        ident = C["ident"]
        w_skip, a_neg = sb("w_skip", [P, HALVES, D]), sb("a_neg", [P, HALVES, DS])
        xn, xnT = sb("xn", [P, TT, D]), sb("xnT", [P, S])
        gate = sb("gate", [P, HALVES, S])
        xi = sb("xi", [P, HALVES, DC - 1 + S])
        xc = sb("xc", [P, 2, HALVES, S])
        size, soft = sb("size", [P, HALVES, S]), sb("soft", [P, HALVES, S])
        rate, dx = sb("rate", [P, 2, HALVES, S]), sb("dx", [P, 2, HALVES, S])
        bc_rest, bc_mid = sb("bc_rest", [P, S]), sb("bc_mid", [P, S], BF16)
        bc = sb("bc", [P, 2, S], BF16)
        b_all = sb("b_all", [P, AHEAD, S])
        decay, inflow = (sb(n, [P, AHEAD, HALVES, S]) for n in ("decay", "inflow"))
        state, seen = sb("state", [P, 3, HALVES, S]), sb("seen", [P, 2, HALVES, S])
        outT = sb("outT", [P, S])
        misc = ps("misc", [P, 3, S])
        p_b, p_c = ps("b", [P, S]), ps("c", [P, 2, S])
        p_out = ps("out", [P, 2, S])

        a_exp, consts_ready = sem("a_exp"), sem("consts_ready")
        xn_ready, xnT_ready = sem("xn_ready"), sem("xnT_ready")
        misc_full = sem("misc_full")
        gate_ready, xi_ready = sem("gate_ready"), sem("xi_ready")
        bc_hi, bc_sub, bc_mid_ready, bc_mid_put, bc_ready = (sem(n) for n in ("bc_hi", "bc_sub", "bc_mid_ready",
                                                                             "bc_mid_put", "bc_ready"))
        ramp_ready, size_ready, size_exp, soft_ready = (sem(n) for n in ("ramp_ready", "size_ready", "size_exp",
                                                                         "soft_ready"))
        conv_done = [sem(f"conv_done_{half}") for half in range(HALVES)]
        tail = sb("tail", [P, HALVES, S])
        tail_ready, rate_ready, dx_ready = sem("tail_ready"), sem("rate_ready"), sem("dx_ready")
        b_psum, b_ready, c_psum = sem("b_psum"), sem("b_ready"), sem("c_psum")
        decay_ready, inflow_ready = sem("decay_ready"), sem("inflow_ready")
        state_ready, seen_ready, out_psum = sem("state_ready"), sem("seen_ready"), sem("out_psum")
        outT_ready, x_done = sem("outT_ready"), sem("x_done")
        mv, rstd, stats_of, std_of, rstd_of = layer_norm_stats(nc, ctx, "m", x_sb)
        N_STEPS = B * DS

        PREPARE = [("xnT", 0), ("gate", 0), ("gate", 1), ("x", 0), ("x", 1), ("bc", 0), ("delta", 0), ("delta", 1)]
        PE_SIDE = {0: [0], 2: [1], 3: [2], 5: [3], 6: [4], 7: [5], 8: [6], 9: [7]}
        uses = [(job, half, 0) for job, half in PREPARE]
        for i in range(N_STEPS + 4):
            b, n = divmod(i, DS)
            if n == 3 and b:
                uses.append(("back", 0, b - 1))
            if b + 1 < B:
                uses += [(*PREPARE[k], b + 1) for k in PE_SIDE.get(n, ())]

        def use(job, half, b):
            return uses.index((job, half, b))

        def bank(job, half, b):
            return misc[:, use(job, half, b) % 3, :]

        def read_of(k):
            job, half, b = uses[k]
            return {"xnT": (xnT_ready, b + 1), "gate": (gate_ready, HALVES * b + half + 1),
                    "x": (xi_ready, HALVES * b + half + 1), "bc": (bc_sub, b + 1),
                    "delta": (size_ready, HALVES * b + half + 1), "back": (x_done, b + 1)}[job]

        block = ctx.enter_context(nc.Block())

        @block.vector
        def _(dve):
            nc.vector.memset(xi[:, :, 0:DC - 1], 0.0).then_inc(consts_ready, 1)
            nc.vector.memset(decay[:, :, :, 0:1], 0.0).then_inc(consts_ready, 1)
            stats_of(dve, 0, TT)
            rstd_of(dve, 0, TT)
            def full(job, half, b):
                dve.wait_ge(misc_full, use(job, half, b) + 1)

            def normalise(b):
                if b:
                    full("xnT", 0, b - 1)
                for t in range(b * TT, (b + 1) * TT):
                    last = nc.vector.tensor_scalar(xn[:, t % TT, :], x_sb[:, t, :], mv[:, t, 0:1],
                                                   rstd[:, t:t + 1], ALU.subtract, ALU.mult)
                last.then_inc(xn_ready, 1)

            def gated(b, half):
                dve.wait_ge(gate_ready, HALVES * b + half + 1)
                full("x", half, b)
                if b:
                    dve.wait_ge(conv_done[half], DC * b)
                nc.vector.tensor_tensor(xi[:, half, DC - 1:], gate[:, half, :], bank("x", half, b),
                                        ALU.mult).then_inc(xi_ready, 1)

            def tap(b, half, k):
                dve.wait_ge(conv_done[half], DC * b + k)
                nc.vector.scalar_tensor_tensor(out=xc[:, b % 2, half, :], in0=xi[:, half, k:k + S],
                                               scalar=conv_w[:, half, k:k + 1], in1=xc[:, b % 2, half, :],
                                               op0=ALU.mult, op1=ALU.add).then_inc(conv_done[half], 1)

            def bc_rest_of(b):
                dve.wait_ge(bc_hi, b + 1)
                if b:
                    dve.wait_ge(bc_ready, b)
                rows = slice(0, 3 * QUAD)
                nc.vector.tensor_tensor(bc_rest[rows, :], bank("bc", 0, b)[rows, :], bc[rows, b % 2, :],
                                        ALU.subtract).then_inc(bc_sub, 1)

            def bc_second(b):
                dve.wait_ge(bc_sub, b + 1)
                nc.vector.tensor_copy(bc_mid[0:3 * QUAD, :], bc_rest[0:3 * QUAD, :]).then_inc(bc_mid_ready, 1)
                dve.wait_ge(bc_mid_ready, b + 1)
                nc.vector.tensor_copy(bc[QUAD:2 * QUAD, b % 2, :], bc_mid[QUAD:2 * QUAD, :]).then_inc(bc_mid_put, 1)

            def bc_third(b):
                dve.wait_ge(bc_mid_put, b + 1)
                nc.vector.tensor_tensor(bc[2 * QUAD:3 * QUAD, b % 2, :], bc_rest[2 * QUAD:3 * QUAD, :],
                                        bc_mid[2 * QUAD:3 * QUAD, :], ALU.subtract).then_inc(bc_ready, 1)

            def rates(b):
                dve.wait_ge(soft_ready, b + 1)
                dve.wait_ge(ramp_ready, HALVES * (b + 1))
                nc.vector.tensor_tensor(rate[:, b % 2, :, :], rate[:, b % 2, :, :], soft[:], ALU.add
                                        ).then_inc(rate_ready, 1)

            def residual(b):
                full("back", 0, b)
                xb = x_sb[:, b * TT:(b + 1) * TT, :]
                nc.vector.tensor_tensor(xb, bank("back", 0, b).rearrange("p (n d) -> p n d", n=TT), xb,
                                        ALU.add).then_inc(x_done, 1)

            normalise(0)
            stats_of(dve, TT, NT)
            rstd_of(dve, TT, NT)
            for half in range(HALVES):
                gated(0, half)
            bc_rest_of(0)
            bc_second(0)
            bc_third(0)
            for half in range(HALVES):
                for k in range(1, DC - 1):
                    tap(0, half, k)
            dve.wait_ge(a_exp, 1)
            nc.vector.tensor_scalar(a_neg[:], a_neg[:], -1.0, None, ALU.mult).then_inc(consts_ready, 1)
            for half in range(HALVES):
                nc.vector.tensor_scalar(w_skip[:, half, :], w_out[:, half, :], skip[:, half:half + 1], None,
                                        ALU.mult).then_inc(consts_ready, 1)
            dve.wait_ge(consts_ready, 5)
            rates(0)
            normalise(1)
            side = {7: [(gated, 0)], 8: [(gated, 1)], 9: [(tap, 0, 1)], 10: [(tap, 0, 2), (bc_rest_of,)],
                    11: [(bc_second,), (tap, 1, 1)], 12: [(bc_third,), (tap, 1, 2)], 14: [(rates,)]}

            def see(i):
                k = i % 2
                dve.wait_ge(state_ready, i + 1)
                dve.wait_ge(c_psum, i + 1)
                if i >= 2:
                    dve.wait_ge(out_psum, (i - 2) // DS + 1 + i - 1)
                nc.vector.tensor_tensor(seen[:, k, :, :], state[:, i % 3, :, :],
                                        p_c[:, k, :].rearrange("p (o t) -> p o t", o=1)
                                        .broadcast_to([P, HALVES, S]), ALU.mult).then_inc(seen_ready, 1)

            for i in range(N_STEPS):
                b, n = divmod(i, DS)
                dve.wait_ge(inflow_ready, i + 1)
                dve.wait_ge(decay_ready, i + 1)
                if i >= 3:
                    dve.wait_ge(seen_ready, i - 2)
                nc.vector.tensor_tensor_scan(state[:, i % 3, :, :].rearrange("p h t -> p (h t)"),
                                             decay[:, i % AHEAD, :, :].rearrange("p h t -> p (h t)"),
                                             inflow[:, i % AHEAD, :, :].rearrange("p h t -> p (h t)"),
                                             0.0, ALU.mult, ALU.add).then_inc(state_ready, 1)
                if b + 1 < B:
                    for job, *args in side.get(n, ()):
                        job(b + 1, *args)
                if n == DS - 1 and b + 2 < B:
                    normalise(b + 2)
                if n == 5 and b:
                    residual(b - 1)
                if i:
                    see(i - 1)
            see(N_STEPS - 1)
            residual(B - 1)

        @block.gpsimd
        def _(pool):
            def last_tap(b, half):
                pool.wait_ge(conv_done[half], DC * (b + 1) - 1)
                pool.wait_ge(tail_ready, HALVES * b + half + 1)
                nc.gpsimd.tensor_tensor(xc[:, b % 2, half, :], tail[:, half, :], xc[:, b % 2, half, :],
                                        ALU.add).then_inc(conv_done[half], 1)

            def drive(b):
                pool.wait_ge(rate_ready, b + 1)
                for half in range(HALVES):
                    pool.wait_ge(conv_done[half], DC * (b + 1))
                nc.gpsimd.tensor_tensor(dx[:, b % 2, :, :], rate[:, b % 2, :, :], xc[:, b % 2, :, :],
                                        ALU.mult).then_inc(dx_ready, 1)
                pool.wait_ge(dx_ready, b + 1)

            for half in range(HALVES):
                last_tap(0, half)
            drive(0)
            for i in range(N_STEPS):
                b, n = divmod(i, DS)
                k = i % AHEAD
                pool.wait_ge(b_ready, i + 1)
                if i >= AHEAD:
                    pool.wait_ge(state_ready, i - AHEAD + 1)
                nc.gpsimd.tensor_tensor(inflow[:, k, :, :], dx[:, b % 2, :, :], b_all[:, k, :]
                                        .rearrange("p (o t) -> p o t", o=1)
                                        .broadcast_to([P, HALVES, S]), ALU.mult).then_inc(inflow_ready, 1)
                if b + 1 < B:
                    if n in (12, 13):
                        last_tap(b + 1, n - 12)
                    if n == DS - 1:
                        drive(b + 1)

        @block.scalar
        def _(act):
            std_of(act, 0, TT)

            def full(job, half, b):
                act.wait_ge(misc_full, use(job, half, b) + 1)

            def tokens_turned(b):
                full("xnT", 0, b)
                if b:
                    full("delta", 1, b - 1)
                nc.scalar.copy(xnT[:], bank("xnT", 0, b)).then_inc(xnT_ready, 1)

            def gates(b):
                for half in range(HALVES):
                    full("gate", half, b)
                    if b:
                        act.wait_ge(xi_ready, HALVES * (b - 1) + half + 1)
                    nc.scalar.activation(gate[:, half, :], bank("gate", half, b), ACT.Silu).then_inc(gate_ready, 1)

            def bc_first(b):
                full("bc", 0, b)
                if b >= 2:
                    act.wait_ge(c_psum, DS * (b - 1))
                rows = slice(0, 3 * QUAD)
                nc.scalar.copy(bc[rows, b % 2, :], bank("bc", 0, b)[rows, :]).then_inc(bc_hi, 1)

            def sizes(b):
                for half in range(HALVES):
                    full("delta", half, b)
                    if b >= 2:
                        act.wait_ge(dx_ready, b - 1)
                    nc.scalar.activation(rate[:, b % 2, half, :], bank("delta", half, b), ACT.Relu,
                                         bias=b_delta[:, half:half + 1]).then_inc(ramp_ready, 1)
                    if b:
                        act.wait_ge(soft_ready, b)
                    nc.scalar.activation(size[:, half, :], bank("delta", half, b), ACT.Abs,
                                         bias=b_delta[:, half:half + 1]).then_inc(size_ready, 1)

            def softs(b):
                act.wait_ge(size_ready, HALVES * (b + 1))
                nc.scalar.activation(size[:], size[:], ACT.Exp, scale=-1.0).then_inc(size_exp, 1)
                act.wait_ge(size_exp, b + 1)
                if b:
                    act.wait_ge(rate_ready, b)
                nc.scalar.activation(soft[:], size[:], ACT.Ln, bias=1.0).then_inc(soft_ready, 1)

            def outer_taps(b):
                for half in range(HALVES):
                    act.wait_ge(xi_ready, HALVES * b + half + 1)
                    if b >= 2:
                        act.wait_ge(dx_ready, b - 1)
                        act.wait_ge(out_psum, (DS + 1) * (b - 2) + 1)
                    nc.scalar.activation(xc[:, b % 2, half, :], xi[:, half, 0:S], ACT.Identity,
                                         bias=conv_b[:, half:half + 1],
                                         scale=conv_w[:, half, 0:1]).then_inc(conv_done[half], 1)
                    if b:
                        act.wait_ge(conv_done[half], DC * b)
                    nc.scalar.activation(tail[:, half, :], xi[:, half, DC - 1:], ACT.Copy,
                                         scale=conv_w[:, half, DC - 1:DC]).then_inc(tail_ready, 1)

            def result(b):
                act.wait_ge(out_psum, (b + 1) * (DS + 1))
                if b:
                    full("back", 0, b - 1)
                nc.scalar.copy(outT[:], p_out[:, b % 2, :]).then_inc(outT_ready, 1)

            tokens_turned(0)
            std_of(act, TT, NT)
            gates(0)
            outer_taps(0)
            bc_first(0)
            nc.scalar.activation(a_neg[:], a_log[:], ACT.Exp).then_inc(a_exp, 1)
            sizes(0)
            softs(0)
            side = {4: [tokens_turned], 7: [gates], 10: [outer_taps], 11: [bc_first], 12: [sizes], 13: [softs]}
            for i in range(N_STEPS):
                b, n = divmod(i, DS)
                k = i % AHEAD
                if n == 0:
                    act.wait_ge(rate_ready, b + 1)
                act.wait_ge(b_psum, i + 1)
                if i >= AHEAD:
                    act.wait_ge(inflow_ready, i - AHEAD + 1)
                nc.scalar.copy(b_all[:, k, :], p_b[:]).then_inc(b_ready, 1)
                if i >= AHEAD:
                    act.wait_ge(state_ready, i - AHEAD + 1)
                for half in range(HALVES):
                    last = nc.scalar.activation(decay[:, k, half, 1:], rate[:, b % 2, half, 1:], ACT.Exp,
                                                scale=a_neg[:, half, n:n + 1])
                last.then_inc(decay_ready, 1)
                if n == 5 and b:
                    result(b - 1)
                if b + 1 < B:
                    for job in side.get(n, ()):
                        job(b + 1)
            result(B - 1)

        @block.tensor
        def _(pe):
            mm = nc.tensor.matmul

            def project(job, half, b):
                u = use(job, half, b)
                if u >= 3:
                    pe.wait_ge(*read_of(u - 3))
                out = bank(job, half, b)
                if job == "xnT":
                    pe.wait_ge(xn_ready, b + 1)
                    for t in range(TT):
                        last = nc.tensor.transpose(out[:, t * P:(t + 1) * P], xn[:, t, :], ident[:])
                elif job == "back":
                    pe.wait_ge(outT_ready, b + 1)
                    for t in range(TT):
                        last = nc.tensor.transpose(out[:, t * P:(t + 1) * P], outT[:, t * P:(t + 1) * P], ident[:])
                else:
                    weights = {"gate": w_in[:, half * P:(half + 1) * P],
                               "x": w_in[:, DI + half * P:DI + (half + 1) * P],
                               "delta": w_delta[:, half * P:(half + 1) * P], "bc": w_bc[:]}[job]
                    pe.wait_ge(xnT_ready, b + 1)
                    last = mm(out[0:weights.shape[1], :], weights, xnT[:], start=True, stop=True)
                last.then_inc(misc_full, 1)

            rows = slice(0, 3 * QUAD)

            def spread_b(i):
                b, n = divmod(i, DS)
                k = i % 2
                if n == 0:
                    pe.wait_ge(bc_ready, b + 1)
                if i:
                    pe.wait_ge(b_ready, i)
                mm(p_b[:], state_rows[rows, n, :], bc[rows, b % 2, :], start=True, stop=True).then_inc(b_psum, 1)

            def spread_c(i):
                b, n = divmod(i, DS)
                k = i % 2
                if i >= 2:
                    pe.wait_ge(seen_ready, i - 1)
                mm(p_c[:, k, :], state_rows[rows, DS + n, :], bc[rows, b % 2, :],
                   start=True, stop=True).then_inc(c_psum, 1)

            for job, half in PREPARE:
                project(job, half, 0)
            for i in range(AHEAD):
                spread_b(i)
            spread_c(0)
            for i in range(N_STEPS):
                b, n = divmod(i, DS)
                k = i % 2
                if n == 0:
                    for half in range(HALVES):
                        pe.wait_ge(conv_done[half], DC * (b + 1))
                    pe.wait_ge(consts_ready, 4)
                    if b >= 2:
                        pe.wait_ge(outT_ready, b - 1)
                    for half in range(HALVES):
                        last = mm(p_out[:, b % 2, :], w_skip[:, half, :], xc[:, b % 2, half, :],
                                  start=(half == 0), stop=False)
                    last.then_inc(out_psum, 1)
                if i + AHEAD < N_STEPS:
                    spread_b(i + AHEAD)
                if i + 1 < N_STEPS:
                    spread_c(i + 1)
                if n == 3 and b:
                    project("back", 0, b - 1)
                if b + 1 < B:
                    for j in PE_SIDE.get(n, ()):
                        project(*PREPARE[j], b + 1)
                pe.wait_ge(seen_ready, i + 1)
                for half in range(HALVES):
                    last = mm(p_out[:, b % 2, :], w_out[:, half, :], seen[:, k, half, :], start=False,
                              stop=(n == DS - 1 and half == HALVES - 1))
                last.then_inc(out_psum, 1)
            project("back", 0, B - 1)


def program(nc, A, out):
    with ExitStack() as ctx:
        x_sb = ctx.enter_context(nc.sbuf_tensor("x_sb", [P, NT, D], F32))
        packs, C = constant_tiles(nc, ctx)
        attention(nc, x_sb, A, packs, C)
        routed_ffn(nc, x_sb, A, C, "f0", 1)
        state_space(nc, x_sb, C)
        routed_ffn(nc, x_sb, A, C, "f1", 2, out)


def host_arrays(inputs):
    import numpy as np
    i = {k: np.asarray(v) for k, v in inputs.items()}
    bf16_bits = lambda a: (np.asarray(a, np.float32).view(np.uint32) >> 16).astype(np.uint16)
    turned = lambda a: np.ascontiguousarray(np.swapaxes(a, -1, -2))
    r_major = lambda a: np.ascontiguousarray(a.reshape(a.shape[0], H, HD).swapaxes(1, 2).reshape(a.shape[0], D))
    A = {"x": i["L0_attn_x"]}
    c = {}
    c["wq"], c["wk"] = (r_major(turned(i[f"L0_attn_W{n}"])) for n in "qk")
    c["wv"], c["wo"] = turned(i["L0_attn_Wv"]), turned(i["L0_attn_Wo"])
    c["bq"], c["bk"] = (turned(r_major(i[f"L0_attn_b{n}"][None])) for n in "qk")
    c["bv"], c["bo"] = i["L0_attn_bv"][None], i["L0_attn_bo"][None]
    c["lam"] = i["L0_attn_lambda_attn"].reshape(1, 1)
    J = np.zeros((HD, H, HD, H), i["L0_attn_J_attn"].dtype)
    for h in range(H):
        J[:, h, :, h] = i["L0_attn_J_attn"][h]
    c["J"] = J.reshape(D, D)
    c["ident"] = np.eye(P, dtype=np.float32)
    after = np.triu(np.ones((P, P), bool), 1)
    mask = np.where(after, -1e30, 0.0)
    c["ident_b"], c["mask_q"], c["mask_k"] = np.eye(P), mask, mask.T
    for tag, names in (("f0", ("router_w", "gate_w", "up_w", "down_w")),
                       ("f1", ("w_router", "w_gate", "w_up", "w_down"))):
        r, g, u, d = (i[f"L{tag[1]}_ffn_{n}"] for n in names)
        c[f"{tag}_wr"] = turned(r)
        w = np.zeros((P, E, 3, IP), g.dtype)
        w[:, :, 0, :I], w[:, :, 1, :I] = g.transpose(2, 0, 1), u.transpose(2, 0, 1)
        rows = np.zeros((E, IP, D), d.dtype)
        rows[:, :I] = d.transpose(0, 2, 1)
        w[:, :, 2, :] = rows.reshape(E, IP // P, P, D).transpose(2, 0, 1, 3).reshape(P, E, IP)
        A[f"{tag}_w"] = w.reshape(P, E, 3 * IP)
    c["m_w_in"], c["m_w_delta"] = i["L1_attn_W_in"], i["L1_attn_W_delta"]
    c["m_w_bc"] = np.concatenate([i["L1_attn_W_B"], i["L1_attn_W_C"]] * 3, axis=1)
    for n in ("W_out", "conv_w", "conv_b", "b_delta", "D", "A_log"):
        name = {"D": "m_skip"}.get(n, f"m_{n.lower()}")
        c[name] = i[f"L1_attn_{n}"].reshape(HALVES, P, -1).swapaxes(0, 1).reshape(P, -1)
    picked = np.zeros((P, 2 * DS, P), np.float32)
    for n in range(2 * DS):
        picked[[n, QUAD + n, 2 * QUAD + n], n, :] = 1.0
    c["m_state_rows"], c["before"] = picked.reshape(P, -1), after
    c["rank"] = np.arange(E, 0, -1, dtype=np.float32)[None]
    c["numbers"] = np.arange(80, dtype=np.float32)[None] * P + np.arange(P, dtype=np.float32)[:, None]
    c["steps"] = np.arange(P, dtype=np.float32)[None]
    for pack, (names, dt) in PACKS.items():
        A[pack] = np.concatenate([np.broadcast_to(c[name], (P, n)) for name, n in names], axis=1)
        if dt == BF16:
            A[pack] = bf16_bits(A[pack])
    return A


def kernel(**inputs):
    import concourse.bacc as bacc
    from concourse.bass_utils import run_bass_kernel_spmd

    nc = bacc.Bacc("TRN2", target_bir_lowering=False, num_devices=1)
    arrays = host_arrays(inputs)
    aps = {n: nc.dram_tensor(f"in_{n}", a.shape, mybir.dt.from_np(a.dtype), kind="ExternalInput").ap()
           for n, a in arrays.items()}
    out = nc.dram_tensor("out", (B, S, D), F32, kind="ExternalOutput").ap()
    for n, a in arrays.items():
        if a.dtype.kind == "u":
            aps[n] = aps[n].bitcast(BF16)
    program(nc, aps, out)
    result = run_bass_kernel_spmd(nc, [{f"in_{n}": a for n, a in arrays.items()}], core_ids=[0])
    return result.results[0]["out"]
```
